# Optimizing a Trainium2 kernel written in Bass

```python
import numpy as np
import jax
import jax.numpy as jnp

def _softmax(x, axis=-1):
    return jax.nn.softmax(x, axis=axis)

def _gelu(x):
    return jax.nn.gelu(x, approximate=True)

def _silu(x):
    return jax.nn.silu(x)

def _sigmoid(x):
    return jax.nn.sigmoid(x)

def _layernorm(x, axis=-1, eps=1e-05):
    m = jnp.mean(x, axis=axis, keepdims=True)
    v = jnp.var(x, axis=axis, keepdims=True)
    return (x - m) / jnp.sqrt(v + eps)

def _scatter_add(tgt, idx, src, axis=0):
    return tgt.at[idx].add(src)

def _segment_sum(src, seg, n):
    return jax.ops.segment_sum(src, seg, n)
kernel_name = 'mk_xattn_ffn_d4_seqx_r8_d3de52'

def setup_inputs(seed: int=0):
    np.random.seed(seed)
    _w = jnp.asarray

    def _rec_inputs():
        import jax
        import jax.numpy as jnp
        _rk = jax.random.key(seed)
        x = -0.000125 + 0.9999 * jax.random.normal(jax.random.fold_in(_rk, 1), (8, 128, 512), jnp.float32)
        _lenS = 128 - jax.random.randint(jax.random.fold_in(_rk, 7), (8,), 0, max(1, 128 // 4) + 1, jnp.int32)
        _lenS2 = 128 - jax.random.randint(jax.random.fold_in(_rk, 8), (8,), 0, max(1, 128 // 4) + 1, jnp.int32)
        _ctx_4096P = jax.random.normal(jax.random.fold_in(_rk, 11), (8, 16, 512), jnp.float32)
        _ctx_4096c = jax.random.dirichlet(jax.random.fold_in(_rk, 511), 0.3 * jnp.ones((16,), jnp.float32), (8, 128))
        _ctx_4096t = jnp.einsum('bsk,bkd->bsd', _ctx_4096c, _ctx_4096P)
        _ctx_4096t = _ctx_4096t * jax.lax.rsqrt(jnp.mean(jnp.square(_ctx_4096t)) + 1e-12) * 0.953939
        ctx_4096 = -1.52775e-05 + 0.999936 * (_ctx_4096t + 0.3 * jax.random.normal(jax.random.fold_in(_rk, 611), (8, 128, 512), jnp.float32))
        pos_BxS2 = jnp.broadcast_to(jnp.arange(128, dtype=jnp.int32), (8, 128))
        _validS = jnp.arange(128)[None, :] < _lenS[:, None]
        _validS2 = jnp.arange(128)[None, :] < _lenS2[:, None]
        _causal = jnp.tril(jnp.ones((128, 128), dtype=bool))
        mask_Bx1x4096_ff1 = jnp.where(jnp.ones((8, 1, 512), dtype=bool), 1.0, 0.0).astype(jnp.float32)
        mask_BxSxS2_ik0 = jnp.where(jnp.broadcast_to(_validS2[:, None, :], (8, 128, 128)), 0, 1).astype(jnp.int32)
        return (x, ctx_4096, pos_BxS2, mask_Bx1x4096_ff1, mask_BxSxS2_ik0)
    x, ctx_4096, pos_BxS2, mask_Bx1x4096_ff1, mask_BxSxS2_ik0 = _rec_inputs()

    def _L0_xattn_setup():
        import jax, jax.numpy as jnp
        import numpy as np
        W = 128
        H = 8
        D = 128
        DK = D // 2

        def _to_patches(x):
            b, d, s = x.shape
            np_ = s // W
            return x.reshape(b, d, np_, W).transpose(0, 2, 1, 3).reshape(b * np_, d, W)
        key = jax.random.key(seed)
        ks = jax.random.split(key, 10)
        B, S = (8, 512)
        qk = jax.random.normal(ks[0], (B, D, S), dtype=jnp.float32)
        v = jax.random.normal(ks[1], (B, D, S), dtype=jnp.float32)
        masks = jnp.ones((B, 1, S), dtype=jnp.float32)
        sc = 1.0 / np.sqrt(D)
        Wq = jax.random.normal(ks[2], (DK, D), dtype=jnp.float32) * sc
        bq = jnp.zeros((DK,), dtype=jnp.float32)
        Wk = jax.random.normal(ks[3], (DK, D), dtype=jnp.float32) * sc
        bk = jnp.zeros((DK,), dtype=jnp.float32)
        Wv = jax.random.normal(ks[4], (DK, D), dtype=jnp.float32) * sc
        bv = jnp.zeros((DK,), dtype=jnp.float32)
        Wo = jax.random.normal(ks[5], (D, DK), dtype=jnp.float32) * (1.0 / np.sqrt(DK))
        bo = jnp.zeros((D,), dtype=jnp.float32)
        return dict(qk=qk, v=v, masks=masks, Wq=Wq, bq=bq, Wk=Wk, bk=bk, Wv=Wv, bv=bv, Wo=Wo, bo=bo)
    _L0_xattn_all = _L0_xattn_setup()
    _L0_xattn_in = {k: v for k, v in _L0_xattn_all.items() if k in ('Wq', 'bq', 'Wk', 'bk', 'Wv', 'bv', 'Wo', 'bo')}
    del _L0_xattn_all

    def _L0_ffn_setup():
        import jax, jax.numpy as jnp
        import numpy as np
        ALPHA = 32
        R = 16
        SCALING = ALPHA / R
        key = jax.random.key(seed)
        k1, k2, k3, k4 = jax.random.split(key, 4)
        B_, S, D = (4, 256, 512)
        H, r, O = (8, R, 512)
        x = jax.random.normal(k1, (B_, S, D), dtype=jnp.float32)
        A = jax.random.normal(k2, (H, r, D), dtype=jnp.float32) * 0.02
        Bm = jax.random.normal(k3, (H, O, r), dtype=jnp.float32) * 0.02
        Wr = jax.random.normal(k4, (H, D), dtype=jnp.float32) * 0.02
        br = jnp.zeros((H,), dtype=jnp.float32)
        return {'x': x, 'A': A, 'B': Bm, 'Wr': Wr, 'br': br}
    _L0_ffn_all = _L0_ffn_setup()
    _L0_ffn_in = {k: v for k, v in _L0_ffn_all.items() if k in ('A', 'B', 'Wr', 'br')}
    del _L0_ffn_all

    def _L1_xattn_setup():
        import jax, jax.numpy as jnp
        import numpy as np
        import math
        EPS = 1e-05
        LAMBDA = 0.6

        def _crucial_k(C):
            f = math.floor(LAMBDA * C)
            return f + f % 2

        def _conv1d(y, w):
            return jax.lax.conv_general_dilated(y, w, window_strides=(1,), padding=((3, 3),), dimension_numbers=('NCH', 'OIH', 'NCH'))

        def _norm_active(z, gamma, beta):
            mu = jnp.mean(z, axis=(0, 2), keepdims=True)
            var = jnp.mean((z - mu) ** 2, axis=(0, 2), keepdims=True)
            zn = (z - mu) * jax.lax.rsqrt(var + EPS)
            zn = zn * gamma.reshape(1, -1, 1) + beta.reshape(1, -1, 1)
            return jax.nn.sigmoid(jax.nn.relu(zn))
        key = jax.random.key(seed)
        k1, k2, k3 = jax.random.split(key, 3)
        B, C, L = (32, 32, 512)
        x = jax.random.normal(k1, (B, C, L), dtype=jnp.float32)
        channel_map = jax.random.normal(k2, (B, C, L), dtype=jnp.float32)
        fan_in = 2 * 7
        bound = 1.0 / math.sqrt(fan_in)
        conv_w = jax.random.uniform(k3, (1, 2, 7), jnp.float32, -bound, bound)
        bn_gamma = jnp.ones((1,), jnp.float32)
        bn_beta = jnp.zeros((1,), jnp.float32)
        return {'x': x, 'channel_map': channel_map, 'conv_w': conv_w, 'bn_gamma': bn_gamma, 'bn_beta': bn_beta}
    _L1_xattn_all = _L1_xattn_setup()
    _L1_xattn_in = {k: v for k, v in _L1_xattn_all.items() if k in ('conv_w', 'bn_gamma', 'bn_beta')}
    del _L1_xattn_all

    def _L1_ffn_setup():
        import jax, jax.numpy as jnp
        import numpy as np
        B, S, D, O, E, R = (2, 512, 512, 512, 8, 16)
        TOP_K = 2
        SCALING = 32.0 / 16.0
        key = jax.random.key(seed)
        k = jax.random.split(key, 6)
        x = jax.random.normal(k[0], (B, S, D), dtype=jnp.float32)
        W_base = jax.random.normal(k[1], (O, D), dtype=jnp.float32) * 0.02
        b_base = jax.random.normal(k[2], (O,), dtype=jnp.float32) * 0.02
        W_router = jax.random.normal(k[3], (E, D), dtype=jnp.float32) * 0.01
        lora_A = jax.random.normal(k[4], (E, R, D), dtype=jnp.float32) * (1.0 / np.sqrt(D))
        lora_B = jax.random.normal(k[5], (E, O, R), dtype=jnp.float32) * 0.02
        return {'x': x, 'W_base': W_base, 'b_base': b_base, 'W_router': W_router, 'lora_A': lora_A, 'lora_B': lora_B}
    _L1_ffn_all = _L1_ffn_setup()
    _L1_ffn_in = {k: v for k, v in _L1_ffn_all.items() if k in ('W_base', 'b_base', 'W_router', 'lora_A', 'lora_B')}
    del _L1_ffn_all

    def _L2_xattn_setup():
        import jax, jax.numpy as jnp
        import numpy as np
        DIM = 512
        NUM_HEADS = 32
        NUM_KV_HEADS = 8
        HEAD_DIM = DIM // NUM_HEADS
        KV_DIM = DIM // (NUM_HEADS // NUM_KV_HEADS)
        B, S = (1, 256)
        key = jax.random.key(seed)
        ks = jax.random.split(key, 7)
        w_scale = DIM ** (-0.5)
        return {'query': jax.random.normal(ks[0], (B, S, DIM), jnp.float32), 'key': jax.random.normal(ks[1], (B, S, DIM), jnp.float32), 'value': jax.random.normal(ks[2], (B, S, DIM), jnp.float32), 'Wq': jax.random.normal(ks[3], (DIM, DIM), jnp.float32) * w_scale, 'Wk': jax.random.normal(ks[4], (DIM, KV_DIM), jnp.float32) * w_scale, 'Wv': jax.random.normal(ks[5], (DIM, KV_DIM), jnp.float32) * w_scale, 'Wo': jax.random.normal(ks[6], (DIM, DIM), jnp.float32) * w_scale}
    _L2_xattn_all = _L2_xattn_setup()
    _L2_xattn_in = {k: v for k, v in _L2_xattn_all.items() if k in ('Wq', 'Wk', 'Wv', 'Wo')}
    del _L2_xattn_all

    def _L2_ffn_setup():
        import jax, jax.numpy as jnp
        import numpy as np
        D = 512
        F = 1376
        B, S = (4, 256)
        key = jax.random.key(seed)
        k_x, k_g, k_u, k_d = jax.random.split(key, 4)
        scale = 0.02
        return {'x': jax.random.normal(k_x, (B, S, D), dtype=jnp.float32), 'W_gate': jax.random.normal(k_g, (F, D), dtype=jnp.float32) * scale, 'W_up': jax.random.normal(k_u, (F, D), dtype=jnp.float32) * scale, 'W_down': jax.random.normal(k_d, (D, F), dtype=jnp.float32) * scale}
    _L2_ffn_all = _L2_ffn_setup()
    _L2_ffn_in = {k: v for k, v in _L2_ffn_all.items() if k in ('W_gate', 'W_up', 'W_down')}
    del _L2_ffn_all

    def _L3_xattn_setup():
        import jax, jax.numpy as jnp
        import numpy as np
        B, S, E = (2, 256, 512)
        H, KVH, D = (32, 8, 128)
        GROUPS = H // KVH
        MAX_POS = 512
        ROPE_THETA = 10000.0

        def _rope_tables(max_pos, dim, theta):
            inv_freq = 1.0 / theta ** (jnp.arange(0, dim, 2, dtype=jnp.float32) / dim)
            t = jnp.arange(max_pos, dtype=jnp.float32)
            freqs = jnp.einsum('i,j->ij', t, inv_freq)
            emb = jnp.concatenate([freqs, freqs], axis=-1)
            return (jnp.cos(emb), jnp.sin(emb))

        def _rotate_half(x):
            x1, x2 = (x[..., :x.shape[-1] // 2], x[..., x.shape[-1] // 2:])
            return jnp.concatenate([-x2, x1], axis=-1)
        key = jax.random.key(seed)
        ks = jax.random.split(key, 8)
        scale_w = 1.0 / np.sqrt(E)
        query = jax.random.normal(ks[0], (B, S, E), dtype=jnp.float32)
        k_in = jax.random.normal(ks[1], (B, S, E), dtype=jnp.float32)
        v_in = jax.random.normal(ks[2], (B, S, E), dtype=jnp.float32)
        position_ids = jnp.broadcast_to(jnp.arange(S, dtype=jnp.int64), (B, S))
        src_mask = jnp.tril(jnp.ones((S, S), dtype=jnp.int32))
        src_mask = jnp.broadcast_to(src_mask, (B, S, S))
        Wq = jax.random.normal(ks[3], (E, H * D), dtype=jnp.float32) * scale_w
        Wk = jax.random.normal(ks[4], (E, KVH * D), dtype=jnp.float32) * scale_w
        Wv = jax.random.normal(ks[5], (E, KVH * D), dtype=jnp.float32) * scale_w
        Wo = jax.random.normal(ks[6], (H * D, E), dtype=jnp.float32) * scale_w
        return {'query': query, 'key': k_in, 'value': v_in, 'position_ids': position_ids, 'src_mask': src_mask, 'Wq': Wq, 'Wk': Wk, 'Wv': Wv, 'Wo': Wo}
    _L3_xattn_all = _L3_xattn_setup()
    _L3_xattn_in = {k: v for k, v in _L3_xattn_all.items() if k in ('Wq', 'Wk', 'Wv', 'Wo')}
    del _L3_xattn_all

    def _L3_ffn_setup():
        import jax, jax.numpy as jnp
        import numpy as np
        B, L, H, Dh, M = (4, 256, 16, 32, 128)
        D = H * Dh
        key = jax.random.key(seed)
        kx, ku, kd, kp = jax.random.split(key, 4)
        x = jax.random.normal(kx, (B, L, D), dtype=jnp.float32)
        up = jax.random.normal(ku, (H, Dh, M), dtype=jnp.float32)
        down = jax.random.normal(kd, (H, M, Dh), dtype=jnp.float32)
        perm = jax.random.permutation(kp, D)
        return {'x': x, 'up': up, 'down': down, 'perm': perm}
    _L3_ffn_all = _L3_ffn_setup()
    _L3_ffn_in = {k: v for k, v in _L3_ffn_all.items() if k in ('up', 'down', 'perm')}
    del _L3_ffn_all
    return {'x': x, 'ctx_4096': ctx_4096, 'pos_BxS2': pos_BxS2, 'mask_Bx1x4096_ff1': mask_Bx1x4096_ff1, 'mask_BxSxS2_ik0': mask_BxSxS2_ik0, 'L0_xattn_Wq': _L0_xattn_in['Wq'], 'L0_xattn_bq': _L0_xattn_in['bq'], 'L0_xattn_Wk': _L0_xattn_in['Wk'], 'L0_xattn_bk': _L0_xattn_in['bk'], 'L0_xattn_Wv': _L0_xattn_in['Wv'], 'L0_xattn_bv': _L0_xattn_in['bv'], 'L0_xattn_Wo': _L0_xattn_in['Wo'], 'L0_xattn_bo': _L0_xattn_in['bo'], 'L0_ffn_A': _L0_ffn_in['A'], 'L0_ffn_B': _L0_ffn_in['B'], 'L0_ffn_Wr': _L0_ffn_in['Wr'], 'L0_ffn_br': _L0_ffn_in['br'], 'L1_xattn_conv_w': _L1_xattn_in['conv_w'], 'L1_xattn_bn_gamma': _L1_xattn_in['bn_gamma'], 'L1_xattn_bn_beta': _L1_xattn_in['bn_beta'], 'L1_ffn_W_base': _L1_ffn_in['W_base'], 'L1_ffn_b_base': _L1_ffn_in['b_base'], 'L1_ffn_W_router': _L1_ffn_in['W_router'], 'L1_ffn_lora_A': _L1_ffn_in['lora_A'], 'L1_ffn_lora_B': _L1_ffn_in['lora_B'], 'L2_xattn_Wq': _L2_xattn_in['Wq'], 'L2_xattn_Wk': _L2_xattn_in['Wk'], 'L2_xattn_Wv': _L2_xattn_in['Wv'], 'L2_xattn_Wo': _L2_xattn_in['Wo'], 'L2_ffn_W_gate': _L2_ffn_in['W_gate'], 'L2_ffn_W_up': _L2_ffn_in['W_up'], 'L2_ffn_W_down': _L2_ffn_in['W_down'], 'L3_xattn_Wq': _L3_xattn_in['Wq'], 'L3_xattn_Wk': _L3_xattn_in['Wk'], 'L3_xattn_Wv': _L3_xattn_in['Wv'], 'L3_xattn_Wo': _L3_xattn_in['Wo'], 'L3_ffn_up': _L3_ffn_in['up'], 'L3_ffn_down': _L3_ffn_in['down'], 'L3_ffn_perm': _L3_ffn_in['perm']}

def reference(x, ctx_4096, pos_BxS2, mask_Bx1x4096_ff1, mask_BxSxS2_ik0, L0_xattn_Wq, L0_xattn_bq, L0_xattn_Wk, L0_xattn_bk, L0_xattn_Wv, L0_xattn_bv, L0_xattn_Wo, L0_xattn_bo, L0_ffn_A, L0_ffn_B, L0_ffn_Wr, L0_ffn_br, L1_xattn_conv_w, L1_xattn_bn_gamma, L1_xattn_bn_beta, L1_ffn_W_base, L1_ffn_b_base, L1_ffn_W_router, L1_ffn_lora_A, L1_ffn_lora_B, L2_xattn_Wq, L2_xattn_Wk, L2_xattn_Wv, L2_xattn_Wo, L2_ffn_W_gate, L2_ffn_W_up, L2_ffn_W_down, L3_xattn_Wq, L3_xattn_Wk, L3_xattn_Wv, L3_xattn_Wo, L3_ffn_up, L3_ffn_down, L3_ffn_perm):
    import jax
    import jax.numpy as jnp

    def _L0_xattn_ref(qk, v, masks, Wq, bq, Wk, bk, Wv, bv, Wo, bo):
        import jax, jax.numpy as jnp
        import numpy as np
        W = 128
        H = 8
        D = 128
        DK = D // 2

        def _to_patches(x):
            b, d, s = x.shape
            np_ = s // W
            return x.reshape(b, d, np_, W).transpose(0, 2, 1, 3).reshape(b * np_, d, W)
        B, _, S = qk.shape
        np_ = S // W
        qp = _to_patches(qk)
        vp = _to_patches(v)
        mp = _to_patches(masks)
        q = jnp.einsum('ed,bdw->bew', Wq, qp) + bq[:, None]
        k = jnp.einsum('ed,bdw->bew', Wk, qp) + bk[:, None]
        val = jnp.einsum('ed,bdw->bew', Wv, vp) + bv[:, None]
        BN = q.shape[0]
        dh = DK // H
        qh = q.reshape(BN, H, dh, W)
        kh = k.reshape(BN, H, dh, W)
        vh = val.reshape(BN, H, dh, W)
        scores = jnp.einsum('bhdi,bhdj->bhij', qh, kh) / jnp.sqrt(jnp.asarray(dh, qh.dtype))
        scores = jnp.where(mp[:, :, None, :] > 0, scores, jnp.asarray(-1000000000.0, scores.dtype))
        attn = jax.nn.softmax(scores, axis=-1)
        o = jnp.einsum('bhij,bhdj->bhdi', attn, vh).reshape(BN, DK, W)
        o = jax.nn.gelu(o, approximate=False)
        out = jnp.einsum('de,bew->bdw', Wo, o) + bo[:, None]
        out = out.reshape(B, np_, D, W).transpose(0, 2, 1, 3).reshape(B, D, S)
        out = out * masks
        return out

    def _L0_ffn_ref(x, A, B, Wr, br):
        import jax, jax.numpy as jnp
        import numpy as np
        ALPHA = 32
        R = 16
        SCALING = ALPHA / R
        H = A.shape[0]
        router_logits = jnp.einsum('bsd,hd->bsh', x, Wr) + br
        scores = H * jax.nn.softmax(router_logits, axis=-1)
        low = jnp.einsum('bsd,hrd->bshr', x, A)
        out = jnp.einsum('bshr,hor,bsh->bso', low, B, scores)
        return SCALING * out

    def _L1_xattn_ref(x, channel_map, conv_w, bn_gamma, bn_beta):
        import jax, jax.numpy as jnp
        import numpy as np
        import math
        EPS = 1e-05
        LAMBDA = 0.6

        def _crucial_k(C):
            f = math.floor(LAMBDA * C)
            return f + f % 2

        def _conv1d(y, w):
            return jax.lax.conv_general_dilated(y, w, window_strides=(1,), padding=((3, 3),), dimension_numbers=('NCH', 'OIH', 'NCH'))

        def _norm_active(z, gamma, beta):
            mu = jnp.mean(z, axis=(0, 2), keepdims=True)
            var = jnp.mean((z - mu) ** 2, axis=(0, 2), keepdims=True)
            zn = (z - mu) * jax.lax.rsqrt(var + EPS)
            zn = zn * gamma.reshape(1, -1, 1) + beta.reshape(1, -1, 1)
            return jax.nn.sigmoid(jax.nn.relu(zn))
        B, C, L = x.shape
        k = _crucial_k(C)
        cm = jnp.moveaxis(channel_map, 1, 2)
        _, topk_idx = jax.lax.top_k(cm, k)
        b_idx = jnp.arange(B)[:, None, None]
        l_idx = jnp.arange(L)[None, :, None]
        mask = jnp.zeros((B, L, C), x.dtype).at[b_idx, l_idx, topk_idx].set(1.0)
        crucial_channels = jnp.moveaxis(mask, 2, 1)
        subcrucial_channels = 1.0 - crucial_channels
        crucial_features = crucial_channels * x
        subcrucial_features = subcrucial_channels * x
        c_max = jnp.max(crucial_features, axis=1, keepdims=True)
        c_avg = jnp.mean(crucial_features, axis=1, keepdims=True) * (C / k)
        s_max = jnp.max(subcrucial_features, axis=1, keepdims=True)
        s_avg = jnp.mean(subcrucial_features, axis=1, keepdims=True) * (C / (C - k))
        crucial_x = jnp.concatenate([c_max, c_avg], axis=1)
        subcrucial_x = jnp.concatenate([s_max, s_avg], axis=1)
        A_S1 = _norm_active(_conv1d(crucial_x, conv_w), bn_gamma, bn_beta)
        A_S2 = _norm_active(_conv1d(subcrucial_x, conv_w), bn_gamma, bn_beta)
        return crucial_features * A_S1 + subcrucial_features * A_S2

    def _L1_ffn_ref(x, W_base, b_base, W_router, lora_A, lora_B):
        import jax, jax.numpy as jnp
        import numpy as np
        B, S, D, O, E, R = (2, 512, 512, 512, 8, 16)
        TOP_K = 2
        SCALING = 32.0 / 16.0
        d = x.shape[-1]
        n_experts = W_router.shape[0]
        xf = x.reshape(-1, d)
        logits = xf @ W_router.T
        probs = jax.nn.softmax(logits, axis=-1)
        topk_p, topk_i = jax.lax.top_k(probs, TOP_K)
        topk_p = topk_p / jnp.sum(topk_p, axis=-1, keepdims=True)
        w = jnp.sum(jax.nn.one_hot(topk_i, n_experts, dtype=xf.dtype) * topk_p[..., None], axis=1)
        h = jnp.einsum('td,erd->ter', xf, lora_A)
        lora_out = jnp.einsum('ter,eor,te->to', h, lora_B, w) * SCALING
        base = x @ W_base.T + b_base
        return base + lora_out.reshape(x.shape[:-1] + (W_base.shape[0],))

    def _L2_xattn_ref(query, key, value, Wq, Wk, Wv, Wo):
        import jax, jax.numpy as jnp
        import numpy as np
        DIM = 512
        NUM_HEADS = 32
        NUM_KV_HEADS = 8
        HEAD_DIM = DIM // NUM_HEADS
        KV_DIM = DIM // (NUM_HEADS // NUM_KV_HEADS)
        B, S = (1, 256)
        b, sq, _ = query.shape
        _, sk, _ = key.shape
        rep = NUM_HEADS // NUM_KV_HEADS
        q = (query @ Wq).reshape(b, sq, NUM_HEADS, HEAD_DIM).transpose(0, 2, 1, 3)
        k = (key @ Wk).reshape(b, sk, NUM_KV_HEADS, HEAD_DIM).transpose(0, 2, 1, 3)
        v = (value @ Wv).reshape(b, sk, NUM_KV_HEADS, HEAD_DIM).transpose(0, 2, 1, 3)
        k = jnp.repeat(k, rep, axis=1)
        v = jnp.repeat(v, rep, axis=1)
        scale = HEAD_DIM ** (-0.5)
        scores = jnp.einsum('bhqd,bhkd->bhqk', q, k) * scale
        probs = jax.nn.softmax(scores, axis=-1)
        out = jnp.einsum('bhqk,bhkd->bhqd', probs, v)
        out = out.transpose(0, 2, 1, 3).reshape(b, sq, DIM)
        return out @ Wo

    def _L2_ffn_ref(x, W_gate, W_up, W_down):
        import jax, jax.numpy as jnp
        import numpy as np
        D = 512
        F = 1376
        B, S = (4, 256)
        out_shape = x.shape[:-1] + (W_down.shape[0],)
        xt = x.reshape(-1, x.shape[-1])
        up = xt @ W_up.T
        gate = jax.nn.silu(xt @ W_gate.T)
        y = gate * up @ W_down.T
        return y.reshape(out_shape)

    def _L3_xattn_ref(query, key, value, position_ids, src_mask, Wq, Wk, Wv, Wo):
        import jax, jax.numpy as jnp
        import numpy as np
        B, S, E = (2, 256, 512)
        H, KVH, D = (32, 8, 128)
        GROUPS = H // KVH
        MAX_POS = 512
        ROPE_THETA = 10000.0

        def _rope_tables(max_pos, dim, theta):
            inv_freq = 1.0 / theta ** (jnp.arange(0, dim, 2, dtype=jnp.float32) / dim)
            t = jnp.arange(max_pos, dtype=jnp.float32)
            freqs = jnp.einsum('i,j->ij', t, inv_freq)
            emb = jnp.concatenate([freqs, freqs], axis=-1)
            return (jnp.cos(emb), jnp.sin(emb))

        def _rotate_half(x):
            x1, x2 = (x[..., :x.shape[-1] // 2], x[..., x.shape[-1] // 2:])
            return jnp.concatenate([-x2, x1], axis=-1)
        nb, q_len, _ = query.shape
        q = (query @ Wq).reshape(nb, q_len, H, D).transpose(0, 2, 1, 3)
        k = (key @ Wk).reshape(nb, q_len, KVH, D).transpose(0, 2, 1, 3)
        v = (value @ Wv).reshape(nb, q_len, KVH, D).transpose(0, 2, 1, 3)
        cos_t, sin_t = _rope_tables(MAX_POS, D, ROPE_THETA)
        cos = cos_t[position_ids][:, None]
        sin = sin_t[position_ids][:, None]
        q = q * cos + _rotate_half(q) * sin
        k = k * cos + _rotate_half(k) * sin
        k = jnp.repeat(k, GROUPS, axis=1)
        v = jnp.repeat(v, GROUPS, axis=1)
        scores = jnp.einsum('bhqd,bhkd->bhqk', q, k) / jnp.sqrt(jnp.float32(D))
        mask = src_mask[:, None]
        scores = jnp.where(mask == 0, jnp.float32(-1000000000.0), scores)
        attn = jax.nn.softmax(scores, axis=-1)
        x = jnp.einsum('bhqk,bhkd->bhqd', attn, v)
        x = x.transpose(0, 2, 1, 3).reshape(nb, q_len, H * D)
        return x @ Wo

    def _L3_ffn_ref(x, up, down, perm):
        import jax, jax.numpy as jnp
        import numpy as np
        B, L, H, Dh, M = (4, 256, 16, 32, 128)
        D = H * Dh
        b, l, Dm = x.shape
        h, d = (up.shape[0], up.shape[1])
        unperm = jnp.argsort(perm)
        t = x.reshape(b * l, Dm)
        t = t[:, perm]
        t = t.reshape(b * l, h, d)
        t = jnp.einsum('bhd,hdm->bhm', t, up)
        t = jax.nn.gelu(t, approximate=False)
        t = jnp.einsum('bhm,hmd->bhd', t, down)
        t = t.reshape(b * l, h * d)
        t = t[:, unperm]
        out = t.reshape(b, l, Dm)
        return out
    x = x + _L0_xattn_ref(_layernorm(x, axis=-1), ctx_4096, mask_Bx1x4096_ff1, L0_xattn_Wq, L0_xattn_bq, L0_xattn_Wk, L0_xattn_bk, L0_xattn_Wv, L0_xattn_bv, L0_xattn_Wo, L0_xattn_bo)
    x = x + _L0_ffn_ref(_layernorm(x, axis=-1), L0_ffn_A, L0_ffn_B, L0_ffn_Wr, L0_ffn_br)
    x = x + _L1_xattn_ref(_layernorm(x, axis=-1), ctx_4096, L1_xattn_conv_w, L1_xattn_bn_gamma, L1_xattn_bn_beta)
    x = x + _L1_ffn_ref(_layernorm(x, axis=-1), L1_ffn_W_base, L1_ffn_b_base, L1_ffn_W_router, L1_ffn_lora_A, L1_ffn_lora_B)
    x = x + _L2_xattn_ref(_layernorm(x, axis=-1), ctx_4096, ctx_4096, L2_xattn_Wq, L2_xattn_Wk, L2_xattn_Wv, L2_xattn_Wo)
    x = x + _L2_ffn_ref(_layernorm(x, axis=-1), L2_ffn_W_gate, L2_ffn_W_up, L2_ffn_W_down)
    x = x + _L3_xattn_ref(_layernorm(x, axis=-1), ctx_4096, ctx_4096, pos_BxS2, mask_BxSxS2_ik0, L3_xattn_Wq, L3_xattn_Wk, L3_xattn_Wv, L3_xattn_Wo)
    x = x + _L3_ffn_ref(_layernorm(x, axis=-1), L3_ffn_up, L3_ffn_down, L3_ffn_perm)
    return x

_drawn_inputs = setup_inputs


def setup_inputs(seed=0):
    import zlib

    import numpy as np

    out = dict(_drawn_inputs(seed))
    spreads = {'L0_xattn_bq': (0.0, 0.8),
     'L0_xattn_bk': (0.0, 2.0),
     'L0_xattn_bv': (0.0, 0.713),
     'L0_xattn_bo': (0.0, 2.0),
     'L0_ffn_br': (0.0, 0.276)}
    factors = {'L1_ffn_b_base': 6.499}
    for name, (base, spread) in spreads.items():
        noise = np.random.default_rng([zlib.crc32(name.encode()), seed]).standard_normal(out[name].shape)
        drawn = base * np.exp(spread * noise) if base else spread * noise
        out[name] = jnp.asarray(drawn.astype(out[name].dtype))
    for name, factor in factors.items():
        out[name] = (out[name] * factor).astype(out[name].dtype)
    return out
```

```python
from contextlib import ExitStack

import concourse.bass as bass
from concourse import mybir
from concourse.alu_op_type import AluOpType as ALU
import numpy as np

F32 = mybir.dt.float32
F32R = mybir.dt.float32r
BF16 = mybir.dt.bfloat16
I32 = mybir.dt.int32
ACT = mybir.ActivationFunctionType
AX = mybir.AxisListType

P = 128
B = 8
D = 512
KT = D // P
TOK = B * P
HALF = TOK // 2
F2 = 1376
FT = [P] * (F2 // P) + [F2 % P]
FGROUPS = [range(0, 4), range(4, 8), range(8, 11)]
RING, STAGE = 10, 5
N_CRUCIAL = 76
N_REST = P - N_CRUCIAL
ROUNDS = 7
DUMMY, TAKEN = 3.0e38, -3.4028234663852886e38
BIG = 1.0e9
EPS = 1e-5

U_L0F = 0
U_L1F = U_L0F + 2
U_L2X = U_L1F + 6
U_L2F = U_L2X + 15
U_L3X = U_L2F + 3 * len(FT)
U_L3F = U_L3X + 80
N_UNITS = U_L3F + 2

(C_QA, C_QM, C_KA, C_KM, C_BIG, C_RA, C_RM, C_EXT) = range(8)
C_IOTA = 8
N_CON = C_IOTA + KT
W0Q, W0K, W0V, W0O = 0, 256, 512, 576
N_W0 = 704


def constants():
    p = np.arange(P)
    con = np.zeros((P, N_CON), np.float32)
    s0 = np.float32(-1 / np.sqrt(8.0))
    hi = (p % 32) // 8 % 2 == 0
    con[:, C_QA], con[:, C_QM] = np.where(hi, s0, -s0), np.where(hi, 0, s0)
    hi = (p % 32) // 8 < 2
    con[:, C_KA], con[:, C_KM] = np.where(hi, 1, -1), np.where(hi, 0, 1)
    big_hi = np.float32(2.0 ** 18 * 3815)
    con[:, C_BIG] = np.where(p % 32 == 0, big_hi, np.where(p % 32 == 1, np.float32(BIG) - big_hi, 0))
    hi = p % 2 == 0
    con[:, C_RA], con[:, C_RM] = np.where(hi, 1, -1), np.where(hi, 0, 1)
    con[:, C_EXT] = p + 192
    for k in range(KT):
        con[:, C_IOTA + k] = p + P * k
    t = np.arange(512, dtype=np.float32)[:, None]
    inv = (1.0 / np.float32(10000.0) ** (np.arange(0, P, 2, dtype=np.float32) / np.float32(P))).astype(np.float32)
    ang = np.concatenate([t * inv, t * inv], 1).astype(np.float32)
    sin = np.sin(ang)
    sin[:, :64] *= -1
    tabs = np.stack([np.cos(ang), sin]).astype(np.float32).reshape(2, KT, P, P)
    return {"con": con, "ident": np.eye(P, dtype=np.float32), "tabs": tabs,
            "iota": np.broadcast_to(np.arange(512, dtype=np.float32), (P, 512)).copy()}


def lay_out(i):
    c = np.ascontiguousarray

    def tiles(w):
        return w.reshape(KT, P, -1).transpose(1, 0, 2).reshape(P, -1)

    def lora(a):
        return a.reshape(P, -1)

    units = [tiles(lora(i["L0_ffn_A"]).T), i["L0_ffn_B"].transpose(0, 2, 1).reshape(P, D)]
    wb = i["L1_ffn_W_base"].T
    units += [tiles(lora(i["L1_ffn_lora_A"]).T)] + [wb[k * P:(k + 1) * P] for k in range(KT)]
    units += [i["L1_ffn_lora_B"].transpose(0, 2, 1).reshape(P, D)]
    wq = i["L2_xattn_Wq"].reshape(D, 2, 4, 4, 16).transpose(0, 1, 3, 2, 4)
    wq = np.repeat(wq[:, :, :, :, None], 2, 4).reshape(D, 2, 4, P)
    wk = np.repeat(i["L2_xattn_Wk"].reshape(D, 2, 4, 1, 16), 2, 3).reshape(D, 2, P)
    for s in range(2):
        units += [tiles(wk[:, s])] + ([tiles(i["L2_xattn_Wv"])] if s == 0 else [])
        units += [tiles(wq[:, s, r]) for r in range(4)]
        units += [i["L2_xattn_Wo"][k * P:(k + 1) * P] for k in (2 * s, 2 * s + 1)]
    zeros = np.zeros((D, P - FT[-1]), np.float32)
    gate, up, down = i["L2_ffn_W_gate"].T, i["L2_ffn_W_up"].T, i["L2_ffn_W_down"].T
    gate, up = np.concatenate([gate, zeros], 1), np.concatenate([up, zeros], 1)
    down = np.concatenate([down, zeros.T], 0)
    for group in FGROUPS:
        for f in group:
            units += [tiles(gate[:, f * P:(f + 1) * P]), tiles(up[:, f * P:(f + 1) * P])]
        units += [down[f * P:(f + 1) * P] for f in group]
    for h in range(8):
        units += [tiles(i["L3_xattn_Wk"][:, h * P:(h + 1) * P])]
        units += [tiles(i["L3_xattn_Wq"][:, (4 * h + r) * P:(4 * h + r + 1) * P]) for r in range(4)]
        units += [tiles(i["L3_xattn_Wv"][:, h * P:(h + 1) * P])]
        units += [i["L3_xattn_Wo"][(4 * h + r) * P:(4 * h + r + 1) * P] for r in range(4)]
    units += [i["L3_ffn_up"].reshape(4, P, P).transpose(1, 0, 2).reshape(P, D)]
    units += [i["L3_ffn_down"].transpose(1, 0, 2).reshape(P, D)]
    w0 = np.concatenate([
        np.repeat(i["L0_xattn_Wq"].T.reshape(P, 8, 1, 8), 4, 2).reshape(P, 256),
        np.repeat(i["L0_xattn_Wk"].T.reshape(P, 8, 1, 8), 4, 2).reshape(P, 256), i["L0_xattn_Wv"].T,
        np.concatenate([i["L0_xattn_Wo"].T] * 2, 0)], 1)
    b0 = np.concatenate([np.repeat(i["L0_xattn_bq"].reshape(8, 1, 8), 4, 1).reshape(256),
                         np.repeat(i["L0_xattn_bk"].reshape(8, 1, 8), 4, 1).reshape(256), i["L0_xattn_bv"],
                         i["L1_ffn_b_base"]])
    context = i["ctx_4096"]
    out = {
        "x": i["x"], "context": context, "contextT": context.transpose(2, 0, 1).reshape(KT, P, TOK),
        "context_lc": context.transpose(0, 2, 1)[:, :, ::-1].reshape(32, P, P),
        "mask_row": i["mask_Bx1x4096_ff1"].reshape(B, D), "mask3": i["mask_BxSxS2_ik0"], "pos": i["pos_BxS2"].reshape(1, TOK),
        "perm_row": i["L3_ffn_perm"].reshape(1, D), "perm_col": i["L3_ffn_perm"].reshape(KT, P).T,
        "units": np.stack(units), "w0": w0, "b0": np.stack([b0, b0]), "bo": i["L0_xattn_bo"].reshape(P, 1),
        "wr": np.stack([tiles(i["L0_ffn_Wr"].T), tiles(i["L1_ffn_W_router"].T)]),
        "br": i["L0_ffn_br"].reshape(1, 8),
        "conv": np.concatenate([i["L1_xattn_conv_w"].reshape(1, 14), i["L1_xattn_bn_gamma"].reshape(1, 1),
                                i["L1_xattn_bn_beta"].reshape(1, 1)], 1),
    }
    out.update(constants())
    return {k: c(v) for k, v in out.items()}

X_BEFORE = [B * n for n in (0, 1, 2, 3, 4, 6, 9, 17)]
XD_L0A = B * 0
XD_L0F = B * 1
XD_L1X = B * 2
XD_L1F = B * 3
XD_CX = B * 4
XD_L2X = B * 4
XD_L2F = B * 6
XD_L3X = B * 9
XD_L3F = B * 17
XD_END = B * 18
LN_L0A = (0, 0)
LN_L0F = (1, 0)
LN_L1X = (2, 1)
LN_L1F = (3, 1)
LN_L2X = (4, 2)
LN_L2F = (5, 3)
LN_L3X = (6, 4)
LN_L3F = (7, 5)


class Stream:

    def __init__(self, step):
        self.step, self.next = step, 0

    def upto(self, n):
        while self.next < min(n, N_UNITS):
            self.step(self.next)
            self.next += 1


def program(nc, d, out):
    with ExitStack() as ctx:
        def sem(name):
            return ctx.enter_context(nc.semaphore(name))

        def sb(name, shape, dt=F32, where=ctx):
            return where.enter_context(nc.sbuf_tensor(name, shape, dt))

        bank = [ctx.enter_context(nc.psum_tensor(f"bank{i}", [P, 512], F32)) for i in range(8)]

        X = sb("X", [P, B, D])
        ring_h = sb("ring_h", [P, RING, 512], F32R)
        ring_l = sb("ring_l", [P, RING, 512], F32R)
        stage = sb("stage", [P, STAGE, 512])
        probs = sb("probs", [P, 3, 512])
        probsT = sb("probsT", [P, 3, 512])
        nbias = sb("nbias", [P, 4, 4])
        psums = sb("psums", [P, 4, 4])
        rsums = sb("rsums", [P, 4, 4])
        xn = sb("xn", [P, 4, D])
        ident = sb("ident", [P, P])
        con = sb("con", [P, N_CON])
        iota = sb("iota", [P, 512])
        ones_r = sb("ones_r", [P, 512], F32R)
        cosT = sb("cosT", [P, TOK])
        sinT = sb("sinT", [P, TOK])
        stats = sb("stats", [P, B, 6])
        mv = sb("mv", [P, B, 2])
        vare = sb("vare", [P, B])
        rstd = sb("rstd", [P, B])
        mhalf = sb("mhalf", [P, B])
        wr = sb("wr", [P, 2, 32])
        wrh = sb("wrh", [P, 2, 32], F32R)
        wrl = sb("wrl", [P, 2, 32], F32R)
        br = sb("br", [P, 8])
        conv = sb("conv", [P, 16])

        eA = ExitStack()
        crucial = sb("crucial", [P, 32, P], BF16, eA)
        bands = sb("bands", [P, 6, P], F32, eA)
        biasr = sb("biasr", [2, 1088], F32R, eA)

        e0 = ExitStack()
        mask0 = sb("mask0", [P, 2, D], F32, e0)
        o0T = sb("o0T", [64, B, D], F32, e0)
        topv = sb("topv", [P, 32, 132], F32, e0)
        top8 = sb("top8", [P, 4, 8], F32, e0)
        w0h = sb("w0h", [P, N_W0], F32R, e0)
        w0l = sb("w0l", [P, N_W0], F32R, e0)
        bo = sb("bo", [P, 1], F32, e0)
        w0v = sb("w0v", [P, 64], F32, e0)
        zeros_r = sb("zeros_r", [2, 64], F32R, e0)
        es = ExitStack()
        w0 = sb("w0", [P, N_W0], F32, es)
        bias_f = sb("bias_f", [2, 1088], F32, es)
        bias_a = sb("bias_a", [2, 1088], F32, es)
        tabs = sb("tabs", [P, 2, KT, P], F32, es)
        pos_i = sb("pos_i", [P, TOK], I32, es)
        hot = sb("hot", [P, KT, TOK], F32, es)
        es.close()
        ea = ExitStack()
        xnh = sb("xnh", [P, 2, D], F32R, ea)
        xnl = sb("xnl", [P, 2, D], F32R, ea)
        keep = sb("keep", [P, D], F32, ea)
        mrow = sb("mrow", [P, 2, D], F32R, ea)
        q0 = sb("q0", [P, 2, 2, D], F32R, ea)
        k0 = sb("k0", [P, 2, 2, D], F32R, ea)
        halfA = sb("halfA", [P, D], F32, ea)
        v0 = sb("v0", [P, 2, 4, 8 * 72], F32, ea)
        ea.close()
        eo = ExitStack()
        g0 = sb("g0", [64, 2, D], F32, eo)
        g0h = sb("g0h", [64, 2, D], F32R, eo)
        g0l = sb("g0l", [64, 2, D], F32R, eo)
        upd = sb("upd", [P, 2, D], F32, eo)
        eo.close()
        e0.close()

        ef = ExitStack()
        xTh_a = sb("xTh_a", [P, KT, TOK], F32R, ef)
        xTl_a = sb("xTl_a", [P, KT, TOK], F32R, ef)
        low = sb("low", [P, B, P], F32, ef)
        lowT_h = sb("lowT_h", [P, TOK], F32R, ef)
        lowT_l = sb("lowT_l", [P, TOK], F32R, ef)
        lg = sb("lg", [P, B, 14], F32, ef)
        rt = sb("rt", [P, 4, B], F32, ef)
        sc = sb("sc", [P, 2, B, 8], F32, ef)
        t8 = sb("t8", [P, B, 8], F32, ef)
        ef.close()

        ex = ExitStack()
        xnf = sb("xnf", [P, B, D], F32, ex)
        cf = sb("cf", [P, 2, 2, 512], F32, ex)
        rows = sb("rows", [P, 2, 2, B, 6], F32, ex)
        junk = sb("junk", [P, 2, 4, P], F32, ex)
        z = sb("z", [P, 2, 32], F32, ex)
        zz = sb("zz", [P, 2, 32], F32, ex)
        zs = sb("zs", [P, 8, 2], F32, ex)
        gains = sb("gains", [P, 3, 32], F32, ex)
        gT = sb("gT", [P, 2, 512], F32, ex)
        tmpx = sb("tmpx", [P, 2, 512], F32, ex)
        shift = sb("shift", [P, 512], F32, ex)
        ones_f = sb("ones_f", [P, P], F32, ex)
        ex.close()
        eA.close()

        eB = ExitStack()
        xTh_b = sb("xTh_b", [P, KT, TOK], F32R, eB)
        xTl_b = sb("xTl_b", [P, KT, TOK], F32R, eB)
        cx = ExitStack()
        cTh = sb("cTh", [P, KT, TOK], F32R, cx)
        cTl = sb("cTl", [P, KT, TOK], F32R, cx)
        e2 = ExitStack()
        q2 = sb("q2", [P, 4, TOK], F32, e2)
        k2 = sb("k2", [P, TOK], F32, e2)
        v2 = sb("v2", [P, B, 8, 17], F32, e2)
        on2 = sb("on2", [P, 2, 256], F32, e2)
        rec2 = sb("rec2", [P, 16], F32, e2)
        onT_h = sb("onT_h", [P, 2, 256], F32R, e2)
        onT_l = sb("onT_l", [P, 2, 256], F32R, e2)
        e2.close()
        eg = ExitStack()
        silu = sb("silu", [P, 2, 512], F32, eg)
        hid = sb("hid", [P, 2, 512], F32, eg)
        hid_h = sb("hid_h", [P, 4, TOK], F32R, eg)
        hid_l = sb("hid_l", [P, 4, TOK], F32R, eg)
        eg.close()
        e3 = ExitStack()
        q3 = sb("q3", [P, 4, TOK], F32, e3)
        k3 = sb("k3", [P, TOK], F32, e3)
        v3 = sb("v3", [P, B, P], F32, e3)
        vT = sb("vT", [P, 2, 512], F32, e3)
        o3h = sb("o3h", [P, 2, 512], F32R, e3)
        o3l = sb("o3l", [P, 2, 512], F32R, e3)
        mask3 = sb("mask3", [P, B, P], I32, e3)
        big = sb("big", [P, P], F32, e3)
        e3.close()
        cx.close()
        e4 = ExitStack()
        tTh = sb("tTh", [P, 4, TOK], F32R, e4)
        tTl = sb("tTl", [P, 4, TOK], F32R, e4)
        pick = sb("pick", [P, KT, 512], F32R, e4)
        put = sb("put", [P, KT, 512], F32R, e4)
        perm_i = sb("perm_i", [P, 520], I32, e4)
        down_h = sb("down_h", [P, 16, P], F32R, e4)
        down_l = sb("down_l", [P, 16, P], F32R, e4)
        gel_h = sb("gel_h", [P, 2, 512], F32R, e4)
        gel_l = sb("gel_l", [P, 2, 512], F32R, e4)
        e4.close()
        eB.close()
        t2h, t2l = xTh_b, xTl_b
        kkeep, ctx_n = stage[:, 2, :], stage[:, 3:5, :]
        gel = probs
        perm_f = probsT[:].rearrange("p a b -> p (a b)")

        def f32(ap):
            return ap.bitcast(F32)

        s_con = sem("s_con")
        s_x = sem("s_x")
        s_w0 = sem("s_w0")
        s_tab = sem("s_tab")
        s_rest = sem("s_rest")
        s_topv = sem("s_topv")
        s_ctx = [sem(f"s_ctx{i}") for i in range(2)]
        s_m0 = [sem(f"s_m0{i}") for i in range(2)]
        s_unit = [sem(f"s_unit{i}") for i in range(STAGE)]
        s_ctxT = [sem(f"s_ctxT{i}") for i in range(2)]
        s_m3 = sem("s_m3")
        s_perm = sem("s_perm")
        s_out = sem("s_out")
        w_hi = sem("w_hi")
        w_lo = sem("w_lo")
        w_used = sem("w_used")
        v_chain = sem("v_chain")
        a_chain = sem("a_chain")
        p_chain = sem("p_chain")
        ln_mv, ln_rstd, ln_xn, ln_t, ln_hi, ln_lo = [sem(f"ln_{n}") for n in ("mv", "rstd", "xn", "t", "hi", "lo")]
        x_done = sem("x_done")

        chains = {}

        def link(eng, chain, ins):
            chains[chain.name] = chains.get(chain.name, 0) + 1
            ins.then_inc(chain, 1)
            eng.wait_ge(chain, chains[chain.name])

        owed = [0]

        def mm3(out_ap, wh, wl, mh, ml, start, stop):
            ins = nc.tensor.matmul(out_ap, wh, mh, start=start, stop=False)
            if owed[0]:
                ins.then_inc(w_used, owed[0])
                owed[0] = 0
            nc.tensor.matmul(out_ap, wh, ml, start=False, stop=False)
            return nc.tensor.matmul(out_ap, wl, mh, start=False, stop=stop)

        def slot(u):
            return ring_h[:, u % RING, :], ring_l[:, u % RING, :]

        def col(k, parts=slice(None)):
            return con[parts, k:k + 1]

        def ln_stats(v, n_ln):
            if X_BEFORE[n_ln]:
                v.wait_ge(x_done, X_BEFORE[n_ln])
            for b in range(B):
                ins = nc.vector.bn_stats(stats[:, b, :], X[:, b, :])
            link(v, v_chain, ins)
            for b in range(B):
                ins = nc.vector.bn_aggr(mv[:, b, :], stats[:, b, :])
            ins.then_inc(ln_mv, 1)
            v.wait_ge(ln_rstd, n_ln + 1)
            v.wait_ge(ln_mv, n_ln + 1)

        def ln_pool(g, n_ln):
            g.wait_ge(ln_mv, n_ln + 1)
            link(g, p_chain, nc.gpsimd.tensor_scalar(vare[:, :], mv[:, :, 1], EPS, 1.0, ALU.add, ALU.mult))
            nc.gpsimd.tensor_tensor(rstd[:, :], vare[:, :], mhalf[:, :], ALU.pow).then_inc(ln_rstd, 1)

        def ln_norm(b, to):
            return nc.vector.tensor_scalar(to, X[:, b, :], mv[:, b, 0:1], rstd[:, b:b + 1], ALU.subtract, ALU.mult)

        def by_tile(ap):
            return ap.rearrange("p (k t) -> p k t", k=KT)

        def ln_dve(v, n_ln, n, th, tl):
            def low_half(b):
                v.wait_ge(ln_hi, B * n + b + 1)
                cut = slice(b * P, (b + 1) * P)
                nc.vector.tensor_tensor(tl[:, :, cut], by_tile(bank[6 + b % 2][:]),
                                        f32(th[:, :, cut]), ALU.subtract).then_inc(ln_lo, 1)

            ln_stats(v, n_ln)
            for b in range(B):
                if b >= 4:
                    v.wait_ge(ln_t, B * n + b - 3)
                ln_norm(b, xn[:, b % 4, :]).then_inc(ln_xn, 1)
                if b >= 2:
                    low_half(b - 2)
            low_half(B - 2)
            low_half(B - 1)

        def ln_pe(t, n):
            for b in range(B):
                t.wait_ge(ln_xn, B * n + b + 1)
                if b >= 2:
                    t.wait_ge(ln_lo, B * n + b - 1)
                for k in range(KT):
                    ins = nc.tensor.transpose(bank[6 + b % 2][:, k * P:(k + 1) * P],
                                              xn[:, b % 4, k * P:(k + 1) * P], ident[:, :])
                ins.then_inc(ln_t, 1)

        def ln_act(a, n, th):
            for b in range(B):
                a.wait_ge(ln_t, B * n + b + 1)
                nc.scalar.activation(th[:, :, b * P:(b + 1) * P], by_tile(bank[6 + b % 2][:]),
                                     ACT.Copy).then_inc(ln_hi, 1)

        su_hot = sem("su_hot")
        su_rope = sem("su_rope")
        su_rc = sem("su_rc")
        su_w0 = sem("su_w0")
        su_ba = sem("su_ba")
        su_bias = sem("su_bias")
        su_wr = sem("su_wr")
        su_one = sem("su_one")
        su_mh = sem("su_mh")
        a0_x = sem("a0_x")
        a0_in = sem("a0_in")
        a0_c = sem("a0_c")
        a0_pj = sem("a0_pj")
        a0_A = sem("a0_A")
        a0_kk = sem("a0_kk")
        a0_pf = sem("a0_pf")
        a0_vc = sem("a0_vc")
        a0_neg = sem("a0_neg")
        a0_m0 = sem("a0_m0")
        a0_s = sem("a0_s")
        a0_mx = sem("a0_mx")
        a0_e = sem("a0_e")
        a0_t = sem("a0_t")
        a0_pt = sem("a0_pt")
        a0_pv = sem("a0_pv")
        a0_rc = sem("a0_rc")
        a0_pn = sem("a0_pn")
        a0_ot = sem("a0_ot")
        a0_one = sem("a0_one")
        o0_gh = sem("o0_gh")
        o0_gl = sem("o0_gl")
        o0_y = sem("o0_y")

        def pj0(b, p):
            return 5 * b + p

        def bank0(b, p):
            return bank[6 + pj0(b, p) % 2]

        def used0(t, i):
            b, p = i // 5, i % 5
            if p < 2:
                t.wait_ge(a0_pf, 4 * b + p + 1)
            elif p < 4:
                t.wait_ge(a0_kk, 2 * b + p - 1)
            else:
                t.wait_ge(a0_vc, b + 1)

        def free0(sp_like, b):
            if b >= 2:
                sp_like.wait_ge(a0_pj, pj0(b - 2, 4) + 1)

        f_low = sem("f_low")
        f_lowc = sem("f_lowc")
        f_mx = sem("f_mx")
        f_e = sem("f_e")
        f_ls = sem("f_ls")
        f_t = sem("f_t")
        f_th = sem("f_th")
        f_tl = sem("f_tl")
        f_y = sem("f_y")

        def router_act(a, i):
            a.wait_ge(f_mx, i + 1)
            nc.scalar.activation(sc[:, 0, :, :], lg[:, :, 0:8], ACT.Exp).then_inc(f_e, 1)
            for j in range(2):
                a.wait_ge(f_t, 2 * i + j + 1)
                nc.scalar.activation(lowT_h[:, j * 512:(j + 1) * 512], bank[4 + j][:], ACT.Copy).then_inc(f_th, 1)

        def router_dve(v, i, x_before):
            for b in range(B):
                v.wait_ge(f_low, B * i + b + 1)
                nc.vector.tensor_copy(low[:, b, :], bank[b % 2][:, 0:P])
                if i == 0:
                    nc.vector.tensor_tensor(lg[:, b, 0:8], bank[b % 2][:, P:P + 8], br[:, :], ALU.add).then_inc(f_lowc, 1)
                else:
                    nc.vector.tensor_copy(lg[:, b, 0:8], bank[b % 2][:, P:P + 8]).then_inc(f_lowc, 1)
            v.wait_ge(f_lowc, B * i + B)
            link(v, v_chain, nc.vector.tensor_reduce(rt[:, 0, :], lg[:, :, 0:8], AX.X, ALU.max))
            nc.vector.tensor_tensor(lg[:, :, 0:8], lg[:, :, 0:8], rt[:, 0, :].unsqueeze(2).to_broadcast((P, B, 8)),
                                    ALU.subtract).then_inc(f_mx, 1)
            if i == 1:
                link(v, v_chain, nc.vector.memset(lg[:, :, 8:14], DUMMY))
                v.wait_ge(f_mx, i + 1)
                for b in range(B):
                    ins = nc.vector.max(t8[:, b, :], lg[:, b, :])
                link(v, v_chain, ins)
            v.wait_ge(f_e, i + 1)
            if i == 1:
                for b in range(B):
                    ins = nc.vector.match_replace(lg[:, b, :], t8[:, b, :], lg[:, b, :], TAKEN)
                link(v, v_chain, ins)
                link(v, v_chain, nc.vector.scalar_tensor_tensor(sc[:, 0, :, :], lg[:, :, 0:8], TAKEN, sc[:, 0, :, :],
                                                                ALU.is_equal, ALU.mult))
            link(v, v_chain, nc.vector.tensor_reduce(rt[:, 1, :], sc[:, 0, :, :], AX.X, ALU.add))
            link(v, v_chain, nc.vector.reciprocal(rt[:, 2, :], rt[:, 1, :]))
            link(v, v_chain, nc.vector.tensor_scalar(rt[:, 3, :], rt[:, 2, :], (16.0, 2.0)[i], None, ALU.mult))
            link(v, v_chain, nc.vector.tensor_tensor(sc[:, 1, :, :], sc[:, 0, :, :],
                                                     rt[:, 3, :].unsqueeze(2).to_broadcast((P, B, 8)), ALU.mult))
            for j in range(2):
                rows4 = low[:, 4 * j:4 * j + 4, :].rearrange("p b (h r) -> p (b h) r", r=16)
                by = sc[:, 1, 4 * j:4 * j + 4, :].rearrange("p b h -> p (b h)").unsqueeze(2).to_broadcast((P, 32, 16))
                nc.vector.tensor_tensor(rows4, rows4, by, ALU.mult).then_inc(f_ls, 1)
            for j in range(2):
                v.wait_ge(f_th, 2 * i + j + 1)
                cut = slice(j * 512, (j + 1) * 512)
                nc.vector.tensor_tensor(lowT_l[:, cut], bank[4 + j][:], f32(lowT_h[:, cut]), ALU.subtract).then_inc(f_tl, 1)
            for b in range(B):
                v.wait_ge(f_y, B * i + b + 1)
                nc.vector.tensor_tensor(X[:, b, :], X[:, b, :], bank[b % 4][:], ALU.add).then_inc(x_done, 1)

        def router_low_pe(t, i, u, th, tl):
            t.wait_ge(su_wr, 2)
            t.wait_ge(w_lo, u + 1)
            ah, al = slot(u)
            for b in range(B):
                if b >= 2:
                    t.wait_ge(f_lowc, B * i + b - 1)
                t.wait_ge(ln_lo, B * LN_L0F[1] + B * i + b + 1)
                c = slice(b * P, (b + 1) * P)
                for k in range(KT):
                    kc = slice(k * P, (k + 1) * P)
                    mm3(bank[b % 2][:, 0:P], th[:, k, c], tl[:, k, c], ah[:, kc], al[:, kc], k == 0, k == KT - 1)
                for k in range(KT):
                    kc = slice(8 * k, 8 * k + 8)
                    ins = mm3(bank[b % 2][:, P:P + 8], th[:, k, c], tl[:, k, c], wrh[:, i, kc], wrl[:, i, kc],
                              k == 0, k == KT - 1)
                ins.then_inc(f_low, 1)
            owed[0] += 1

        def router_turn_pe(t, i):
            for j in range(2):
                t.wait_ge(f_ls, 2 * i + j + 1)
                for q in range(4):
                    ins = nc.tensor.transpose(bank[4 + j][:, q * P:(q + 1) * P], low[:, 4 * j + q, :], ident[:, :])
                ins.then_inc(f_t, 1)

        x_x = sem("x_x")
        x_t = sem("x_t")
        x_cf = sem("x_cf")
        x_mx = sem("x_mx")
        x_sum = sem("x_sum")
        x_rows = sem("x_rows")
        x_z = sem("x_z")
        x_zs = sem("x_zs")
        x_tot = sem("x_tot")
        x_var = sem("x_var")
        x_rs = sem("x_rs")
        x_arg = sem("x_arg")
        x_e = sem("x_e")
        x_gt = sem("x_gt")
        x_gp = sem("x_gp")
        c_hi = sem("c_hi")
        c_lo = sem("c_lo")

        def chunk(k):
            return xn[:, 2 * (k % 2):2 * (k % 2) + 2, :].rearrange("p a f -> p (a f)")

        a2_pj = sem("a2_pj")
        a2_pf = sem("a2_pf")
        a2_one = sem("a2_one")
        a2_s = sem("a2_s")
        a2_mx = sem("a2_mx")
        a2_e = sem("a2_e")
        a2_t = sem("a2_t")
        a2_pt = sem("a2_pt")
        a2_pv = sem("a2_pv")
        a2_on = sem("a2_on")
        a2_ot = sem("a2_ot")
        a2_oh = sem("a2_oh")
        a2_ol = sem("a2_ol")
        a2_y = sem("a2_y")

        def pj2(s, j):
            return 12 * s + j if j < 2 or s else 2 + j

        g_p = sem("g_p")
        g_s = sem("g_s")
        g_h = sem("g_h")
        g_hh = sem("g_hh")
        g_hl = sem("g_hl")
        g_y = sem("g_y")
        a3_pj = sem("a3_pj")
        a3_rp = sem("a3_rp")
        a3_qk = sem("a3_qk")
        a3_vc = sem("a3_vc")
        a3_vt = sem("a3_vt")
        a3_v = sem("a3_v")
        a3_m = sem("a3_m")
        a3_s = sem("a3_s")
        a3_mx = sem("a3_mx")
        a3_e = sem("a3_e")
        a3_rc = sem("a3_rc")
        a3_pn = sem("a3_pn")
        a3_t = sem("a3_t")
        a3_pt = sem("a3_pt")
        a3_pv = sem("a3_pv")
        a3_oh = sem("a3_oh")
        a3_ol = sem("a3_ol")
        a3_y = sem("a3_y")
        z_pf = sem("z_pf")
        z_pick = sem("z_pick")
        z_t = sem("z_t")
        z_th = sem("z_th")
        z_tl = sem("z_tl")
        z_dz = sem("z_dz")
        z_dn = sem("z_dn")
        z_up = sem("z_up")
        z_g = sem("z_g")
        z_gh = sem("z_gh")
        z_gl = sem("z_gl")
        z_dp = sem("z_dp")
        z_oh = sem("z_oh")
        z_ol = sem("z_ol")
        z_y = sem("z_y")
        block = ctx.enter_context(nc.Block())

        @block.sync
        def _(sp):
            nc.sync.dma_start(con[:, :], d["con"]).then_inc(s_con, 16)
            nc.sync.dma_start(X[:, 0:4, :], d["x"][0:4].rearrange("b p s -> p b s")).then_inc(s_x, 16)
            nc.sync.dma_start(ident[:, :], d["ident"]).then_inc(s_con, 16)
            nc.sync.dma_start(w0[:, :], d["w0"]).then_inc(s_w0, 16)
            nc.sync.dma_start(bias_f[:, :], d["b0"]).then_inc(s_w0, 16)
            nc.sync.dma_start(bo[:, :], d["bo"]).then_inc(s_w0, 16)
            nc.sync.dma_start(w0v[:, :], d["w0"][:, W0V:W0O]).then_inc(s_w0, 16)
            nc.sync.dma_start(pos_i[:, :], d["pos"][0].partition_broadcast(P)).then_inc(s_tab, 16)
            nc.sync.dma_start(tabs[:, :, :, :], d["tabs"].rearrange("a k p j -> p a k j")).then_inc(s_tab, 16)
            nc.sync.dma_start(iota[:, :], d["iota"]).then_inc(s_con, 16)
            nc.sync.dma_start(conv[:, :], d["conv"][0].partition_broadcast(P)).then_inc(s_rest, 16)
            nc.sync.dma_start(br[:, :], d["br"][0].partition_broadcast(P)).then_inc(s_rest, 16)
            nc.sync.dma_start(wr[:, :, :], d["wr"].rearrange("a p j -> p a j")).then_inc(s_rest, 16)
            nc.sync.dma_start(topv[:, :, 0:P], d["context_lc"].rearrange("n p c -> p n c")).then_inc(s_topv, 16)

            def unit_step(u):
                if u >= STAGE:
                    sp.wait_ge(w_lo, u - STAGE + 1)
                nc.sync.dma_start(stage[:, u % STAGE, :], d["units"][u]).then_inc(s_unit[u % STAGE], 16)

            load = Stream(unit_step)
            sp.wait_ge(su_w0, 2)
            sp.wait_ge(su_rope, 4)
            sp.wait_ge(su_bias, 1)
            for b in range(B):
                if b >= 2:
                    sp.wait_ge(a0_pj, pj0(b - 2, 4) + 1)
                    sp.wait_ge(a0_m0, b - 1)
                nc.sync.dma_start(ctx_n[:, b % 2, :], d["context"][b]).then_inc(s_ctx[b % 2], 16)
                nc.sync.dma_start(mask0[:, b % 2, :], d["mask_row"][b].partition_broadcast(P)).then_inc(s_m0[b % 2], 16)
                if b == 1:
                    load.upto(2)
            for b in range(B):
                if b < 2:
                    sp.wait_ge(a0_m0, B + b - 1)
                else:
                    sp.wait_ge(x_done, XD_L0A + b - 1)
                nc.sync.dma_start(mask0[:, b % 2, :], d["mask_row"][b].partition_broadcast(P)).then_inc(s_m0[b % 2], 16)
            load.upto(U_L1F + 6)
            load.upto(U_L2X + 2)
            if XD_CX:
                sp.wait_ge(x_done, XD_CX)
            for k in range(KT):
                if k >= 2:
                    sp.wait_ge(c_lo, k - 1)
                nc.sync.dma_start(chunk(k), d["contextT"][k]).then_inc(s_ctxT[k % 2], 16)
            load.upto(U_L3X)
            if XD_L3X:
                sp.wait_ge(x_done, XD_L3X)
            nc.sync.dma_start(mask3[:, :, :], d["mask3"].rearrange("b i j -> i b j")).then_inc(s_m3, 16)
            load.upto(N_UNITS)
            if XD_L3F:
                sp.wait_ge(x_done, XD_L3F)
            nc.sync.dma_start(perm_i[:, 0:512], d["perm_row"][0].partition_broadcast(P)).then_inc(s_perm, 16)
            nc.sync.dma_start(perm_i[:, 512:516], d["perm_col"]).then_inc(s_perm, 16)
            load.upto(N_UNITS)
            for b in range(B):
                sp.wait_ge(x_done, XD_END - B + b + 1)
                nc.sync.dma_start(out[b], X[:, b, :]).then_inc(s_out, 16)
            sp.wait_ge(s_out, 16 * B)


        @block.gpsimd
        def _(g):
            def lo_step(u):
                g.wait_ge(w_hi, u + 1)
                nc.gpsimd.tensor_tensor(ring_l[:, u % RING, :], stage[:, u % STAGE, :], f32(ring_h[:, u % RING, :]),
                                        ALU.subtract).then_inc(w_lo, 1)

            lo = Stream(lo_step)
            link(g, p_chain, nc.gpsimd.memset(mhalf[:, :], -0.5))
            g.wait_ge(su_w0, 1)
            nc.gpsimd.tensor_tensor(w0l[:, :], w0[:, :], f32(w0h[:, :]), ALU.subtract).then_inc(su_w0, 1)
            g.wait_ge(su_wr, 1)
            nc.gpsimd.tensor_tensor(wrl[:, :, :], wr[:, :, :], f32(wrh[:, :, :]), ALU.subtract).then_inc(su_wr, 1)
            ln_pool(g, LN_L0A[0])
            g.wait_ge(s_topv, 16)
            nc.gpsimd.tensor_scalar(topv[:, :, 0:P], topv[:, :, 0:P], -1.0, 0.0, ALU.mult, ALU.add).then_inc(a0_neg, 1)
            g.wait_ge(su_rope, 4)
            g.wait_ge(su_bias, 1)
            nc.gpsimd.memset(v0[:, :, :, :], 0.0)
            nc.gpsimd.memset(zeros_r[:, :].bitcast(F32), 0.0).then_inc(a0_one, 1)

            def low0(b):
                g.wait_ge(a0_in, b + 1)
                g.wait_ge(a0_x, b + 1)
                free0(g, b)
                nc.gpsimd.tensor_tensor(xnl[:, b % 2, :], xn[:, b % 4, :], f32(xnh[:, b % 2, :]), ALU.subtract).then_inc(a0_c, 1)

            low0(0)
            low0(1)
            for n in range(64):
                b, u = n // 8, n % 8
                if u == 6 and b + 2 < B:
                    low0(b + 2)
                g.wait_ge(a0_rc, n + 1)
                pb = by_tile(probs[:, n % 3, :])
                nc.gpsimd.tensor_tensor(pb, pb, rsums[:, n % 4, :].unsqueeze(2).to_broadcast((P, 4, P)), ALU.mult).then_inc(a0_pn, 1)
                if u == 0:
                    lo.upto(min(b, 2))
            for b in range(B):
                g.wait_ge(o0_gh, b + 1)
                if b >= 2:
                    g.wait_ge(o0_y, b - 1)
                nc.gpsimd.tensor_tensor(g0l[:, b % 2, :], g0[:, b % 2, :], f32(g0h[:, b % 2, :]),
                                        ALU.subtract).then_inc(o0_gl, 1)
            ln_pool(g, LN_L0F[0])
            lo.upto(U_L0F + RING)
            ln_pool(g, LN_L1X[0])
            g.wait_ge(x_var, 1)
            link(g, p_chain, nc.gpsimd.tensor_scalar(zs[:, 4, :], zs[:, 3, :], EPS, 1.0, ALU.add, ALU.mult))
            nc.gpsimd.tensor_tensor(zs[:, 5, :], zs[:, 4, :], mhalf[:, 0:2], ALU.pow).then_inc(x_rs, 1)
            ln_pool(g, LN_L1F[0])
            lo.upto(U_L2X + 2)
            for k in range(KT):
                g.wait_ge(c_hi, k + 1)
                g.wait_ge(s_ctxT[k % 2], 16 * (k // 2 + 1))
                nc.gpsimd.tensor_tensor(cTl[:, k, :], chunk(k), f32(cTh[:, k, :]), ALU.subtract).then_inc(c_lo, 1)
            lo.upto(U_L2X + 2)
            ln_pool(g, LN_L2X[0])
            lo.upto(U_L2X + 23)
            ln_pool(g, LN_L2F[0])
            lo.upto(U_L3X)
            lo.upto(U_L3X + 6)
            ln_pool(g, LN_L3X[0])
            for h in range(8):
                for j in range(10):
                    i = 10 * h + j
                    g.wait_ge(a3_rp, i + 1)
                    half = (j - 2) // 4
                    dst = k3[:, j * HALF:(j + 1) * HALF] if j < 2 else q3[:, (j - 2) % 4, half * HALF:(half + 1) * HALF]
                    nc.gpsimd.tensor_tensor(dst, xn[:, j % 2, :], xn[:, 2 + j % 2, :], ALU.add).then_inc(a3_qk, 1)
                    if j == 5:
                        lo.upto(U_L3X + 10 * h + 10)
                for b in range(B):
                    n = B * h + b
                    g.wait_ge(a3_rc, n + 1)
                    pb = probs[:, n % 3, :].rearrange("p (r j) -> p r j", r=4)
                    nc.gpsimd.tensor_tensor(pb, pb, rsums[:, n % 4, :].unsqueeze(2).to_broadcast((P, 4, P)),
                                            ALU.mult).then_inc(a3_pn, 1)
                    if b >= 3:
                        lo.upto(U_L3X + 10 * h + 9 + b)
            lo.upto(N_UNITS)
            ln_pool(g, LN_L3F[0])
            for n in range(32):
                g.wait_ge(z_gh, n + 1)
                if n >= 2:
                    g.wait_ge(z_dp, n - 1)
                nc.gpsimd.tensor_tensor(gel_l[:, n % 2, :], gel[:, n % 2, :], f32(gel_h[:, n % 2, :]), ALU.subtract).then_inc(z_gl, 1)


        @block.scalar
        def _(a):
            def hi_step(u):
                a.wait_ge(s_unit[u % STAGE], 16 * (u // STAGE + 1))
                if u >= RING:
                    a.wait_ge(w_used, u - RING + 1)
                nc.scalar.activation(ring_h[:, u % RING, :], stage[:, u % STAGE, :], ACT.Copy).then_inc(w_hi, 1)

            hi = Stream(hi_step)
            nc.scalar.dma_start(X[:, 4:8, :], d["x"][4:8].rearrange("b p s -> p b s")).then_inc(s_x, 16)
            a.wait_ge(s_w0, 64)
            a.wait_ge(s_con, 48)
            nc.scalar.activation(w0h[:, :], w0[:, :], ACT.Copy).then_inc(su_w0, 1)
            nc.scalar.activation(bias_a[:, :].bitcast(F32R), bias_f[:, :], ACT.Identity,
                                 scale=con[0:2, C_RA:C_RA + 1]).then_inc(su_ba, 1)
            a.wait_ge(s_rest, 48)
            nc.scalar.activation(wrh[:, :, :], wr[:, :, :], ACT.Copy).then_inc(su_wr, 1)
            def inputs0(b):
                a.wait_ge(a0_x, b + 1)
                free0(a, b)
                nc.scalar.activation(xnh[:, b % 2, :], xn[:, b % 4, :], ACT.Copy).then_inc(a0_in, 1)

            def first_half(b, p):
                if p or b:
                    a.wait_ge(a0_pf, 4 * b + p)
                if p < 2:
                    a.wait_ge(a0_pj, pj0(b, p) + 1)
                    src, scale = bank0(b, p)[:], col(C_QA)
                else:
                    a.wait_ge(a0_kk, 2 * b + p - 1)
                    src, scale = kkeep, col(C_KA)
                nc.scalar.activation(halfA[:, :].bitcast(F32R), src, ACT.Identity, scale=scale).then_inc(a0_A, 1)

            def values0(b):
                a.wait_ge(a0_pj, pj0(b, 4) + 1)
                if b >= 2:
                    a.wait_ge(a0_pv, 8 * (b - 1))
                else:
                    a.wait_ge(a0_one, 1)
                nc.scalar.activation(v0[:, b % 2, :, :].rearrange("j p (h c) -> j p h c", c=72)[:, :, :, 0:8],
                                     bank0(b, 4)[:, 0:256].rearrange("j (p h e) -> j p h e", p=4, h=8), ACT.Copy).then_inc(a0_vc, 1)

            a.wait_ge(su_w0, 2)
            a.wait_ge(su_rope, 4)
            a.wait_ge(su_bias, 1)
            inputs0(0)
            for p in range(4):
                first_half(0, p)
            values0(0)
            inputs0(1)
            for n in range(66):
                b, u = n // 8, n % 8
                if n >= 2:
                    a.wait_ge(a0_t, n - 1)
                    if n >= 5:
                        a.wait_ge(a0_pv, n - 4)
                    nc.scalar.activation(probsT[:, (n - 2) % 3, :], bank[3 + n % 2][:], ACT.Copy).then_inc(a0_pt, 1)
                if n < 64:
                    a.wait_ge(a0_mx, n + 1)
                    if n >= 3:
                        a.wait_ge(a0_t, n - 2)
                    for p in range(4):
                        ins = nc.scalar.activation(probs[:, n % 3, p * P:(p + 1) * P], bank[n % 3][:, p * P:(p + 1) * P],
                                                   ACT.Exp, bias=nbias[:, n % 4, p:p + 1], scale=-1.0,
                                                   accum_out=psums[:, n % 4, p:p + 1])
                    ins.then_inc(a0_e, 1)
                if b < B - 1 and u < 4:
                    first_half(b + 1, u)
                if b < B - 1 and u == 4:
                    values0(b + 1)
                if u == 5 and b + 2 < B:
                    inputs0(b + 2)
                if u == 7:
                    hi.upto(min(b + 1, 2))
            a.wait_ge(a0_pv, 64)
            a.wait_ge(a0_ot, B)
            for b in range(B):
                a.wait_ge(a0_ot, b + 1)
                if b >= 2:
                    a.wait_ge(o0_y, b - 1)
                    a.wait_ge(o0_gl, b - 1)
                link(a, a_chain, nc.scalar.activation(g0[:, b % 2, :], o0T[:, b, :], ACT.Gelu))
                nc.scalar.activation(g0h[:, b % 2, :], g0[:, b % 2, :], ACT.Copy).then_inc(o0_gh, 1)
            ln_act(a, LN_L0F[1], xTh_a)
            hi.upto(U_L0F + RING)
            router_act(a, 0)
            for b in range(B):
                a.wait_ge(x_cf, b + 1)
                if b >= 1:
                    a.wait_ge(x_sum, b)
                for i in range(2):
                    for q in range(4):
                        ins = nc.scalar.activation(junk[:, i, q, :], cf[:, b % 2, i, q * P:(q + 1) * P], ACT.Copy,
                                                   accum_out=rows[:, 1, i, b, q + 1:q + 2])
                ins.then_inc(x_sum, 1)
            a.wait_ge(x_arg, 1)
            nc.scalar.activation(zz[:, :, :], z[:, :, :], ACT.Exp, scale=-1.0).then_inc(x_e, 1)
            hi.upto(U_L1F + 6)
            ln_act(a, LN_L1F[1], xTh_a)
            router_act(a, 1)
            hi.upto(U_L2X + 2)
            for k in range(KT):
                a.wait_ge(s_ctxT[k % 2], 16 * (k // 2 + 1))
                nc.scalar.activation(cTh[:, k, :], chunk(k), ACT.Copy).then_inc(c_hi, 1)
            def copied2(s, j):
                i = pj2(s, j)
                a.wait_ge(a2_pj, i + 1)
                half = j if j < 2 else (j - 2) // 4
                c = slice(half * HALF, (half + 1) * HALF)
                if j < 2:
                    nc.scalar.activation(k2[:, c], bank[6 + i % 2][:], ACT.Copy).then_inc(a2_pf, 1)
                else:
                    nc.scalar.activation(q2[:, (j - 2) % 4, c], bank[6 + i % 2][:], ACT.Copy, scale=-0.25).then_inc(a2_pf, 1)

            hi.upto(U_L2X + 2)
            for s in range(2):
                for j in range(2):
                    copied2(s, j)
                if s == 0:
                    for half in range(2):
                        a.wait_ge(a2_pj, 3 + half)
                        nc.scalar.activation(v2[:, 4 * half:4 * half + 4, :, 0:16],
                                             bank[6 + half][:].rearrange("p (b h e) -> p b h e", b=4, h=8), ACT.Copy).then_inc(a2_pf, 1)
                    ln_act(a, LN_L2X[1], xTh_b)
                    hi.upto(U_L2X + 8)
                for j in range(2, 10):
                    copied2(s, j)
                if s == 0:
                    hi.upto(U_L2X + 12)
                for l in range(36):
                    n = 32 * s + l
                    m = n - 2
                    if 2 <= l < 34:
                        a.wait_ge(a2_t, m + 1)
                        if m >= 3:
                            a.wait_ge(a2_pv, m - 2)
                        nc.scalar.activation(probsT[:, m % 3, :], bank[3 + m % 2][:], ACT.Copy).then_inc(a2_pt, 1)
                    if l < 32:
                        a.wait_ge(a2_mx, n + 1)
                        if n >= 3:
                            a.wait_ge(a2_t, n - 2)
                        for r in range(4):
                            c = slice(r * P, (r + 1) * P)
                            ins = nc.scalar.activation(probs[:, n % 3, c], bank[n % 3][:, c], ACT.Exp,
                                                       bias=nbias[:, n % 4, r:r + 1], scale=-1.0)
                        ins.then_inc(a2_e, 1)
                    if l >= 7 and l % 4 == 3:
                        m = 8 * s + (l - 7) // 4
                        a.wait_ge(a2_ot, m + 1)
                        if m >= 2:
                            a.wait_ge(a2_y, m - 1)
                        nc.scalar.activation(onT_h[:, m % 2, :], bank[6][:, 0:256], ACT.Copy).then_inc(a2_oh, 1)
                    if l >= 12 and l % 4 == 0 and l < 32:
                        hi.upto(U_L2X + (min(12 + (l - 8) // 4, 16) if s == 0 else min(16 + (l - 8) // 4 * 2, 23)))
                hi.upto(U_L2X + (16 if s == 0 else 23))
            def high2(n, group, i):
                a.wait_ge(g_h, n + 1)
                if i:
                    a.wait_ge(g_y, B * i)
                f, half = n // 2 - group[0], n % 2
                nc.scalar.activation(hid_h[:, f, half * HALF:(half + 1) * HALF], hid[:, n % 2, :], ACT.Copy).then_inc(g_hh, 1)

            ln_act(a, LN_L2F[1], xTh_b)
            u = U_L2F
            hi.upto(u + RING)
            for i, group in enumerate(FGROUPS):
                for f in group:
                    for half in range(2):
                        n = 2 * f + half
                        a.wait_ge(g_p, 2 * n + 1)
                        if n >= 2:
                            a.wait_ge(g_h, n - 1)
                        nc.scalar.activation(silu[:, n % 2, :], bank[n % 2][:], ACT.Silu).then_inc(g_s, 1)
                        if n > 2 * group[0]:
                            high2(n - 1, group, i)
                        if half == 0:
                            hi.upto(min(u + RING, U_L3X))
                    u += 2
                high2(2 * group[-1] + 1, group, i)
                hi.upto(min(u + RING, U_L3X))
                u += len(group)
            hi.upto(U_L3X + 6)
            ln_act(a, LN_L3X[1], xTh_b)
            for h in range(8):
                hi.upto(U_L3X + 10 * h + 10)
                for half in range(2):
                    a.wait_ge(a3_pj, 12 * h + 11 + half)
                    nc.scalar.activation(vT[:, half, :], bank[6 + half][:], ACT.Copy).then_inc(a3_vc, 1)
                for l in range(10):
                    n = B * h + l
                    m = n - 2
                    if l >= 2:
                        a.wait_ge(a3_t, m + 1)
                        if m >= 3:
                            a.wait_ge(a3_pv, m - 2)
                        nc.scalar.activation(probsT[:, m % 3, :], bank[2 + m % 2][:], ACT.Copy).then_inc(a3_pt, 1)
                    if l < B:
                        a.wait_ge(a3_mx, n + 1)
                        if n >= 3:
                            a.wait_ge(a3_t, n - 2)
                        for r in range(4):
                            c = slice(r * P, (r + 1) * P)
                            ins = nc.scalar.activation(probs[:, n % 3, c], bank[n % 2][:, c], ACT.Exp,
                                                       bias=nbias[:, n % 4, r:r + 1], scale=-1.0,
                                                       accum_out=psums[:, n % 4, r:r + 1])
                        ins.then_inc(a3_e, 1)
                    if l < 2:
                        a.wait_ge(a3_vt, 2 * h + l + 1)
                        nc.scalar.activation(v3[:, 4 * l:4 * l + 4, :], bank[6 + l][:].rearrange("p (b e) -> p b e", b=4),
                                             ACT.Copy).then_inc(a3_v, 1)
                    if l >= 2:
                        a.wait_ge(a3_pv, m + 1)
                        if m >= 2:
                            a.wait_ge(a3_y, m - 1)
                        nc.scalar.activation(o3h[:, m % 2, :], bank[4][:], ACT.Copy).then_inc(a3_oh, 1)
                    if 2 <= l <= 6:
                        hi.upto(U_L3X + 10 * h + 10 + l)
            hi.upto(N_UNITS)
            ln_act(a, LN_L3F[1], xTh_b)
            for n in range(8):
                a.wait_ge(z_t, n + 1)
                c = slice(n % 2 * HALF, (n % 2 + 1) * HALF)
                nc.scalar.activation(tTh[:, n // 2, c], bank[n % 4][:], ACT.Copy).then_inc(z_th, 1)

            def last_hi(o):
                a.wait_ge(z_dp, 4 * o + 4)
                c = slice(o % 2 * HALF, (o % 2 + 1) * HALF)
                nc.scalar.activation(t2h[:, o // 2, c], bank[6 + o % 2][:], ACT.Copy).then_inc(z_oh, 1)

            for n in range(32):
                a.wait_ge(z_up, n + 1)
                if n >= 2:
                    a.wait_ge(z_gl, n - 1)
                nc.scalar.activation(gel[:, n % 2, :], bank[4 + n % 2][:], ACT.Gelu).then_inc(z_g, 1)
                if n % 4 == 2 and n > 4:
                    last_hi(n // 4 - 1)
            last_hi(7)


        @block.vector
        def _(v):
            nc.vector.memset(ones_r[:, :].bitcast(F32), 1.0).then_inc(su_one, 1)
            v.wait_ge(s_con, 48)
            v.wait_ge(s_tab, 32)
            for k in range(KT):
                ins = nc.vector.tensor_scalar(hot[:, k, :], pos_i[:, :], col(C_IOTA + k), None, ALU.is_equal)
            ins.then_inc(su_hot, 1)
            v.wait_ge(su_ba, 1)
            nc.vector.scalar_tensor_tensor(biasr[:, :], bias_f[:, :], con[0:2, C_RM:C_RM + 1], bias_a[:, :],
                                           ALU.mult, ALU.add).then_inc(su_bias, 1)
            for i in range(4):
                v.wait_ge(su_rope, i + 1)
                nc.vector.tensor_copy((cosT, sinT)[i // 2][:, i % 2 * HALF:(i % 2 + 1) * HALF], bank[i][:]).then_inc(su_rc, 1)
            v.wait_ge(s_x, 32)
            ln_stats(v, LN_L0A[0])
            for b in range(4):
                ln_norm(b, xn[:, b, :]).then_inc(a0_x, 1)

            v.wait_ge(a0_neg, 1)
            link(v, v_chain, nc.vector.memset(topv[:, :, P:P + 4], DUMMY))

            def choose(k):
                tiles = range(k // ROUNDS * 4, k // ROUNDS * 4 + 4)
                for i in tiles:
                    ins = nc.vector.max(top8[:, i % 4, :], topv[:, i, :])
                link(v, v_chain, ins)
                for i in tiles:
                    ins = nc.vector.match_replace(topv[:, i, :], top8[:, i % 4, :], topv[:, i, :], TAKEN)
                link(v, v_chain, ins)

            v.wait_ge(su_w0, 2)

            def mask_rows(b):
                v.wait_ge(s_m0[b % 2], 16 * (b // 2 + 1))
                if b >= 1:
                    v.wait_ge(a0_kk, 2 * b)
                nc.vector.tensor_scalar(keep[:, :], mask0[:, b % 2, :], 0.0, None, ALU.is_gt)
                if b >= 2:
                    v.wait_ge(a0_s, 8 * (b - 1))
                nc.vector.tensor_scalar(mrow[:, b % 2, :], mask0[:, b % 2, :], 0.0, col(C_BIG), ALU.is_le,
                                        ALU.mult).then_inc(a0_m0, 1)

            def masked_keys(b, p):
                v.wait_ge(a0_pj, pj0(b, p) + 1)
                v.wait_ge(a0_m0, b + 1)
                v.wait_ge(a0_pf, 4 * b + p)
                nc.vector.tensor_tensor(kkeep, bank0(b, p)[:], keep[:, :], ALU.mult).then_inc(a0_kk, 1)

            def second_half(b, p):
                if b >= 2:
                    v.wait_ge(a0_s, 8 * (b - 1))
                v.wait_ge(a0_A, 4 * b + p + 1)
                src, dst, scale = (bank0(b, p)[:], q0[:, b % 2, p, :], C_QM) if p < 2 else (kkeep, k0[:, b % 2, p - 2, :], C_KM)
                nc.vector.scalar_tensor_tensor(dst, src, col(scale), halfA[:, :], ALU.mult, ALU.add).then_inc(a0_pf, 1)

            def output0(b):
                v.wait_ge(a0_pv, 8 * b + 8)
                nc.vector.tensor_copy(o0T[:, b, :], bank[5][0:64, :]).then_inc(a0_ot, 1)

            mask_rows(0)
            for p in range(4):
                if p >= 2:
                    masked_keys(0, p)
                second_half(0, p)
            for n in range(64):
                b, u = n // 8, n % 8
                if b >= 1 and u == 3:
                    output0(b - 1)
                v.wait_ge(a0_s, n + 1)
                if n >= 4:
                    v.wait_ge(a0_e, n - 3)
                nc.vector.tensor_reduce(nbias[:, n % 4, :], by_tile(bank[n % 3][:]), AX.X, ALU.min).then_inc(a0_mx, 1)
                if b < B - 1 and 1 <= u <= 4:
                    second_half(b + 1, u - 1)
                if b < B - 1 and u in (2, 3):
                    masked_keys(b + 1, u)
                if b < B - 1 and u == 0:
                    mask_rows(b + 1)
                if n < 56:
                    choose(n)
                v.wait_ge(a0_e, n + 1)
                if n >= 4:
                    v.wait_ge(a0_pn, n - 3)
                nc.vector.reciprocal(rsums[:, n % 4, :], psums[:, n % 4, :]).then_inc(a0_rc, 1)
                if u == 7 and b + 4 < B:
                    v.wait_ge(a0_c, b + 1)
                    ln_norm(b + 4, xn[:, b % 4, :]).then_inc(a0_x, 1)
            nc.vector.tensor_scalar(crucial[:, :, ::-1], topv[:, :, 0:P], TAKEN, None, ALU.not_equal)
            output0(B - 1)
            for b in range(B):
                v.wait_ge(o0_y, b + 1)
                v.wait_ge(s_m0[b % 2], 16 * (B // 2 + b // 2 + 1))
                link(v, v_chain, nc.vector.scalar_tensor_tensor(upd[:, b % 2, :], bank[b % 2][:], bo[:, 0:1],
                                                                mask0[:, b % 2, :], ALU.add, ALU.mult))
                nc.vector.tensor_tensor(X[:, b, :], X[:, b, :], upd[:, b % 2, :], ALU.add).then_inc(x_done, 1)
            ln_dve(v, *LN_L0F, xTh_a, xTl_a)
            router_dve(v, 0, XD_L0F)
            link(v, v_chain, nc.vector.tensor_scalar(shift[:, :], iota[:, :], col(C_EXT), None, ALU.is_equal))
            for ch in range(2):
                for dt in (-1, 0, 1):
                    band = bands[:, ch * 3 + dt + 1, :]
                    taps = {0: range(7), 1: range(4, 7), -1: range(0, 3)}[dt]
                    for k in taps:
                        at = 189 + k - P * dt
                        w = conv[:, ch * 7 + k:ch * 7 + k + 1]
                        if k == taps[0]:
                            link(v, v_chain, nc.vector.tensor_scalar(band, shift[:, at:at + P], w, None, ALU.mult))
                        else:
                            link(v, v_chain, nc.vector.scalar_tensor_tensor(band, shift[:, at:at + P], w, band, ALU.mult, ALU.add))
            nc.vector.memset(ones_f[:, :], 1.0)
            nc.vector.memset(rows[:, :, :, :, :], 0.0)
            ln_stats(v, LN_L1X[0])
            for b in range(B):
                ln_norm(b, xnf[:, b, :]).then_inc(x_x, 1)
            for b in range(B):
                v.wait_ge(x_t, b + 1)
                if b >= 2:
                    v.wait_ge(x_sum, b - 1)
                    v.wait_ge(x_mx, b - 1)
                keep01 = crucial[:, 4 * b:4 * b + 4, :].rearrange("p k t -> p (k t)")
                link(v, v_chain, nc.vector.tensor_tensor(cf[:, b % 2, 0, :], bank[b % 2][:], keep01, ALU.mult))
                nc.vector.tensor_tensor(cf[:, b % 2, 1, :], bank[b % 2][:], cf[:, b % 2, 0, :], ALU.subtract).then_inc(x_cf, 1)
                v.wait_ge(x_cf, b + 1)
                nc.vector.tensor_reduce(rows[:, 0, 0, b, 1:5], by_tile(cf[:, b % 2, 0, :]), AX.X, ALU.max)
                nc.vector.tensor_reduce(rows[:, 0, 1, b, 1:5], by_tile(cf[:, b % 2, 1, :]), AX.X, ALU.max).then_inc(x_mx, 1)
            v.wait_ge(x_sum, B)
            for i in range(2):
                ins = nc.vector.tensor_scalar(rows[:, 1, i, :, 1:5], rows[:, 1, i, :, 1:5], 1.0 / (N_CRUCIAL, N_REST)[i], None, ALU.mult)
            ins.then_inc(x_rows, 1)
            v.wait_ge(x_z, 1)
            link(v, v_chain, nc.vector.tensor_copy(z[:, :, :], bank[2][:, 0:64].rearrange("p (i n) -> p i n", i=2)))
            link(v, v_chain, nc.vector.tensor_reduce(zs[:, 0, :], z[:, :, :], AX.X, ALU.add))
            nc.vector.tensor_scalar(zs[:, 1, :], zs[:, 0, :], 1.0 / (B * D), None, ALU.mult).then_inc(x_zs, 1)
            v.wait_ge(x_tot, 1)
            link(v, v_chain, nc.vector.tensor_copy(zs[:, 6, :], bank[3][:, 0:2]))
            for i in range(2):
                ins = nc.vector.tensor_scalar(z[:, i, :], z[:, i, :], zs[:, 6, i:i + 1], None, ALU.subtract)
            link(v, v_chain, ins)
            link(v, v_chain, nc.vector.tensor_tensor(zz[:, :, :], z[:, :, :], z[:, :, :], ALU.mult))
            link(v, v_chain, nc.vector.tensor_reduce(zs[:, 0, :], zz[:, :, :], AX.X, ALU.add))
            nc.vector.tensor_scalar(zs[:, 2, :], zs[:, 0, :], 1.0 / (B * D), None, ALU.mult).then_inc(x_zs, 1)
            v.wait_ge(x_tot, 2)
            nc.vector.tensor_copy(zs[:, 3, :], bank[4][:, 0:2]).then_inc(x_var, 1)
            v.wait_ge(x_rs, 1)
            link(v, v_chain, nc.vector.tensor_scalar(zs[:, 7, :], zs[:, 5, :], conv[:, 14:15], None, ALU.mult))
            for i in range(2):
                ins = nc.vector.tensor_scalar(z[:, i, :], z[:, i, :], zs[:, 7, i:i + 1], conv[:, 15:16], ALU.mult, ALU.add)
            link(v, v_chain, ins)
            nc.vector.tensor_scalar(z[:, :, :], z[:, :, :], 0.0, None, ALU.max).then_inc(x_arg, 1)
            v.wait_ge(x_e, 1)
            link(v, v_chain, nc.vector.tensor_scalar(zz[:, :, :], zz[:, :, :], 1.0, None, ALU.add))
            link(v, v_chain, nc.vector.reciprocal(gains[:, 0:2, :], zz[:, :, :]))
            link(v, v_chain, nc.vector.tensor_tensor(gains[:, 2, :], gains[:, 0, :], gains[:, 1, :], ALU.subtract))

            def gains_by_channel(b):
                if b >= 2:
                    v.wait_ge(x_gp, b - 1)
                for q in range(4):
                    i = 4 * b + q
                    ins = nc.vector.tensor_scalar(gT[:, b % 2, q * P:(q + 1) * P], crucial[:, i, :], gains[:, 2, i:i + 1],
                                                  gains[:, 1, i:i + 1], ALU.mult, ALU.add)
                ins.then_inc(x_gt, 1)

            gains_by_channel(0)
            for b in range(B):
                if b + 1 < B:
                    gains_by_channel(b + 1)
                v.wait_ge(x_gp, b + 1)
                link(v, v_chain, nc.vector.tensor_tensor(tmpx[:, b % 2, :], bank[b % 2][:], xnf[:, b, :], ALU.mult))
                nc.vector.tensor_tensor(X[:, b, :], X[:, b, :], tmpx[:, b % 2, :], ALU.add).then_inc(x_done, 1)
            ln_dve(v, *LN_L1F, xTh_a, xTl_a)
            router_dve(v, 1, XD_L1F)
            v.wait_ge(c_lo, KT)
            nc.vector.memset(v2[:, :, :, 16:17], 1.0).then_inc(a2_one, 1)

            ln_dve(v, *LN_L2X, xTh_b, xTl_b)
            for s in range(2):
                for l in range(39):
                    n = 32 * s + l
                    if l < 32:
                        v.wait_ge(a2_s, n + 1)
                        if n >= 4:
                            v.wait_ge(a2_e, n - 3)
                        nc.vector.tensor_reduce(nbias[:, n % 4, :], by_tile(bank[n % 3][:]), AX.X, ALU.min).then_inc(a2_mx, 1)
                    if l >= 6 and l % 4 == 2 and l < 38:
                        m = 8 * s + (l - 6) // 4
                        v.wait_ge(a2_pv, 4 * m + 4)
                        if m >= 2:
                            v.wait_ge(a2_ot, m - 1)
                        o = bank[5][:, 0:272].rearrange("p (n e) -> p n e", e=17)
                        link(v, v_chain, nc.vector.reciprocal(rec2[:, :], o[:, :, 16]))
                        nc.vector.tensor_tensor(on2[:, m % 2, :].rearrange("p (n e) -> p n e", e=16), o[:, :, 0:16],
                                                rec2[:, :].unsqueeze(2).to_broadcast((P, 16, 16)), ALU.mult).then_inc(a2_on, 1)
                    if l >= 8 and l % 4 == 0:
                        m = 8 * s + (l - 8) // 4
                        v.wait_ge(a2_oh, m + 1)
                        nc.vector.tensor_tensor(onT_l[:, m % 2, :], bank[6][:, 0:256], f32(onT_h[:, m % 2, :]),
                                                ALU.subtract).then_inc(a2_ol, 1)
                    if l >= 10 and l % 4 == 2:
                        b = (l - 10) // 4
                        v.wait_ge(a2_y, 8 * s + b + 1)
                        if s:
                            v.wait_ge(x_done, XD_L2X + B)
                        nc.vector.tensor_tensor(X[:, b, :], X[:, b, :], bank[7][:], ALU.add).then_inc(x_done, 1)
            def low2(n, group):
                v.wait_ge(g_hh, n + 1)
                f, half = n // 2 - group[0], n % 2
                c = slice(half * HALF, (half + 1) * HALF)
                nc.vector.tensor_tensor(hid_l[:, f, c], hid[:, n % 2, :], f32(hid_h[:, f, c]), ALU.subtract).then_inc(g_hl, 1)

            ln_dve(v, *LN_L2F, xTh_b, xTl_b)
            for i, group in enumerate(FGROUPS):
                for n in range(2 * group[0], 2 * group[-1] + 2):
                    v.wait_ge(g_s, n + 1)
                    v.wait_ge(g_p, 2 * n + 2)
                    if n >= 2:
                        v.wait_ge(g_hl, n - 1)
                    nc.vector.tensor_tensor(hid[:, n % 2, :], silu[:, n % 2, :], bank[2 + n % 2][:], ALU.mult).then_inc(g_h, 1)
                    if n > 2 * group[0]:
                        low2(n - 1, group)
                low2(2 * group[-1] + 1, group)
                for b in range(B):
                    v.wait_ge(g_y, B * i + b + 1)
                    if i:
                        v.wait_ge(x_done, XD_L2F + B * i)
                    nc.vector.tensor_tensor(X[:, b, :], X[:, b, :], bank[4 + b % 2][:], ALU.add).then_inc(x_done, 1)
            nc.vector.memset(big[:, :], BIG)
            v.wait_ge(s_m3, 16)
            nc.vector.tensor_scalar(mask3[:, :, :], mask3[:, :, :], 0.0, None, ALU.is_equal).then_inc(a3_m, 1)
            v.wait_ge(a3_m, 1)
            ln_dve(v, *LN_L3X, xTh_b, xTl_b)
            v.wait_ge(ln_t, B * (LN_L3X[1] + 1))
            SCALE3 = -1.0 / float(np.sqrt(np.float32(P)))
            for h in range(8):
                for j in range(10):
                    i = 10 * h + j
                    half = j if j < 2 else (j - 2) // 4
                    c = slice(half * HALF, (half + 1) * HALF)
                    v.wait_ge(a3_pj, 12 * h + j + 1)
                    if i >= 2:
                        v.wait_ge(a3_qk, i - 1)
                    src, swapped = bank[6 + j % 2], ((slice(0, 64), slice(64, P)), (slice(64, P), slice(0, 64)))
                    if j < 2:
                        nc.vector.scalar_tensor_tensor(xn[:, j % 2, :], src[:], SCALE3, cosT[:, c], ALU.mult, ALU.mult)
                        for to, fro in swapped:
                            ins = nc.vector.scalar_tensor_tensor(xn[to, 2 + j % 2, :], src[fro, :], SCALE3, sinT[to, c],
                                                                 ALU.mult, ALU.mult)
                    else:
                        nc.vector.tensor_tensor(xn[:, j % 2, :], src[:], cosT[:, c], ALU.mult)
                        for to, fro in swapped:
                            ins = nc.vector.tensor_tensor(xn[to, 2 + j % 2, :], src[fro, :], sinT[to, c], ALU.mult)
                    ins.then_inc(a3_rp, 1)
                for l in range(11):
                    n = B * h + l
                    if 1 <= l <= B:
                        m = n - 1
                        v.wait_ge(a3_e, m + 1)
                        if m >= 4:
                            v.wait_ge(a3_pn, m - 3)
                        nc.vector.reciprocal(rsums[:, m % 4, :], psums[:, m % 4, :]).then_inc(a3_rc, 1)
                    if l < B:
                        v.wait_ge(a3_s, n + 1)
                        if n >= 4:
                            v.wait_ge(a3_e, n - 3)
                        s4 = by_tile(bank[n % 2][:])
                        link(v, v_chain, nc.vector.copy_predicated(s4, mask3[:, l, :].unsqueeze(1).to_broadcast((P, 4, P)),
                                                                   big[:, :].unsqueeze(1).to_broadcast((P, 4, P))))
                        nc.vector.tensor_reduce(nbias[:, n % 4, :], s4, AX.X, ALU.min).then_inc(a3_mx, 1)
                    if 2 <= l < B + 2:
                        m = n - 2
                        v.wait_ge(a3_oh, m + 1)
                        nc.vector.tensor_tensor(o3l[:, m % 2, :], bank[4][:], f32(o3h[:, m % 2, :]), ALU.subtract).then_inc(a3_ol, 1)
                    if l >= 3:
                        m = n - 3
                        v.wait_ge(a3_y, m + 1)
                        if h:
                            v.wait_ge(x_done, XD_L3X + B * h)
                        nc.vector.tensor_tensor(X[:, l - 3, :], X[:, l - 3, :], bank[5][:], ALU.add).then_inc(x_done, 1)
            ln_dve(v, *LN_L3F, xTh_b, xTl_b)
            v.wait_ge(s_perm, 32)
            nc.vector.tensor_copy(perm_f[:, 0:516], perm_i[:, 0:516]).then_inc(z_pf, 1)
            v.wait_ge(z_pf, 1)
            for k in range(KT):
                ins = nc.vector.tensor_scalar(pick[:, k, :], perm_f[:, 0:512], col(C_IOTA + k), None, ALU.is_equal)
            ins.then_inc(z_pick, 1)
            for k in range(KT):
                ins = nc.vector.tensor_scalar(put[:, k, :], iota[:, :], perm_f[:, 512 + k:513 + k], None, ALU.is_equal)
            ins.then_inc(z_pick, 1)
            nc.vector.memset(down_h[:, :, :].bitcast(F32), 0.0)
            nc.vector.memset(down_l[:, :, :].bitcast(F32), 0.0).then_inc(z_dz, 1)
            v.wait_ge(z_dz, 1)
            v.wait_ge(w_lo, U_L3F + 2)
            for to, fro in ((down_h, slot(U_L3F + 1)[0]), (down_l, slot(U_L3F + 1)[1])):
                for gr in range(4):
                    dst = to[:, :, :].rearrange("p (t g) c -> p t g c", g=4)[:, :, gr, 32 * gr:32 * gr + 32]
                    ins = nc.vector.tensor_copy(dst, f32(fro).rearrange("p (t g c) -> p t g c", t=4, g=4)[:, :, gr, :])
            ins.then_inc(z_dn, 1)
            for n in range(8):
                v.wait_ge(z_th, n + 1)
                c = slice(n % 2 * HALF, (n % 2 + 1) * HALF)
                nc.vector.tensor_tensor(tTl[:, n // 2, c], bank[n % 4][:], f32(tTh[:, n // 2, c]), ALU.subtract).then_inc(z_tl, 1)

            def last_lo(o):
                v.wait_ge(z_oh, o + 1)
                c = slice(o % 2 * HALF, (o % 2 + 1) * HALF)
                nc.vector.tensor_tensor(t2l[:, o // 2, c], bank[6 + o % 2][:], f32(t2h[:, o // 2, c]), ALU.subtract).then_inc(z_ol, 1)

            for n in range(32):
                v.wait_ge(z_g, n + 1)
                if n >= 2:
                    v.wait_ge(z_dp, n - 1)
                nc.vector.tensor_copy(gel_h[:, n % 2, :], gel[:, n % 2, :]).then_inc(z_gh, 1)
                if n % 4 == 3 and n > 4:
                    last_lo(n // 4 - 1)
            last_lo(7)
            for b in range(B):
                v.wait_ge(z_y, b + 1)
                nc.vector.tensor_tensor(X[:, b, :], X[:, b, :], bank[b % 4][:], ALU.add).then_inc(x_done, 1)


        @block.tensor
        def _(t):
            used = [0]

            def unit(u):
                t.wait_ge(w_lo, u + 1)
                return slot(u)

            t.wait_ge(s_tab, 32)
            t.wait_ge(s_con, 48)
            t.wait_ge(su_hot, 1)
            for i in range(4):
                for k in range(KT):
                    ins = nc.tensor.matmul(bank[i][:], tabs[:, i // 2, k, :], hot[:, k, i % 2 * HALF:(i % 2 + 1) * HALF],
                                           start=k == 0, stop=k == KT - 1)
                ins.then_inc(su_rope, 1)
            def projection0(b, p):
                if pj0(b, p) >= 2:
                    used0(t, pj0(b, p) - 2)
                dst = bank0(b, p)
                if p < 4:
                    c = slice((W0Q, W0K)[p // 2] + p % 2 * P, (W0Q, W0K)[p // 2] + p % 2 * P + P)
                    mm3(dst[:], w0h[:, c], w0l[:, c], xnh[:, b % 2, :], xnl[:, b % 2, :], True, False)
                    nc.tensor.matmul(dst[:], biasr[:, c], ones_r[0:2, :], start=False, stop=True).then_inc(a0_pj, 1)
                    return
                t.wait_ge(s_ctx[b % 2], 16 * (b // 2 + 1))
                nc.tensor.matmul(dst[:, 0:256].rearrange("j (p e) -> j p e", p=4), ones_r[0:2, 0:P],
                                 biasr[:, W0V:W0V + 64].unsqueeze(1).to_broadcast((2, 4, 64)), start=True, stop=False)
                for q in range(4):
                    ins = nc.tensor.matmul(dst[:, q * 64:(q + 1) * 64], ctx_n[:, b % 2, q * P:(q + 1) * P], w0v[:, :],
                                           start=False, stop=q == 3)
                ins.then_inc(a0_pj, 1)

            t.wait_ge(su_w0, 2)
            t.wait_ge(su_bias, 1)
            t.wait_ge(su_rc, 4)
            t.wait_ge(a0_one, 1)
            t.wait_ge(a0_c, 1)
            for p in range(5):
                projection0(0, p)
            for n in range(67):
                b, u = n // 8, n % 8
                if n < 64:
                    s, gr, rows32 = u // 4, u % 4, slice(32 * (u % 4), 32 * (u % 4) + 32)
                    if u == 0:
                        t.wait_ge(a0_pf, 4 * b + 4)
                        t.wait_ge(a0_vc, b + 1)
                        t.wait_ge(a0_m0, b + 1)
                    if n >= 3:
                        t.wait_ge(a0_e, n - 2)
                    two = slice(32 * gr, 32 * gr + 2)
                    nc.tensor.matmul(bank[n % 3][:], ones_r[two, 0:P], mrow[two, b % 2, :], start=True, stop=False)
                    for p in range(4):
                        c = slice(p * P, (p + 1) * P)
                        ins = nc.tensor.matmul(bank[n % 3][:, c], q0[rows32, b % 2, s, c], k0[rows32, b % 2, s, c],
                                               start=False, stop=p == 3)
                    ins.then_inc(a0_s, 1)
                m = n - 2
                if 0 <= m < 64:
                    t.wait_ge(a0_pn, m + 1)
                    if m >= 2:
                        t.wait_ge(a0_pt, m - 1)
                    for p in range(4):
                        c = slice(p * P, (p + 1) * P)
                        ins = nc.tensor.transpose(bank[3 + m % 2][:, c], probs[:, m % 3, c], ident[:, :])
                    ins.then_inc(a0_t, 1)
                if b < B - 1 and u <= 4:
                    if u == 0:
                        t.wait_ge(a0_c, b + 2)
                    projection0(b + 1, u)
                m = n - 3
                if m >= 0:
                    t.wait_ge(a0_pt, m + 1)
                    h = m % 8
                    if h == 0:
                        if m:
                            t.wait_ge(a0_ot, m // 8)
                        nc.tensor.matmul(bank[5][0:64, :], zeros_r[:, :], ones_r[0:2, :], start=True, stop=False)
                    for p in range(4):
                        c = slice(p * P, (p + 1) * P)
                        ins = nc.tensor.matmul(bank[5][0:64, c], v0[:, m // 8 % 2, p, 64 * h:64 * h + 64], probsT[:, m % 3, c],
                                               start=False, stop=h == 7 and p == 3)
                    ins.then_inc(a0_pv, 1)
            for b in range(B):
                t.wait_ge(o0_gl, b + 1)
                if b >= 2:
                    t.wait_ge(x_done, XD_L0A + b - 1)
                mm3(bank[b % 2][:], w0h[0:64, W0O:W0O + P], w0l[0:64, W0O:W0O + P], g0h[:, b % 2, :], g0l[:, b % 2, :],
                    True, True).then_inc(o0_y, 1)
            ln_pe(t, LN_L0F[1])
            router_low_pe(t, 0, U_L0F, xTh_a, xTl_a)
            router_turn_pe(t, 0)
            bh, bl = unit(U_L0F + 1)
            for b in range(B):
                if b in (0, 4):
                    t.wait_ge(f_tl, b // 4 + 1)
                if b >= 4:
                    t.wait_ge(x_done, XD_L0F + b - 3)
                elif b < 2:
                    t.wait_ge(f_lowc, B)
                c = slice(b * P, (b + 1) * P)
                mm3(bank[b % 4][:], lowT_h[:, c], lowT_l[:, c], bh, bl, True, True).then_inc(f_y, 1)
            owed[0] += 1
            for b in range(B):
                t.wait_ge(x_x, b + 1)
                if b >= 2:
                    t.wait_ge(x_cf, b - 1)
                for k in range(KT):
                    c = slice(k * P, (k + 1) * P)
                    ins = nc.tensor.transpose(bank[b % 2][:, c], xnf[:, b, c], ident[:, :])
                ins.then_inc(x_t, 1)
            t.wait_ge(x_rows, 1)
            for s in range(2):
                o = bank[2][:, s * 32:(s + 1) * 32].rearrange("p (b q) -> p b q", b=B)
                for i in range(6):
                    ins = nc.tensor.matmul(o, bands[:, i, :], rows[:, i // 3, s, :, i % 3:i % 3 + 4], start=i == 0, stop=i == 5)
            ins.then_inc(x_z, 1)
            for j in range(2):
                t.wait_ge(x_zs, j + 1)
                nc.tensor.matmul(bank[3 + j][:, 0:2], ones_f[:, :], zs[:, 1 + j, :], start=True, stop=True).then_inc(x_tot, 1)
            for b in range(B):
                t.wait_ge(x_gt, b + 1)
                if b >= 2:
                    t.wait_ge(x_done, XD_L1X + b - 1)
                for k in range(KT):
                    c = slice(k * P, (k + 1) * P)
                    ins = nc.tensor.transpose(bank[b % 2][:, c], gT[:, b % 2, c], ident[:, :])
                ins.then_inc(x_gp, 1)
            ln_pe(t, LN_L1F[1])
            router_low_pe(t, 1, U_L1F, xTh_a, xTl_a)

            def base1(b):
                if b >= 4:
                    t.wait_ge(x_done, XD_L1F + b - 3)
                elif b < 2:
                    t.wait_ge(f_lowc, 2 * B - 1 + b % 2)
                c = slice(b * P, (b + 1) * P)
                for k in range(KT):
                    wh, wl = unit(U_L1F + 1 + k)
                    mm3(bank[b % 4][:], xTh_a[:, k, c], xTl_a[:, k, c], wh, wl, k == 0, False)
                nc.tensor.matmul(bank[b % 4][:], ones_r[0:2, 0:P], biasr[:, 576:1088], start=False, stop=False)

            base1(0)
            base1(1)
            router_turn_pe(t, 1)
            bh, bl = unit(U_L1F + 5)
            for b in range(B):
                if b + 2 < B:
                    base1(b + 2)
                if b in (0, 4):
                    t.wait_ge(f_tl, 3 + b // 4)
                c = slice(b * P, (b + 1) * P)
                mm3(bank[b % 4][:], lowT_h[:, c], lowT_l[:, c], bh, bl, False, True).then_inc(f_y, 1)
            owed[0] += 5
            t.wait_ge(c_lo, KT)
            def piece2(i, uh, ul, th, tl, half):
                if i >= 2:
                    t.wait_ge(a2_pf, i - 1)
                for k in range(KT):
                    kc, c = slice(k * P, (k + 1) * P), slice(half * HALF, (half + 1) * HALF)
                    ins = mm3(bank[6 + i % 2][:], uh[:, kc], ul[:, kc], th[:, k, c], tl[:, k, c], k == 0, k == KT - 1)
                ins.then_inc(a2_pj, 1)

            for s in range(2):
                base = U_L2X + 8 * s
                if s:
                    t.wait_ge(x_done, XD_L2X + B)
                uh, ul = unit(base)
                for half in range(2):
                    piece2(pj2(s, half), uh, ul, cTh, cTl, half)
                owed[0] += 1
                if s == 0:
                    uh, ul = unit(U_L2X + 1)
                    for half in range(2):
                        t.wait_ge(a2_pf, 1 + half)
                        for b in range(4 * half, 4 * half + 4):
                            o, c = bank[6 + half][:, b % 4 * P:(b % 4 + 1) * P], slice(b * P, (b + 1) * P)
                            for k in range(KT):
                                kc = slice(k * P, (k + 1) * P)
                                ins = mm3(o, cTh[:, k, c], cTl[:, k, c], uh[:, kc], ul[:, kc], k == 0, k == KT - 1)
                        ins.then_inc(a2_pj, 1)
                    owed[0] += 1
                    t.wait_ge(a2_pf, 4)
                    ln_pe(t, LN_L2X[1])
                    t.wait_ge(ln_lo, B * (LN_L2X[1] + 1))
                for half in range(2):
                    for r in range(4):
                        uh, ul = unit(base + (2 - s) + r)
                        piece2(pj2(s, 2 + 4 * half + r), uh, ul, xTh_b, xTl_b, half)
                owed[0] += 4
                t.wait_ge(a2_pf, pj2(s, 9) + 1)
                t.wait_ge(a2_one, 1)
                for l in range(38):
                    n = 32 * s + l
                    if l < 32:
                        b, gr = l // 4, slice(32 * (l % 4), 32 * (l % 4) + 16)
                        c = slice(b * P, (b + 1) * P)
                        if n >= 3:
                            t.wait_ge(a2_e, n - 2)
                        for r in range(4):
                            ins = nc.tensor.matmul(bank[n % 3][:, r * P:(r + 1) * P], q2[gr, r, c], k2[gr, c], start=True, stop=True)
                        ins.then_inc(a2_s, 1)
                    m = n - 2
                    if 2 <= l < 34:
                        t.wait_ge(a2_e, m + 1)
                        if m >= 2:
                            t.wait_ge(a2_pt, m - 1)
                        for r in range(4):
                            c = slice(r * P, (r + 1) * P)
                            ins = nc.tensor.transpose(bank[3 + m % 2][:, c], probs[:, m % 3, c], ident[:, :])
                        ins.then_inc(a2_t, 1)
                    m = n - 3
                    if 3 <= l < 35:
                        t.wait_ge(a2_pt, m + 1)
                        if m % 4 == 0 and m:
                            t.wait_ge(a2_on, m // 4)
                        for r in range(4):
                            at = (m % 4 * 4 + r) * 17
                            ins = nc.tensor.matmul(bank[5][:, at:at + 17], probsT[:, m % 3, r * P:(r + 1) * P],
                                                   v2[:, m % 32 // 4, 4 * s + m % 4, :], start=True, stop=True)
                        ins.then_inc(a2_pv, 1)
                    if l >= 7 and l % 4 == 3:
                        m = 8 * s + (l - 7) // 4
                        t.wait_ge(a2_on, m + 1)
                        if m % 8:
                            t.wait_ge(a2_ol, m)
                        for c in range(2):
                            ins = nc.tensor.transpose(bank[6][:, c * P:(c + 1) * P], on2[:, m % 2, c * P:(c + 1) * P], ident[:, :])
                        ins.then_inc(a2_ot, 1)
                    if l >= 9 and l % 4 == 1:
                        m = 8 * s + (l - 9) // 4
                        t.wait_ge(a2_ol, m + 1)
                        if m % 8:
                            t.wait_ge(x_done, XD_L2X + m)
                        for c in range(2):
                            uh, ul = unit(base + (6 - s) + c)
                            ins = mm3(bank[7][:], onT_h[:, m % 2, c * P:(c + 1) * P], onT_l[:, m % 2, c * P:(c + 1) * P], uh, ul,
                                      c == 0, c == 1)
                        ins.then_inc(a2_y, 1)
                owed[0] += 2
            ln_pe(t, LN_L2F[1])
            t.wait_ge(ln_lo, B * (LN_L2F[1] + 1))
            u = U_L2F
            for i, group in enumerate(FGROUPS):
                for f in group:
                    for half in range(2):
                        n = 2 * f + half
                        if n >= 2:
                            t.wait_ge(g_h, n - 1)
                        for j in range(2):
                            uh, ul = unit(u + j)
                            for k in range(KT):
                                kc, c = slice(k * P, (k + 1) * P), slice(half * HALF, (half + 1) * HALF)
                                ins = mm3(bank[2 * j + n % 2][:], uh[:, kc], ul[:, kc], xTh_b[:, k, c], xTl_b[:, k, c],
                                          k == 0, k == KT - 1)
                            ins.then_inc(g_p, 1)
                            owed[0] += half
                    u += 2
                for b in range(B):
                    t.wait_ge(g_hl, 2 * group[-1] + 1 + b // 4)
                    if i or b >= 2:
                        t.wait_ge(x_done, XD_L2F + B * i + b - 1)
                    c = slice(b * P, (b + 1) * P)
                    for f in range(len(group)):
                        uh, ul = unit(u + f)
                        ins = mm3(bank[4 + b % 2][:], hid_h[:, f, c], hid_l[:, f, c], uh, ul, f == 0, f == len(group) - 1)
                    ins.then_inc(g_y, 1)
                u += len(group)
                owed[0] += len(group)
            ln_pe(t, LN_L3X[1])
            t.wait_ge(ln_lo, B * (LN_L3X[1] + 1))
            for h in range(8):
                base = U_L3X + 10 * h
                for j in range(12):
                    half, r = ((j - 2) // 4, (j - 2) % 4) if 2 <= j < 10 else (j % 2, 0)
                    uh, ul = unit(base + (0 if j < 2 else 5 if j >= 10 else 1 + r))
                    th, tl = (xTh_b, xTl_b) if 2 <= j < 10 else (cTh, cTl)
                    if j >= 2:
                        t.wait_ge(a3_rp, 10 * h + j - 1)
                    elif h:
                        t.wait_ge(a3_v, 2 * h)
                    for k in range(KT):
                        kc, c = slice(k * P, (k + 1) * P), slice(half * HALF, (half + 1) * HALF)
                        ins = mm3(bank[6 + j % 2][:], uh[:, kc], ul[:, kc], th[:, k, c], tl[:, k, c], k == 0, k == KT - 1)
                    ins.then_inc(a3_pj, 1)
                    owed[0] += {1: 1, 9: 4, 11: 1}.get(j, 0)
                for l in range(11):
                    n = B * h + l
                    m = n - 2
                    if 2 <= l < B + 2:
                        t.wait_ge(a3_pn, m + 1)
                        if m >= 2:
                            t.wait_ge(a3_pt, m - 1)
                        for r in range(4):
                            c = slice(r * P, (r + 1) * P)
                            ins = nc.tensor.transpose(bank[2 + m % 2][:, c], probs[:, m % 3, c], ident[:, :])
                        ins.then_inc(a3_t, 1)
                    if l < B:
                        if n >= 2:
                            t.wait_ge(a3_e, n - 1)
                        t.wait_ge(a3_qk, 10 * h + (6 if l < 4 else 10))
                        b = slice(l * P, (l + 1) * P)
                        for r in range(4):
                            ins = nc.tensor.matmul(bank[n % 2][:, r * P:(r + 1) * P], q3[:, r, b], k3[:, b], start=True, stop=True)
                        ins.then_inc(a3_s, 1)
                    if l < 2:
                        t.wait_ge(a3_vc, 2 * h + l + 1)
                        for q in range(4):
                            c = slice(q * P, (q + 1) * P)
                            ins = nc.tensor.transpose(bank[6 + l][:, c], vT[:, l, c], ident[:, :])
                        ins.then_inc(a3_vt, 1)
                    if 2 <= l < B + 2:
                        t.wait_ge(a3_pt, m + 1)
                        t.wait_ge(a3_v, 2 * h + 2)
                        if m:
                            t.wait_ge(a3_ol, m)
                        nc.tensor.matmul(bank[4][:], v3[:, l - 2, :], probsT[:, m % 3, :], start=True, stop=True).then_inc(a3_pv, 1)
                    if l >= 3:
                        m = n - 3
                        t.wait_ge(a3_ol, m + 1)
                        if m:
                            t.wait_ge(x_done, XD_L3X + m)
                        for r in range(4):
                            uh, ul = unit(base + 6 + r)
                            c = slice(r * P, (r + 1) * P)
                            ins = mm3(bank[5][:], o3h[:, m % 2, c], o3l[:, m % 2, c], uh, ul, r == 0, r == 3)
                        ins.then_inc(a3_y, 1)
                owed[0] += 4
            ln_pe(t, LN_L3F[1])
            t.wait_ge(ln_lo, B * (LN_L3F[1] + 1))
            t.wait_ge(z_pick, 1)
            for n in range(8):
                if n >= 4:
                    t.wait_ge(z_tl, n - 3)
                c = slice(n % 2 * HALF, (n % 2 + 1) * HALF)
                for k in range(KT):
                    w = pick[:, k, n // 2 * P:(n // 2 + 1) * P]
                    nc.tensor.matmul(bank[n % 4][:], w, xTh_b[:, k, c], start=k == 0, stop=False)
                    ins = nc.tensor.matmul(bank[n % 4][:], w, xTl_b[:, k, c], start=False, stop=k == KT - 1)
                ins.then_inc(z_t, 1)
            uh, ul = unit(U_L3F)
            for n in range(34):
                if n < 32:
                    i4, half, gr = n // 8, n // 4 % 2, slice(32 * (n % 4), 32 * (n % 4) + 32)
                    if n % 4 == 0:
                        t.wait_ge(z_tl, n // 4 + 1)
                    if n >= 2:
                        t.wait_ge(z_g, n - 1)
                    w, c = slice(i4 * P, (i4 + 1) * P), slice(half * HALF, (half + 1) * HALF)
                    mm3(bank[4 + n % 2][:], uh[gr, w], ul[gr, w], tTh[gr, i4, c], tTl[gr, i4, c], True, True).then_inc(z_up, 1)
                m = n - 2
                if m >= 0:
                    o = m // 4
                    if m == 0:
                        t.wait_ge(z_dn, 1)
                    if m % 4 == 0 and o >= 2:
                        t.wait_ge(z_ol, o - 1)
                    t.wait_ge(z_gl, m + 1)
                    hh = 4 * (m // 8) + m % 4
                    dst = bank[6 + o % 2][:]
                    nc.tensor.matmul(dst, down_h[:, hh, :], gel_h[:, m % 2, :], start=m % 4 == 0, stop=False)
                    nc.tensor.matmul(dst, down_l[:, hh, :], gel_h[:, m % 2, :], start=False, stop=False)
                    nc.tensor.matmul(dst, down_h[:, hh, :], gel_l[:, m % 2, :], start=False, stop=m % 4 == 3).then_inc(z_dp, 1)
            t.wait_ge(z_pick, 2)
            t.wait_ge(z_ol, 8)
            for b in range(B):
                if b >= 4:
                    t.wait_ge(x_done, XD_L3F + b - 3)
                c = slice(b * P, (b + 1) * P)
                for k in range(KT):
                    nc.tensor.matmul(bank[b % 4][:], t2h[:, k, c], put[:, k, :], start=k == 0, stop=False)
                    ins = nc.tensor.matmul(bank[b % 4][:], t2l[:, k, c], put[:, k, :], start=False, stop=k == KT - 1)
                ins.then_inc(z_y, 1)



def kernel(**inputs):
    import numpy as _np
    import concourse.bacc as _bacc
    from concourse import mybir as _mybir
    from concourse.bass_utils import run_bass_kernel_spmd as _run

    nc = _bacc.Bacc("TRN2", target_bir_lowering=False, num_devices=1)
    arrays, d = {}, {}
    for name, a in lay_out({k: _np.asarray(v) for k, v in inputs.items()}).items():
        arrays[f"in_{name}_dram"] = a
        d[name] = nc.dram_tensor(f"in_{name}_dram", a.shape, _mybir.dt.from_np(a.dtype), kind="ExternalInput").ap()
    out = nc.dram_tensor("out_0_dram", (B, P, D), _mybir.dt.float32, kind="ExternalOutput").ap()
    program(nc, d, out)
    r = _run(nc, [arrays], core_ids=[0])
    return r.results[0]["out_0_dram"]
```

```python
from contextlib import ExitStack

import concourse.bass as bass
from concourse import mybir
from concourse.alu_op_type import AluOpType as ALU
import numpy as np

F32 = mybir.dt.float32
F32R = mybir.dt.float32r
BF16 = mybir.dt.bfloat16
I32 = mybir.dt.int32
ACT = mybir.ActivationFunctionType
AX = mybir.AxisListType

P = 128
B = 8
D = 512
KT = D // P
TOK = B * P
HALF = TOK // 2
F2 = 1376
FT = [P] * (F2 // P) + [F2 % P]
FGROUPS = [range(0, 4), range(4, 8), range(8, 11)]
RING, STAGE = 10, 5
N_CRUCIAL = 76
N_REST = P - N_CRUCIAL
ROUNDS = 7
DUMMY, TAKEN = 3.0e38, -3.4028234663852886e38
BIG = 1.0e9
EPS = 1e-5

U_L0F = 0
U_L1F = U_L0F + 2
U_L2X = U_L1F + 6
U_L2F = U_L2X + 19
U_L3X = U_L2F + 3 * len(FT)
U_L3F = U_L3X + 80
N_UNITS = U_L3F + 2

(C_QA, C_QM, C_KA, C_KM, C_BIG, C_RA, C_RM, C_EXT) = range(8)
C_IOTA = 8
N_CON = C_IOTA + KT
W0Q, W0K, W0V, W0O = 0, 256, 512, 576
N_W0 = 704


def constants():
    p = np.arange(P)
    con = np.zeros((P, N_CON), np.float32)
    s0 = np.float32(-1 / np.sqrt(8.0))
    hi = (p % 32) // 8 % 2 == 0
    con[:, C_QA], con[:, C_QM] = np.where(hi, s0, -s0), np.where(hi, 0, s0)
    hi = (p % 32) // 8 < 2
    con[:, C_KA], con[:, C_KM] = np.where(hi, 1, -1), np.where(hi, 0, 1)
    big_hi = np.float32(2.0 ** 18 * 3815)
    con[:, C_BIG] = np.where(p % 32 == 0, big_hi, np.where(p % 32 == 1, np.float32(BIG) - big_hi, 0))
    hi = p % 2 == 0
    con[:, C_RA], con[:, C_RM] = np.where(hi, 1, -1), np.where(hi, 0, 1)
    con[:, C_EXT] = p + 192
    for k in range(KT):
        con[:, C_IOTA + k] = p + P * k
    t = np.arange(512, dtype=np.float32)[:, None]
    inv = (1.0 / np.float32(10000.0) ** (np.arange(0, P, 2, dtype=np.float32) / np.float32(P))).astype(np.float32)
    ang = np.concatenate([t * inv, t * inv], 1).astype(np.float32)
    sin = np.sin(ang)
    sin[:, :64] *= -1
    tabs = np.stack([np.cos(ang), sin]).astype(np.float32).reshape(2, KT, P, P)
    return {"con": con, "ident": np.eye(P, dtype=np.float32), "tabs": tabs,
            "iota": np.broadcast_to(np.arange(512, dtype=np.float32), (P, 512)).copy()}


def lay_out(i):
    c = np.ascontiguousarray

    def tiles(w):
        return w.reshape(KT, P, -1).transpose(1, 0, 2).reshape(P, -1)

    def lora(a):
        return a.reshape(P, -1)

    units = [tiles(lora(i["L0_ffn_A"]).T), i["L0_ffn_B"].transpose(0, 2, 1).reshape(P, D)]
    wb = i["L1_ffn_W_base"].T
    units += [tiles(lora(i["L1_ffn_lora_A"]).T)] + [wb[k * P:(k + 1) * P] for k in range(KT)]
    units += [i["L1_ffn_lora_B"].transpose(0, 2, 1).reshape(P, D)]
    wq = i["L2_xattn_Wq"].reshape(D, 2, 4, 4, 16).transpose(0, 1, 3, 2, 4)
    wq = np.repeat(wq[:, :, :, :, None], 2, 4).reshape(D, 2, 4, P)
    wo = i["L2_xattn_Wo"].reshape(2, 4, 4, 16, D).transpose(0, 2, 1, 3, 4)
    wo = np.concatenate([wo, np.zeros_like(wo)], 3).reshape(2, 4, P, D)
    wk = np.repeat(i["L2_xattn_Wk"].reshape(D, 2, 4, 1, 16), 2, 3).reshape(D, 2, P)
    for s in range(2):
        q = [tiles(wq[:, s, r]) for r in range(4)]
        units += q + [tiles(wk[:, s]), tiles(i["L2_xattn_Wv"])] if s == 0 else [tiles(wk[:, s])] + q
        units += [wo[s, r] for r in range(4)]
    zeros = np.zeros((D, P - FT[-1]), np.float32)
    gate, up, down = i["L2_ffn_W_gate"].T, i["L2_ffn_W_up"].T, i["L2_ffn_W_down"].T
    gate, up = np.concatenate([gate, zeros], 1), np.concatenate([up, zeros], 1)
    down = np.concatenate([down, zeros.T], 0)
    for group in FGROUPS:
        for f in group:
            units += [tiles(gate[:, f * P:(f + 1) * P]), tiles(up[:, f * P:(f + 1) * P])]
        units += [down[f * P:(f + 1) * P] for f in group]
    for h in range(8):
        units += [tiles(i["L3_xattn_Wk"][:, h * P:(h + 1) * P])]
        units += [tiles(i["L3_xattn_Wq"][:, (4 * h + r) * P:(4 * h + r + 1) * P]) for r in range(4)]
        units += [tiles(i["L3_xattn_Wv"][:, h * P:(h + 1) * P])]
        units += [i["L3_xattn_Wo"][(4 * h + r) * P:(4 * h + r + 1) * P] for r in range(4)]
    units += [i["L3_ffn_up"].reshape(4, P, P).transpose(1, 0, 2).reshape(P, D)]
    units += [i["L3_ffn_down"].transpose(1, 0, 2).reshape(P, D)]
    w0 = np.concatenate([
        np.repeat(i["L0_xattn_Wq"].T.reshape(P, 8, 1, 8), 4, 2).reshape(P, 256),
        np.repeat(i["L0_xattn_Wk"].T.reshape(P, 8, 1, 8), 4, 2).reshape(P, 256), i["L0_xattn_Wv"].T,
        np.concatenate([i["L0_xattn_Wo"].T] * 2, 0)], 1)
    b0 = np.concatenate([np.repeat(i["L0_xattn_bq"].reshape(8, 1, 8), 4, 1).reshape(256),
                         np.repeat(i["L0_xattn_bk"].reshape(8, 1, 8), 4, 1).reshape(256), i["L0_xattn_bv"],
                         i["L1_ffn_b_base"]])
    context = i["ctx_4096"]
    out = {
        "x": i["x"], "context": context, "contextT": context.transpose(2, 0, 1).reshape(KT, P, TOK),
        "context_lc": context.transpose(0, 2, 1)[:, :, ::-1].reshape(32, P, P),
        "mask_row": i["mask_Bx1x4096_ff1"].reshape(B, D), "mask3": i["mask_BxSxS2_ik0"], "pos": i["pos_BxS2"].reshape(1, TOK),
        "perm_row": i["L3_ffn_perm"].reshape(1, D), "perm_col": i["L3_ffn_perm"].reshape(KT, P).T,
        "units": np.stack(units), "w0": w0, "b0": np.stack([b0, b0]), "bo": i["L0_xattn_bo"].reshape(P, 1),
        "wr": np.stack([tiles(i["L0_ffn_Wr"].T), tiles(i["L1_ffn_W_router"].T)]),
        "br": i["L0_ffn_br"].reshape(1, 8),
        "conv": np.concatenate([i["L1_xattn_conv_w"].reshape(1, 14), i["L1_xattn_bn_gamma"].reshape(1, 1),
                                i["L1_xattn_bn_beta"].reshape(1, 1)], 1),
    }
    out.update(constants())
    return {k: c(v) for k, v in out.items()}

X_BEFORE = [B * n for n in (0, 1, 2, 3, 4, 6, 9, 17)]
XD_L0A = B * 0
XD_L0F = B * 1
XD_L1X = B * 2
XD_L1F = B * 3
XD_CX = B * 4
XD_L2X = B * 4
XD_L2F = B * 6
XD_L3X = B * 9
XD_L3F = B * 17
XD_END = B * 18
LN_L0A = (0, 0)
LN_L0F = (1, 0)
LN_L1X = (2, 1)
LN_L1F = (3, 1)
LN_L2X = (4, 2)
LN_L2F = (5, 3)
LN_L3X = (6, 4)
LN_L3F = (7, 5)


class Stream:

    def __init__(self, step):
        self.step, self.next = step, 0

    def upto(self, n):
        while self.next < min(n, N_UNITS):
            self.step(self.next)
            self.next += 1


def program(nc, d, out):
    with ExitStack() as ctx:
        def sem(name):
            return ctx.enter_context(nc.semaphore(name))

        def sb(name, shape, dt=F32, where=ctx):
            return where.enter_context(nc.sbuf_tensor(name, shape, dt))

        bank = [ctx.enter_context(nc.psum_tensor(f"bank{i}", [P, 512], F32)) for i in range(8)]

        X = sb("X", [P, B, D])
        ring_h = sb("ring_h", [P, RING, 512], F32R)
        ring_l = sb("ring_l", [P, RING, 512], F32R)
        stage = sb("stage", [P, STAGE, 512])
        probs = sb("probs", [P, 3, 512])
        probsT = sb("probsT", [P, 3, 512])
        nbias = sb("nbias", [P, 4, 4])
        psums = sb("psums", [P, 4, 4])
        rsums = sb("rsums", [P, 4, 4])
        xn = sb("xn", [P, 4, D])
        ident = sb("ident", [P, P])
        con = sb("con", [P, N_CON])
        iota = sb("iota", [P, 512])
        ones_r = sb("ones_r", [P, 512], F32R)
        cosT = sb("cosT", [P, TOK])
        sinT = sb("sinT", [P, TOK])
        stats = sb("stats", [P, B, 6])
        mv = sb("mv", [P, B, 2])
        vare = sb("vare", [P, B])
        rstd = sb("rstd", [P, B])
        mhalf = sb("mhalf", [P, B])
        wr = sb("wr", [P, 2, 32])
        wrh = sb("wrh", [P, 2, 32], F32R)
        wrl = sb("wrl", [P, 2, 32], F32R)
        br = sb("br", [P, 8])
        conv = sb("conv", [P, 16])

        eA = ExitStack()
        crucial = sb("crucial", [P, 32, P], BF16, eA)
        bands = sb("bands", [P, 6, P], F32, eA)
        biasr = sb("biasr", [2, 1088], F32R, eA)

        e0 = ExitStack()
        mask0 = sb("mask0", [P, 2, D], F32, e0)
        o0T = sb("o0T", [64, B, D], F32, e0)
        topv = sb("topv", [P, 32, 132], F32, e0)
        top8 = sb("top8", [P, 4, 8], F32, e0)
        w0h = sb("w0h", [P, N_W0], F32R, e0)
        w0l = sb("w0l", [P, N_W0], F32R, e0)
        bo = sb("bo", [P, 1], F32, e0)
        w0v = sb("w0v", [P, 64], F32, e0)
        zeros_r = sb("zeros_r", [2, 64], F32R, e0)
        es = ExitStack()
        w0 = sb("w0", [P, N_W0], F32, es)
        bias_f = sb("bias_f", [2, 1088], F32, es)
        bias_a = sb("bias_a", [2, 1088], F32, es)
        tabs = sb("tabs", [P, 2, KT, P], F32, es)
        pos_i = sb("pos_i", [P, TOK], I32, es)
        hot = sb("hot", [P, KT, TOK], F32, es)
        es.close()
        ea = ExitStack()
        xnh = sb("xnh", [P, 2, D], F32R, ea)
        xnl = sb("xnl", [P, 2, D], F32R, ea)
        keep = sb("keep", [P, D], F32, ea)
        mrow = sb("mrow", [P, 2, D], F32R, ea)
        q0 = sb("q0", [P, 2, 2, D], F32R, ea)
        k0 = sb("k0", [P, 2, 2, D], F32R, ea)
        halfA = sb("halfA", [P, D], F32, ea)
        v0 = sb("v0", [P, 2, 4, 8 * 72], F32, ea)
        ea.close()
        eo = ExitStack()
        g0 = sb("g0", [64, 2, D], F32, eo)
        g0h = sb("g0h", [64, 2, D], F32R, eo)
        g0l = sb("g0l", [64, 2, D], F32R, eo)
        upd = sb("upd", [P, 2, D], F32, eo)
        eo.close()
        e0.close()

        ef = ExitStack()
        xTh_a = sb("xTh_a", [P, KT, TOK], F32R, ef)
        xTl_a = sb("xTl_a", [P, KT, TOK], F32R, ef)
        low = sb("low", [P, B, P], F32, ef)
        lowT_h = sb("lowT_h", [P, TOK], F32R, ef)
        lowT_l = sb("lowT_l", [P, TOK], F32R, ef)
        lg = sb("lg", [P, B, 14], F32, ef)
        rt = sb("rt", [P, 4, B], F32, ef)
        sc = sb("sc", [P, 2, B, 8], F32, ef)
        t8 = sb("t8", [P, B, 8], F32, ef)
        ef.close()

        ex = ExitStack()
        xnf = sb("xnf", [P, B, D], F32, ex)
        cf = sb("cf", [P, 2, 2, 512], F32, ex)
        rows = sb("rows", [P, 2, 2, B, 6], F32, ex)
        junk = sb("junk", [P, 2, 4, P], F32, ex)
        z = sb("z", [P, 2, 32], F32, ex)
        zz = sb("zz", [P, 2, 32], F32, ex)
        zs = sb("zs", [P, 8, 2], F32, ex)
        gains = sb("gains", [P, 3, 32], F32, ex)
        gT = sb("gT", [P, 2, 512], F32, ex)
        tmpx = sb("tmpx", [P, 2, 512], F32, ex)
        ones_f = sb("ones_f", [P, P], F32, ex)
        ex.close()
        eA.close()

        eB = ExitStack()
        xTh_b = sb("xTh_b", [P, KT, TOK], F32R, eB)
        xTl_b = sb("xTl_b", [P, KT, TOK], F32R, eB)
        cx = ExitStack()
        cTh = sb("cTh", [P, KT, TOK], F32R, cx)
        cTl = sb("cTl", [P, KT, TOK], F32R, cx)
        e2 = ExitStack()
        q2 = sb("q2", [P, 4, TOK], F32, e2)
        k2 = sb("k2", [P, TOK], F32, e2)
        v2 = sb("v2", [P, B, 8, 32], F32, e2)
        onT_h = sb("onT_h", [P, 2, 512], F32R, e2)
        onT_l = sb("onT_l", [P, 2, 512], F32R, e2)
        e2.close()
        eg = ExitStack()
        silu = sb("silu", [P, 2, 512], F32, eg)
        hid = sb("hid", [P, 2, 512], F32, eg)
        hid_h = sb("hid_h", [P, 4, TOK], F32R, eg)
        hid_l = sb("hid_l", [P, 4, TOK], F32R, eg)
        eg.close()
        e3 = ExitStack()
        q3 = sb("q3", [P, 4, TOK], F32, e3)
        k3 = sb("k3", [P, TOK], F32, e3)
        v3 = sb("v3", [P, B, P], F32, e3)
        vT = sb("vT", [P, 2, 512], F32, e3)
        o3h = sb("o3h", [P, 2, 512], F32R, e3)
        o3l = sb("o3l", [P, 2, 512], F32R, e3)
        mask3 = sb("mask3", [P, B, P], I32, e3)
        big = sb("big", [P, P], F32, e3)
        e3.close()
        cx.close()
        e4 = ExitStack()
        tTh = sb("tTh", [P, 4, TOK], F32R, e4)
        tTl = sb("tTl", [P, 4, TOK], F32R, e4)
        pick = sb("pick", [P, KT, 512], F32R, e4)
        put = sb("put", [P, KT, 512], F32R, e4)
        perm_i = sb("perm_i", [P, 520], I32, e4)
        down_h = sb("down_h", [P, 16, P], F32R, e4)
        down_l = sb("down_l", [P, 16, P], F32R, e4)
        gel_h = sb("gel_h", [P, 2, 512], F32R, e4)
        gel_l = sb("gel_l", [P, 2, 512], F32R, e4)
        e4.close()
        eB.close()
        t2h, t2l = xTh_b, xTl_b
        kkeep, ctx_n = stage[:, 2, :], stage[:, 3:5, :]
        gel = probs
        perm_f = probsT[:].rearrange("p a b -> p (a b)")

        def f32(ap):
            return ap.bitcast(F32)

        s_con = sem("s_con")
        s_x = sem("s_x")
        s_w0 = sem("s_w0")
        s_tab = sem("s_tab")
        s_rest = sem("s_rest")
        s_topv = sem("s_topv")
        s_ctx = [sem(f"s_ctx{i}") for i in range(2)]
        s_m0 = [sem(f"s_m0{i}") for i in range(2)]
        s_unit = [sem(f"s_unit{i}") for i in range(STAGE)]
        s_ctxT = [sem(f"s_ctxT{i}") for i in range(2)]
        s_m3 = sem("s_m3")
        s_perm = sem("s_perm")
        s_out = sem("s_out")
        w_hi = sem("w_hi")
        w_lo = sem("w_lo")
        w_used = sem("w_used")
        v_chain = sem("v_chain")
        a_chain = sem("a_chain")
        p_chain = sem("p_chain")
        ln_st, ln_mv, ln_rstd, ln_xn, ln_t, ln_hi, ln_lo = [sem(f"ln_{n}") for n in ("st", "mv", "rstd", "xn", "t", "hi", "lo")]
        ln_ve = sem("ln_ve")
        x_done = sem("x_done")

        chains = {}

        def link(eng, chain, ins):
            chains[chain.name] = chains.get(chain.name, 0) + 1
            ins.then_inc(chain, 1)
            eng.wait_ge(chain, chains[chain.name])

        owed = [0]

        def mm3(out_ap, wh, wl, mh, ml, start, stop):
            ins = nc.tensor.matmul(out_ap, wh, mh, start=start, stop=False)
            if owed[0]:
                ins.then_inc(w_used, owed[0])
                owed[0] = 0
            nc.tensor.matmul(out_ap, wh, ml, start=False, stop=False)
            return nc.tensor.matmul(out_ap, wl, mh, start=False, stop=stop)

        def slot(u):
            return ring_h[:, u % RING, :], ring_l[:, u % RING, :]

        def col(k, parts=slice(None)):
            return con[parts, k:k + 1]

        def ln_step(v, n_ln, b):
            if 1 <= b <= B:
                if X_BEFORE[n_ln]:
                    v.wait_ge(x_done, X_BEFORE[n_ln] - B + b)
                nc.vector.bn_stats(stats[:, b - 1, :], X[:, b - 1, :]).then_inc(ln_st, 1)
            if b >= 2:
                v.wait_ge(ln_st, B * n_ln + b - 1)
                nc.vector.bn_aggr(mv[:, b - 2, :], stats[:, b - 2, :]).then_inc(ln_mv, 1)

        def ln_pool(g, n_ln):
            for b in range(B + 1):
                if b < B:
                    g.wait_ge(ln_mv, B * n_ln + b + 1)
                    nc.gpsimd.tensor_scalar(vare[:, b:b + 1], mv[:, b, 1:2], EPS, 1.0, ALU.add, ALU.mult).then_inc(ln_ve, 1)
                if b >= 1:
                    g.wait_ge(ln_ve, B * n_ln + b)
                    nc.gpsimd.tensor_tensor(rstd[:, b - 1:b], vare[:, b - 1:b], mhalf[:, b - 1:b], ALU.pow).then_inc(ln_rstd, 1)

        def ln_norm(v, n_ln, b, to):
            v.wait_ge(ln_rstd, B * n_ln + b + 1)
            v.wait_ge(ln_mv, B * n_ln + b + 1)
            return nc.vector.tensor_scalar(to, X[:, b, :], mv[:, b, 0:1], rstd[:, b:b + 1], ALU.subtract, ALU.mult)

        def by_tile(ap):
            return ap.rearrange("p (k t) -> p k t", k=KT)

        def ln_dve(v, n_ln, n, th, tl):
            def low_half(b):
                v.wait_ge(ln_hi, B * n + b + 1)
                cut = slice(b * P, (b + 1) * P)
                nc.vector.tensor_tensor(tl[:, :, cut], by_tile(bank[6 + b % 2][:]),
                                        f32(th[:, :, cut]), ALU.subtract).then_inc(ln_lo, 1)

            for b in range(B):
                if b >= 4:
                    v.wait_ge(ln_t, B * n + b - 3)
                ln_norm(v, n_ln, b, xn[:, b % 4, :]).then_inc(ln_xn, 1)
                if b >= 2:
                    low_half(b - 2)
            low_half(B - 2)
            low_half(B - 1)

        def ln_pe(t, n):
            for b in range(B):
                t.wait_ge(ln_xn, B * n + b + 1)
                if b >= 2:
                    t.wait_ge(ln_lo, B * n + b - 1)
                for k in range(KT):
                    ins = nc.tensor.transpose(bank[6 + b % 2][:, k * P:(k + 1) * P],
                                              xn[:, b % 4, k * P:(k + 1) * P], ident[:, :])
                ins.then_inc(ln_t, 1)

        def ln_act(a, n, th):
            for b in range(B):
                a.wait_ge(ln_t, B * n + b + 1)
                nc.scalar.activation(th[:, :, b * P:(b + 1) * P], by_tile(bank[6 + b % 2][:]),
                                     ACT.Copy).then_inc(ln_hi, 1)

        su_hot = sem("su_hot")
        su_rope = sem("su_rope")
        su_rc = sem("su_rc")
        su_w0 = sem("su_w0")
        su_ba = sem("su_ba")
        su_bias = sem("su_bias")
        su_wr = sem("su_wr")
        su_one = sem("su_one")
        su_mh = sem("su_mh")
        a0_x = sem("a0_x")
        a0_in = sem("a0_in")
        a0_c = sem("a0_c")
        a0_pj = sem("a0_pj")
        a0_A = sem("a0_A")
        a0_kk = sem("a0_kk")
        a0_pf = sem("a0_pf")
        a0_vc = sem("a0_vc")
        a0_neg = sem("a0_neg")
        a0_tf = sem("a0_tf")
        a0_tk = sem("a0_tk")
        a0_m0 = sem("a0_m0")
        a0_s = sem("a0_s")
        a0_mx = sem("a0_mx")
        a0_e = sem("a0_e")
        a0_t = sem("a0_t")
        a0_pt = sem("a0_pt")
        a0_pv = sem("a0_pv")
        a0_rc = sem("a0_rc")
        a0_pn = sem("a0_pn")
        a0_ot = sem("a0_ot")
        a0_one = sem("a0_one")
        o0_gh = sem("o0_gh")
        o0_gl = sem("o0_gl")
        o0_y = sem("o0_y")

        def pj0(b, p):
            return 5 * b + p

        def bank0(b, p):
            return bank[6 + pj0(b, p) % 2]

        def used0(t, i):
            b, p = i // 5, i % 5
            if p < 2:
                t.wait_ge(a0_pf, 4 * b + p + 1)
            elif p < 4:
                t.wait_ge(a0_kk, 2 * b + p - 1)
            else:
                t.wait_ge(a0_vc, b + 1)

        def free0(sp_like, b):
            if b >= 2:
                sp_like.wait_ge(a0_pj, pj0(b - 2, 4) + 1)

        f_low = sem("f_low")
        f_lowc = sem("f_lowc")
        f_mx = sem("f_mx")
        f_e = sem("f_e")
        f_ls = sem("f_ls")
        f_t = sem("f_t")
        f_th = sem("f_th")
        f_tl = sem("f_tl")
        f_y = sem("f_y")

        def router_act(a, i):
            a.wait_ge(f_mx, i + 1)
            nc.scalar.activation(sc[:, 0, :, :], lg[:, :, 0:8], ACT.Exp).then_inc(f_e, 1)
            for j in range(2):
                a.wait_ge(f_t, 2 * i + j + 1)
                nc.scalar.activation(lowT_h[:, j * 512:(j + 1) * 512], bank[4 + j][:], ACT.Copy).then_inc(f_th, 1)

        def band(v, i):
            shift = probs[:, 2, :]
            if i == 0:
                link(v, v_chain, nc.vector.tensor_scalar(shift, iota[:, :], col(C_EXT), None, ALU.is_equal))
            ch, dt = i // 3, i % 3 - 1
            taps = {0: range(7), 1: range(4, 7), -1: range(0, 3)}[dt]
            for k in taps:
                at = 189 + k - P * dt
                w = conv[:, ch * 7 + k:ch * 7 + k + 1]
                if k == taps[0]:
                    link(v, v_chain, nc.vector.tensor_scalar(bands[:, i, :], shift[:, at:at + P], w, None, ALU.mult))
                else:
                    link(v, v_chain, nc.vector.scalar_tensor_tensor(bands[:, i, :], shift[:, at:at + P], w, bands[:, i, :],
                                                                    ALU.mult, ALU.add))

        def router_dve(v, i, n_next):
            for b in range(B):
                v.wait_ge(f_low, B * i + b + 1)
                nc.vector.tensor_copy(low[:, b, :], bank[b % 2][:, 0:P])
                if i == 0:
                    nc.vector.tensor_tensor(lg[:, b, 0:8], bank[b % 2][:, P:P + 8], br[:, :], ALU.add).then_inc(f_lowc, 1)
                else:
                    nc.vector.tensor_copy(lg[:, b, 0:8], bank[b % 2][:, P:P + 8]).then_inc(f_lowc, 1)
                if i == 0 and b < 6:
                    band(v, b)
            v.wait_ge(f_lowc, B * i + B)
            link(v, v_chain, nc.vector.tensor_reduce(rt[:, 0, :], lg[:, :, 0:8], AX.X, ALU.max))
            nc.vector.tensor_tensor(lg[:, :, 0:8], lg[:, :, 0:8], rt[:, 0, :].unsqueeze(2).to_broadcast((P, B, 8)),
                                    ALU.subtract).then_inc(f_mx, 1)
            if i == 1:
                link(v, v_chain, nc.vector.memset(lg[:, :, 8:14], DUMMY))
                v.wait_ge(f_mx, i + 1)
                for b in range(B):
                    ins = nc.vector.max(t8[:, b, :], lg[:, b, :])
                link(v, v_chain, ins)
            v.wait_ge(f_e, i + 1)
            if i == 1:
                for b in range(B):
                    ins = nc.vector.match_replace(lg[:, b, :], t8[:, b, :], lg[:, b, :], TAKEN)
                link(v, v_chain, ins)
                link(v, v_chain, nc.vector.scalar_tensor_tensor(sc[:, 0, :, :], lg[:, :, 0:8], TAKEN, sc[:, 0, :, :],
                                                                ALU.is_equal, ALU.mult))
            link(v, v_chain, nc.vector.tensor_reduce(rt[:, 1, :], sc[:, 0, :, :], AX.X, ALU.add))
            link(v, v_chain, nc.vector.reciprocal(rt[:, 2, :], rt[:, 1, :]))
            link(v, v_chain, nc.vector.tensor_scalar(rt[:, 3, :], rt[:, 2, :], (16.0, 2.0)[i], None, ALU.mult))
            link(v, v_chain, nc.vector.tensor_tensor(sc[:, 1, :, :], sc[:, 0, :, :],
                                                     rt[:, 3, :].unsqueeze(2).to_broadcast((P, B, 8)), ALU.mult))
            for j in range(2):
                rows4 = low[:, 4 * j:4 * j + 4, :].rearrange("p b (h r) -> p (b h) r", r=16)
                by = sc[:, 1, 4 * j:4 * j + 4, :].rearrange("p b h -> p (b h)").unsqueeze(2).to_broadcast((P, 32, 16))
                nc.vector.tensor_tensor(rows4, rows4, by, ALU.mult).then_inc(f_ls, 1)
            for j in range(2):
                v.wait_ge(f_th, 2 * i + j + 1)
                cut = slice(j * 512, (j + 1) * 512)
                nc.vector.tensor_tensor(lowT_l[:, cut], bank[4 + j][:], f32(lowT_h[:, cut]), ALU.subtract).then_inc(f_tl, 1)
            for b in range(B):
                v.wait_ge(f_y, B * i + b + 1)
                nc.vector.tensor_tensor(X[:, b, :], X[:, b, :], bank[b % 4][:], ALU.add).then_inc(x_done, 1)
                ln_step(v, n_next, b)
            ln_step(v, n_next, B)
            ln_step(v, n_next, B + 1)

        def router_low_pe(t, i, u, th, tl):
            t.wait_ge(su_wr, 2)
            t.wait_ge(w_lo, u + 1)
            ah, al = slot(u)
            for b in range(B):
                if b >= 2:
                    t.wait_ge(f_lowc, B * i + b - 1)
                t.wait_ge(ln_lo, B * LN_L0F[1] + B * i + b + 1)
                c = slice(b * P, (b + 1) * P)
                for k in range(KT):
                    kc = slice(k * P, (k + 1) * P)
                    mm3(bank[b % 2][:, 0:P], th[:, k, c], tl[:, k, c], ah[:, kc], al[:, kc], k == 0, k == KT - 1)
                for k in range(KT):
                    kc = slice(8 * k, 8 * k + 8)
                    ins = mm3(bank[b % 2][:, P:P + 8], th[:, k, c], tl[:, k, c], wrh[:, i, kc], wrl[:, i, kc],
                              k == 0, k == KT - 1)
                ins.then_inc(f_low, 1)
            owed[0] += 1

        def router_turn_pe(t, i):
            for j in range(2):
                t.wait_ge(f_ls, 2 * i + j + 1)
                for q in range(4):
                    ins = nc.tensor.transpose(bank[4 + j][:, q * P:(q + 1) * P], low[:, 4 * j + q, :], ident[:, :])
                ins.then_inc(f_t, 1)

        x_x = sem("x_x")
        x_t = sem("x_t")
        x_cf = sem("x_cf")
        x_mx = sem("x_mx")
        x_sum = sem("x_sum")
        x_rows = sem("x_rows")
        x_z = sem("x_z")
        x_zs = sem("x_zs")
        x_tot = sem("x_tot")
        x_var = sem("x_var")
        x_rs = sem("x_rs")
        x_arg = sem("x_arg")
        x_e = sem("x_e")
        x_gt = sem("x_gt")
        x_gp = sem("x_gp")
        c_hi = sem("c_hi")
        c_lo = sem("c_lo")

        def chunk(k):
            return (probs, probsT)[k % 2][:, 0:2, :].rearrange("p a f -> p (a f)")

        a2_pj = sem("a2_pj")
        a2_pf = sem("a2_pf")
        a2_one = sem("a2_one")
        a2_s = sem("a2_s")
        a2_mx = sem("a2_mx")
        a2_e = sem("a2_e")
        a2_t = sem("a2_t")
        a2_pt = sem("a2_pt")
        a2_pv = sem("a2_pv")
        a2_rc = sem("a2_rc")
        a2_pn = sem("a2_pn")
        a2_oh = sem("a2_oh")
        a2_ol = sem("a2_ol")
        a2_y = sem("a2_y")

        def pj2(s, j):
            return 12 + j if s else (j - 2) % 12 if j < 10 and j >= 2 else 8 + (j if j < 2 else j - 8)

        def unit2(s, kind, r=0):
            return U_L2X + ({"q": 0, "k": 4, "v": 5, "o": 6} if s == 0 else {"k": 10, "q": 11, "o": 15})[kind] + r

        g_p = sem("g_p")
        g_s = sem("g_s")
        g_h = sem("g_h")
        g_hh = sem("g_hh")
        g_hl = sem("g_hl")
        g_y = sem("g_y")
        a3_pj = sem("a3_pj")
        a3_rp = sem("a3_rp")
        a3_qk = sem("a3_qk")
        a3_vc = sem("a3_vc")
        a3_vt = sem("a3_vt")
        a3_v = sem("a3_v")
        a3_m = sem("a3_m")
        a3_s = sem("a3_s")
        a3_mx = sem("a3_mx")
        a3_e = sem("a3_e")
        a3_rc = sem("a3_rc")
        a3_pn = sem("a3_pn")
        a3_t = sem("a3_t")
        a3_pt = sem("a3_pt")
        a3_pv = sem("a3_pv")
        a3_oh = sem("a3_oh")
        a3_ol = sem("a3_ol")
        a3_y = sem("a3_y")
        z_pf = sem("z_pf")
        z_pick = sem("z_pick")
        z_t = sem("z_t")
        z_th = sem("z_th")
        z_tl = sem("z_tl")
        z_dz = sem("z_dz")
        z_dn = sem("z_dn")
        z_up = sem("z_up")
        z_g = sem("z_g")
        z_gh = sem("z_gh")
        z_gl = sem("z_gl")
        z_dp = sem("z_dp")
        z_oh = sem("z_oh")
        z_ol = sem("z_ol")
        z_y = sem("z_y")
        block = ctx.enter_context(nc.Block())

        @block.sync
        def _(sp):
            nc.sync.dma_start(con[:, :], d["con"]).then_inc(s_con, 16)
            nc.sync.dma_start(ident[:, :], d["ident"]).then_inc(s_con, 16)
            nc.sync.dma_start(iota[:, :], d["iota"]).then_inc(s_con, 16)
            nc.sync.dma_start(X[:, 0:4, :], d["x"][0:4].rearrange("b p s -> p b s")).then_inc(s_x, 16)
            nc.sync.dma_start(w0[:, :], d["w0"]).then_inc(s_w0, 16)
            nc.sync.dma_start(bias_f[:, :], d["b0"]).then_inc(s_w0, 16)
            nc.sync.dma_start(bo[:, :], d["bo"]).then_inc(s_w0, 16)
            nc.sync.dma_start(w0v[:, :], d["w0"][:, W0V:W0O]).then_inc(s_w0, 16)
            nc.sync.dma_start(conv[:, :], d["conv"][0].partition_broadcast(P)).then_inc(s_rest, 16)
            nc.sync.dma_start(br[:, :], d["br"][0].partition_broadcast(P)).then_inc(s_rest, 16)
            nc.sync.dma_start(wr[:, :, :], d["wr"].rearrange("a p j -> p a j")).then_inc(s_rest, 16)
            nc.sync.dma_start(topv[:, :, 0:P], d["context_lc"].rearrange("n p c -> p n c")).then_inc(s_topv, 16)

            def unit_step(u):
                if u >= STAGE:
                    sp.wait_ge(w_lo, u - STAGE + 1)
                nc.sync.dma_start(stage[:, u % STAGE, :], d["units"][u]).then_inc(s_unit[u % STAGE], 16)

            load = Stream(unit_step)
            sp.wait_ge(su_w0, 2)
            sp.wait_ge(su_rope, 4)
            sp.wait_ge(su_bias, 1)
            for b in range(B):
                if b >= 2:
                    sp.wait_ge(a0_pj, pj0(b - 2, 4) + 1)
                    sp.wait_ge(a0_m0, b - 1)
                nc.sync.dma_start(ctx_n[:, b % 2, :], d["context"][b]).then_inc(s_ctx[b % 2], 16)
                nc.sync.dma_start(mask0[:, b % 2, :], d["mask_row"][b].partition_broadcast(P)).then_inc(s_m0[b % 2], 16)
                if b == 1:
                    load.upto(2)
            for b in range(B):
                if b < 2:
                    sp.wait_ge(a0_m0, B + b - 1)
                else:
                    sp.wait_ge(x_done, XD_L0A + b - 1)
                nc.sync.dma_start(mask0[:, b % 2, :], d["mask_row"][b].partition_broadcast(P)).then_inc(s_m0[b % 2], 16)
            load.upto(U_L1F + 6)
            load.upto(U_L2X + 4)
            if XD_CX:
                sp.wait_ge(x_done, B)
            for k in range(KT):
                if k == 2:
                    load.upto(U_L2X + 10)
                if k >= 2:
                    sp.wait_ge(c_lo, k - 1)
                nc.sync.dma_start(chunk(k), d["contextT"][k]).then_inc(s_ctxT[k % 2], 16)
            load.upto(U_L3X)
            if XD_L3X:
                sp.wait_ge(x_done, XD_L3X)
            nc.sync.dma_start(mask3[:, :, :], d["mask3"].rearrange("b i j -> i b j")).then_inc(s_m3, 16)
            load.upto(N_UNITS)
            if XD_L3F:
                sp.wait_ge(x_done, XD_L3F)
            nc.sync.dma_start(perm_i[:, 0:512], d["perm_row"][0].partition_broadcast(P)).then_inc(s_perm, 16)
            nc.sync.dma_start(perm_i[:, 512:516], d["perm_col"]).then_inc(s_perm, 16)
            load.upto(N_UNITS)
            for b in range(B):
                sp.wait_ge(x_done, XD_END - B + b + 1)
                nc.sync.dma_start(out[b], X[:, b, :]).then_inc(s_out, 16)
            sp.wait_ge(s_out, 16 * B)


        @block.gpsimd
        def _(g):
            def lo_step(u):
                g.wait_ge(w_hi, u + 1)
                nc.gpsimd.tensor_tensor(ring_l[:, u % RING, :], stage[:, u % STAGE, :], f32(ring_h[:, u % RING, :]),
                                        ALU.subtract).then_inc(w_lo, 1)

            lo = Stream(lo_step)
            link(g, p_chain, nc.gpsimd.memset(mhalf[:, :], -0.5))
            ln_pool(g, LN_L0A[0])
            g.wait_ge(su_w0, 1)
            nc.gpsimd.tensor_tensor(w0l[:, :], w0[:, :], f32(w0h[:, :]), ALU.subtract).then_inc(su_w0, 1)
            g.wait_ge(su_wr, 1)
            nc.gpsimd.tensor_tensor(wrl[:, :, :], wr[:, :, :], f32(wrh[:, :, :]), ALU.subtract).then_inc(su_wr, 1)
            g.wait_ge(s_topv, 16)
            nc.gpsimd.tensor_scalar(topv[:, :, 0:P], topv[:, :, 0:P], -1.0, 0.0, ALU.mult, ALU.add).then_inc(a0_neg, 1)
            g.wait_ge(su_rope, 4)
            g.wait_ge(su_bias, 1)

            def low0(b):
                g.wait_ge(a0_in, b + 1)
                g.wait_ge(a0_x, b + 1)
                free0(g, b)
                nc.gpsimd.tensor_tensor(xnl[:, b % 2, :], xn[:, b % 4, :], f32(xnh[:, b % 2, :]), ALU.subtract).then_inc(a0_c, 1)

            low0(0)
            nc.gpsimd.memset(v0[:, :, :, :], 0.0)
            nc.gpsimd.memset(zeros_r[:, :].bitcast(F32), 0.0).then_inc(a0_one, 1)
            low0(1)
            for n in range(64):
                b, u = n // 8, n % 8
                if u == 6 and b + 2 < B:
                    low0(b + 2)
                g.wait_ge(a0_rc, n + 1)
                pb = by_tile(probs[:, n % 3, :])
                nc.gpsimd.tensor_tensor(pb, pb, rsums[:, n % 4, :].unsqueeze(2).to_broadcast((P, 4, P)), ALU.mult).then_inc(a0_pn, 1)
                if u == 0:
                    lo.upto(min(b, 2))
            for b in range(B):
                g.wait_ge(o0_gh, b + 1)
                if b >= 2:
                    g.wait_ge(o0_y, b - 1)
                nc.gpsimd.tensor_tensor(g0l[:, b % 2, :], g0[:, b % 2, :], f32(g0h[:, b % 2, :]),
                                        ALU.subtract).then_inc(o0_gl, 1)
            ln_pool(g, LN_L0F[0])
            lo.upto(U_L0F + RING)
            ln_pool(g, LN_L1X[0])
            g.wait_ge(x_var, 1)
            link(g, p_chain, nc.gpsimd.tensor_scalar(zs[:, 4, :], zs[:, 3, :], EPS, 1.0, ALU.add, ALU.mult))
            nc.gpsimd.tensor_tensor(zs[:, 5, :], zs[:, 4, :], mhalf[:, 0:2], ALU.pow).then_inc(x_rs, 1)
            ln_pool(g, LN_L1F[0])
            lo.upto(U_L2X + 4)
            lo.upto(U_L2X + 4)
            ln_pool(g, LN_L2X[0])
            lo.upto(U_L2X + 10)
            for k in range(KT):
                g.wait_ge(c_hi, k + 1)
                g.wait_ge(s_ctxT[k % 2], 16 * (k // 2 + 1))
                nc.gpsimd.tensor_tensor(cTl[:, k, :], chunk(k), f32(cTh[:, k, :]), ALU.subtract).then_inc(c_lo, 1)
            lo.upto(U_L2X + 12)
            for n in range(64):
                g.wait_ge(a2_rc, n + 1)
                pb = by_tile(xn[:, n % 4, :])
                nc.gpsimd.tensor_tensor(pb, pb, rsums[:, n % 4, :].unsqueeze(2).to_broadcast((P, 4, P)), ALU.mult).then_inc(a2_pn, 1)
                if n == 31:
                    lo.upto(U_L2X + 16)
                elif n == 32:
                    lo.upto(U_L2X + 20)
                elif n % 32 >= 16 and n % 4 == 0:
                    lo.upto(U_L2X + 12 + n // 32 * 8 + (n % 32 - 12) // 4)
            lo.upto(U_L2X + 25)
            ln_pool(g, LN_L2F[0])
            lo.upto(U_L3X)
            lo.upto(U_L3X + 6)
            ln_pool(g, LN_L3X[0])
            for h in range(8):
                for j in range(10):
                    i = 10 * h + j
                    g.wait_ge(a3_rp, i + 1)
                    half = (j - 2) // 4
                    dst = k3[:, j * HALF:(j + 1) * HALF] if j < 2 else q3[:, (j - 2) % 4, half * HALF:(half + 1) * HALF]
                    nc.gpsimd.tensor_tensor(dst, xn[:, j % 2, :], xn[:, 2 + j % 2, :], ALU.add).then_inc(a3_qk, 1)
                    if j == 5:
                        lo.upto(U_L3X + 10 * h + 10)
                for b in range(B):
                    n = B * h + b
                    g.wait_ge(a3_rc, n + 1)
                    pb = probs[:, n % 3, :].rearrange("p (r j) -> p r j", r=4)
                    nc.gpsimd.tensor_tensor(pb, pb, rsums[:, n % 4, :].unsqueeze(2).to_broadcast((P, 4, P)),
                                            ALU.mult).then_inc(a3_pn, 1)
                    if b >= 3:
                        lo.upto(U_L3X + 10 * h + 9 + b)
            lo.upto(N_UNITS)
            ln_pool(g, LN_L3F[0])
            for n in range(32):
                g.wait_ge(z_gh, n + 1)
                if n >= 2:
                    g.wait_ge(z_dp, n - 1)
                nc.gpsimd.tensor_tensor(gel_l[:, n % 2, :], gel[:, n % 2, :], f32(gel_h[:, n % 2, :]), ALU.subtract).then_inc(z_gl, 1)


        @block.scalar
        def _(a):
            def hi_step(u):
                a.wait_ge(s_unit[u % STAGE], 16 * (u // STAGE + 1))
                if u >= RING:
                    a.wait_ge(w_used, u - RING + 1)
                nc.scalar.activation(ring_h[:, u % RING, :], stage[:, u % STAGE, :], ACT.Copy).then_inc(w_hi, 1)

            hi = Stream(hi_step)
            nc.scalar.dma_start(pos_i[:, :], d["pos"][0].partition_broadcast(P)).then_inc(s_tab, 16)
            nc.scalar.dma_start(tabs[:, :, :, :], d["tabs"].rearrange("a k p j -> p a k j")).then_inc(s_tab, 16)
            nc.scalar.dma_start(X[:, 4:8, :], d["x"][4:8].rearrange("b p s -> p b s")).then_inc(s_x, 16)
            a.wait_ge(s_w0, 64)
            a.wait_ge(s_con, 48)
            nc.scalar.activation(w0h[:, :], w0[:, :], ACT.Copy).then_inc(su_w0, 1)
            nc.scalar.activation(bias_a[:, :].bitcast(F32R), bias_f[:, :], ACT.Identity,
                                 scale=con[0:2, C_RA:C_RA + 1]).then_inc(su_ba, 1)
            a.wait_ge(s_rest, 48)
            nc.scalar.activation(wrh[:, :, :], wr[:, :, :], ACT.Copy).then_inc(su_wr, 1)
            def inputs0(b):
                a.wait_ge(a0_x, b + 1)
                free0(a, b)
                nc.scalar.activation(xnh[:, b % 2, :], xn[:, b % 4, :], ACT.Copy).then_inc(a0_in, 1)

            def first_half(b, p):
                if p or b:
                    a.wait_ge(a0_pf, 4 * b + p)
                if p < 2:
                    a.wait_ge(a0_pj, pj0(b, p) + 1)
                    src, scale = bank0(b, p)[:], col(C_QA)
                else:
                    a.wait_ge(a0_kk, 2 * b + p - 1)
                    src, scale = kkeep, col(C_KA)
                nc.scalar.activation(halfA[:, :].bitcast(F32R), src, ACT.Identity, scale=scale).then_inc(a0_A, 1)

            def values0(b):
                a.wait_ge(a0_pj, pj0(b, 4) + 1)
                if b >= 2:
                    a.wait_ge(a0_pv, 8 * (b - 1))
                else:
                    a.wait_ge(a0_one, 1)
                nc.scalar.activation(v0[:, b % 2, :, :].rearrange("j p (h c) -> j p h c", c=72)[:, :, :, 0:8],
                                     bank0(b, 4)[:, 0:256].rearrange("j (p h e) -> j p h e", p=4, h=8), ACT.Copy).then_inc(a0_vc, 1)

            a.wait_ge(su_w0, 2)
            a.wait_ge(su_rope, 4)
            a.wait_ge(su_bias, 1)
            inputs0(0)
            for p in range(4):
                first_half(0, p)
            values0(0)
            inputs0(1)
            for n in range(66):
                b, u = n // 8, n % 8
                if n >= 2:
                    a.wait_ge(a0_t, n - 1)
                    if n >= 5:
                        a.wait_ge(a0_pv, n - 4)
                    nc.scalar.activation(probsT[:, (n - 2) % 3, :], bank[3 + n % 2][:], ACT.Copy).then_inc(a0_pt, 1)
                if n < 64:
                    a.wait_ge(a0_mx, n + 1)
                    if n >= 3:
                        a.wait_ge(a0_t, n - 2)
                    for p in range(4):
                        ins = nc.scalar.activation(probs[:, n % 3, p * P:(p + 1) * P], bank[n % 3][:, p * P:(p + 1) * P],
                                                   ACT.Exp, bias=nbias[:, n % 4, p:p + 1], scale=-1.0,
                                                   accum_out=psums[:, n % 4, p:p + 1])
                    ins.then_inc(a0_e, 1)
                if b < B - 1 and u < 4:
                    first_half(b + 1, u)
                if b < B - 1 and u == 4:
                    values0(b + 1)
                if u == 5 and b + 2 < B:
                    inputs0(b + 2)
                if u == 7:
                    hi.upto(min(b + 1, 2))
            a.wait_ge(a0_pv, 64)
            a.wait_ge(a0_ot, B)
            for b in range(B):
                a.wait_ge(a0_ot, b + 1)
                if b >= 2:
                    a.wait_ge(o0_y, b - 1)
                    a.wait_ge(o0_gl, b - 1)
                link(a, a_chain, nc.scalar.activation(g0[:, b % 2, :], o0T[:, b, :], ACT.Gelu))
                nc.scalar.activation(g0h[:, b % 2, :], g0[:, b % 2, :], ACT.Copy).then_inc(o0_gh, 1)
            ln_act(a, LN_L0F[1], xTh_a)
            hi.upto(U_L0F + RING)
            router_act(a, 0)
            for b in range(B):
                a.wait_ge(x_cf, b + 1)
                if b >= 1:
                    a.wait_ge(x_sum, b)
                for i in range(2):
                    for q in range(4):
                        ins = nc.scalar.activation(junk[:, i, q, :], cf[:, b % 2, i, q * P:(q + 1) * P], ACT.Copy,
                                                   accum_out=rows[:, 1, i, b, q + 1:q + 2])
                ins.then_inc(x_sum, 1)
            a.wait_ge(x_arg, 1)
            nc.scalar.activation(zz[:, :, :], z[:, :, :], ACT.Exp, scale=-1.0).then_inc(x_e, 1)
            hi.upto(U_L1F + 6)
            ln_act(a, LN_L1F[1], xTh_a)
            router_act(a, 1)
            hi.upto(U_L2X + 4)
            def context_hi(k):
                if XD_CX:
                    a.wait_ge(x_done, XD_CX)
                a.wait_ge(s_ctxT[k % 2], 16 * (k // 2 + 1))
                nc.scalar.activation(cTh[:, k, :], chunk(k), ACT.Copy).then_inc(c_hi, 1)

            def copied2(s, j):
                i = pj2(s, j)
                a.wait_ge(a2_pj, i + 1)
                half = j if j < 2 else (j - 2) // 4
                c = slice(half * HALF, (half + 1) * HALF)
                if j < 2:
                    nc.scalar.activation(k2[:, c], bank[6 + i % 2][:], ACT.Copy).then_inc(a2_pf, 1)
                else:
                    nc.scalar.activation(q2[:, (j - 2) % 4, c], bank[6 + i % 2][:], ACT.Copy, scale=-0.25).then_inc(a2_pf, 1)

            hi.upto(U_L2X + 4)
            for s in range(2):
                if s == 0:
                    ln_act(a, LN_L2X[1], xTh_b)
                    for j in range(2, 10):
                        copied2(0, j)
                        if j == 2:
                            hi.upto(U_L2X + 10)
                        if j < 2 + KT:
                            context_hi(j - 2)
                    copied2(0, 0)
                    copied2(0, 1)
                    a.wait_ge(a2_one, 1)
                    for half in range(2):
                        a.wait_ge(a2_pj, 11 + half)
                        nc.scalar.activation(v2[:, 4 * half:4 * half + 4, :, 0:16],
                                             bank[6 + half][:].rearrange("p (b h e) -> p b h e", b=4, h=8), ACT.Copy).then_inc(a2_pf, 1)
                    hi.upto(U_L2X + 12)
                else:
                    for j in range(2):
                        copied2(s, j)
                    hi.upto(U_L2X + 20)
                    for j in range(2, 10):
                        copied2(s, j)
                for l in range(37):
                    n = 32 * s + l
                    m = n - 3
                    if 3 <= l < 35:
                        a.wait_ge(a2_t, m + 1)
                        if m >= 3:
                            a.wait_ge(a2_pv, m - 2)
                        nc.scalar.activation(probsT[:, m % 3, :], bank[3 + m % 2][:], ACT.Copy).then_inc(a2_pt, 1)
                    if l < 32:
                        a.wait_ge(a2_mx, n + 1)
                        if n >= 4:
                            a.wait_ge(a2_t, n - 3)
                        for r in range(4):
                            c = slice(r * P, (r + 1) * P)
                            ins = nc.scalar.activation(xn[:, n % 4, c], bank[n % 3][:, c], ACT.Exp,
                                                       bias=nbias[:, n % 4, r:r + 1], scale=-1.0,
                                                       accum_out=psums[:, n % 4, r:r + 1])
                        ins.then_inc(a2_e, 1)
                    if l >= 8 and l % 4 == 0:
                        m = 8 * s + (l - 8) // 4
                        a.wait_ge(a2_pv, 4 * m + 4)
                        if m >= 2:
                            a.wait_ge(a2_y, m - 1)
                        nc.scalar.activation(onT_h[:, m % 2, :], bank[5 + m % 2][:], ACT.Copy).then_inc(a2_oh, 1)
                    if l >= 16 and l % 4 == 0 and l < 32:
                        hi.upto(U_L2X + 12 + 8 * s + (l - 12) // 4)
                hi.upto(U_L2X + (16 if s == 0 else 25))
            def high2(n, group, i):
                a.wait_ge(g_h, n + 1)
                if i:
                    a.wait_ge(g_y, B * i)
                f, half = n // 2 - group[0], n % 2
                nc.scalar.activation(hid_h[:, f, half * HALF:(half + 1) * HALF], hid[:, n % 2, :], ACT.Copy).then_inc(g_hh, 1)

            ln_act(a, LN_L2F[1], xTh_b)
            u = U_L2F
            hi.upto(u + RING)
            for i, group in enumerate(FGROUPS):
                for f in group:
                    for half in range(2):
                        n = 2 * f + half
                        a.wait_ge(g_p, 2 * n + 1)
                        if n >= 2:
                            a.wait_ge(g_h, n - 1)
                        nc.scalar.activation(silu[:, n % 2, :], bank[n % 2][:], ACT.Silu).then_inc(g_s, 1)
                        if n > 2 * group[0]:
                            high2(n - 1, group, i)
                        if half == 0:
                            hi.upto(min(u + RING, U_L3X))
                    u += 2
                high2(2 * group[-1] + 1, group, i)
                hi.upto(min(u + RING, U_L3X))
                u += len(group)
            hi.upto(U_L3X + 6)
            ln_act(a, LN_L3X[1], xTh_b)

            def values3(h, half):
                a.wait_ge(a3_vt, 2 * h + half + 1)
                nc.scalar.activation(v3[:, 4 * half:4 * half + 4, :], bank[6 + half][:].rearrange("p (b e) -> p b e", b=4),
                                     ACT.Copy).then_inc(a3_v, 1)

            for h in range(8):
                hi.upto(U_L3X + 10 * h + 10)
                for l in range(10):
                    n = B * h + l
                    if l == 2:
                        values3(h, 1)
                    m = n - 2
                    if l >= 2:
                        a.wait_ge(a3_t, m + 1)
                        if m >= 3:
                            a.wait_ge(a3_pv, m - 2)
                        nc.scalar.activation(probsT[:, m % 3, :], bank[2 + m % 2][:], ACT.Copy).then_inc(a3_pt, 1)
                    if l < B:
                        a.wait_ge(a3_mx, n + 1)
                        if n >= 3:
                            a.wait_ge(a3_t, n - 2)
                        for r in range(4):
                            c = slice(r * P, (r + 1) * P)
                            ins = nc.scalar.activation(probs[:, n % 3, c], bank[n % 2][:, c], ACT.Exp,
                                                       bias=nbias[:, n % 4, r:r + 1], scale=-1.0,
                                                       accum_out=psums[:, n % 4, r:r + 1])
                        ins.then_inc(a3_e, 1)
                    if l < 2:
                        a.wait_ge(a3_pj, 12 * h + 11 + l)
                        nc.scalar.activation(vT[:, l, :], bank[6 + l][:], ACT.Copy).then_inc(a3_vc, 1)
                    if l == 1:
                        values3(h, 0)
                    if l >= 2:
                        a.wait_ge(a3_pv, m + 1)
                        if m >= 2:
                            a.wait_ge(a3_y, m - 1)
                        nc.scalar.activation(o3h[:, m % 2, :], bank[4][:], ACT.Copy).then_inc(a3_oh, 1)
                    if 2 <= l <= 6:
                        hi.upto(U_L3X + 10 * h + 10 + l)
            hi.upto(N_UNITS)
            ln_act(a, LN_L3F[1], xTh_b)

            def tile_hi(n):
                a.wait_ge(z_t, n + 1)
                c = slice(n % 2 * HALF, (n % 2 + 1) * HALF)
                nc.scalar.activation(tTh[:, n // 2, c], bank[n % 4][:], ACT.Copy).then_inc(z_th, 1)

            for n in range(3):
                tile_hi(n)

            def last_hi(o):
                a.wait_ge(z_dp, 4 * o + 4)
                c = slice(o % 2 * HALF, (o % 2 + 1) * HALF)
                nc.scalar.activation(t2h[:, o // 2, c], bank[6 + o % 2][:], ACT.Copy).then_inc(z_oh, 1)

            for n in range(32):
                a.wait_ge(z_up, n + 1)
                if n >= 2:
                    a.wait_ge(z_gl, n - 1)
                nc.scalar.activation(gel[:, n % 2, :], bank[4 + n % 2][:], ACT.Gelu).then_inc(z_g, 1)
                if n < 5:
                    tile_hi(n + 3)
                if n % 4 == 2 and n > 4:
                    last_hi(n // 4 - 1)
            last_hi(7)


        @block.vector
        def _(v):
            nc.vector.memset(ones_r[:, :].bitcast(F32), 1.0).then_inc(su_one, 1)
            v.wait_ge(s_con, 48)
            v.wait_ge(s_tab, 32)
            for k in range(KT):
                ins = nc.vector.tensor_scalar(hot[:, k, :], pos_i[:, :], col(C_IOTA + k), None, ALU.is_equal)
            ins.then_inc(su_hot, 1)
            v.wait_ge(s_x, 32)
            for b in range(B + 2):
                ln_step(v, LN_L0A[0], b)
            for b in range(4):
                ln_norm(v, LN_L0A[0], b, xn[:, b, :]).then_inc(a0_x, 1)
            v.wait_ge(su_ba, 1)
            nc.vector.scalar_tensor_tensor(biasr[:, :], bias_f[:, :], con[0:2, C_RM:C_RM + 1], bias_a[:, :],
                                           ALU.mult, ALU.add).then_inc(su_bias, 1)
            for i in range(4):
                v.wait_ge(su_rope, i + 1)
                nc.vector.tensor_copy((cosT, sinT)[i // 2][:, i % 2 * HALF:(i % 2 + 1) * HALF], bank[i][:]).then_inc(su_rc, 1)

            v.wait_ge(a0_neg, 1)
            link(v, v_chain, nc.vector.memset(topv[:, :, P:P + 4], DUMMY))

            def tiles_of(k):
                return range(k // ROUNDS * 4, k // ROUNDS * 4 + 4)

            def find(k):
                if k:
                    v.wait_ge(a0_tk, k)
                for i in tiles_of(k):
                    ins = nc.vector.max(top8[:, i % 4, :], topv[:, i, :])
                ins.then_inc(a0_tf, 1)

            def take(k):
                v.wait_ge(a0_tf, k + 1)
                for i in tiles_of(k):
                    ins = nc.vector.match_replace(topv[:, i, :], top8[:, i % 4, :], topv[:, i, :], TAKEN)
                ins.then_inc(a0_tk, 1)

            v.wait_ge(su_w0, 2)

            def mask_rows(b):
                v.wait_ge(s_m0[b % 2], 16 * (b // 2 + 1))
                if b >= 1:
                    v.wait_ge(a0_kk, 2 * b)
                nc.vector.tensor_scalar(keep[:, :], mask0[:, b % 2, :], 0.0, None, ALU.is_gt)
                if b >= 2:
                    v.wait_ge(a0_s, 8 * (b - 1))
                nc.vector.tensor_scalar(mrow[:, b % 2, :], mask0[:, b % 2, :], 0.0, col(C_BIG), ALU.is_le,
                                        ALU.mult).then_inc(a0_m0, 1)

            def masked_keys(b, p):
                v.wait_ge(a0_pj, pj0(b, p) + 1)
                v.wait_ge(a0_m0, b + 1)
                v.wait_ge(a0_pf, 4 * b + p)
                nc.vector.tensor_tensor(kkeep, bank0(b, p)[:], keep[:, :], ALU.mult).then_inc(a0_kk, 1)

            def second_half(b, p):
                if b >= 2:
                    v.wait_ge(a0_s, 8 * (b - 1))
                v.wait_ge(a0_A, 4 * b + p + 1)
                src, dst, scale = (bank0(b, p)[:], q0[:, b % 2, p, :], C_QM) if p < 2 else (kkeep, k0[:, b % 2, p - 2, :], C_KM)
                nc.vector.scalar_tensor_tensor(dst, src, col(scale), halfA[:, :], ALU.mult, ALU.add).then_inc(a0_pf, 1)

            def output0(b):
                v.wait_ge(a0_pv, 8 * b + 8)
                nc.vector.tensor_copy(o0T[:, b, :], bank[5][0:64, :]).then_inc(a0_ot, 1)

            mask_rows(0)
            for p in range(4):
                if p >= 2:
                    masked_keys(0, p)
                second_half(0, p)
            for n in range(64):
                b, u = n // 8, n % 8
                v.wait_ge(a0_s, n + 1)
                if n >= 4:
                    v.wait_ge(a0_e, n - 3)
                nc.vector.tensor_reduce(nbias[:, n % 4, :], by_tile(bank[n % 3][:]), AX.X, ALU.min).then_inc(a0_mx, 1)
                if b >= 1 and u == 2:
                    output0(b - 1)
                if n < 56:
                    find(n)
                if b < B - 1 and 1 <= u <= 4:
                    second_half(b + 1, u - 1)
                if b < B - 1 and u in (2, 3):
                    masked_keys(b + 1, u)
                if b < B - 1 and u == 0:
                    mask_rows(b + 1)
                v.wait_ge(a0_e, n + 1)
                if n >= 4:
                    v.wait_ge(a0_pn, n - 3)
                nc.vector.reciprocal(rsums[:, n % 4, :], psums[:, n % 4, :]).then_inc(a0_rc, 1)
                if n < 56:
                    take(n)
                if u == 7 and b + 4 < B:
                    v.wait_ge(a0_c, b + 1)
                    ln_norm(v, LN_L0A[0], b + 4, xn[:, b % 4, :]).then_inc(a0_x, 1)
            v.wait_ge(a0_tk, 56)
            nc.vector.tensor_scalar(crucial[:, :, ::-1], topv[:, :, 0:P], TAKEN, None, ALU.not_equal)
            output0(B - 1)
            for b in range(B):
                v.wait_ge(o0_y, b + 1)
                v.wait_ge(s_m0[b % 2], 16 * (B // 2 + b // 2 + 1))
                link(v, v_chain, nc.vector.scalar_tensor_tensor(upd[:, b % 2, :], bank[b % 2][:], bo[:, 0:1],
                                                                mask0[:, b % 2, :], ALU.add, ALU.mult))
                nc.vector.tensor_tensor(X[:, b, :], X[:, b, :], upd[:, b % 2, :], ALU.add).then_inc(x_done, 1)
                ln_step(v, LN_L0F[0], b)
            ln_step(v, LN_L0F[0], B)
            ln_step(v, LN_L0F[0], B + 1)
            v.wait_ge(s_rest, 48)
            ln_dve(v, *LN_L0F, xTh_a, xTl_a)
            router_dve(v, 0, LN_L1X[0])
            nc.vector.memset(ones_f[:, :], 1.0)
            nc.vector.memset(rows[:, :, :, :, :], 0.0)
            for b in range(B):
                ln_norm(v, LN_L1X[0], b, xnf[:, b, :]).then_inc(x_x, 1)
            for b in range(B):
                v.wait_ge(x_t, b + 1)
                if b >= 2:
                    v.wait_ge(x_sum, b - 1)
                    v.wait_ge(x_mx, b - 1)
                keep01 = crucial[:, 4 * b:4 * b + 4, :].rearrange("p k t -> p (k t)")
                link(v, v_chain, nc.vector.tensor_tensor(cf[:, b % 2, 0, :], bank[b % 2][:], keep01, ALU.mult))
                nc.vector.tensor_tensor(cf[:, b % 2, 1, :], bank[b % 2][:], cf[:, b % 2, 0, :], ALU.subtract).then_inc(x_cf, 1)
                v.wait_ge(x_cf, b + 1)
                nc.vector.tensor_reduce(rows[:, 0, 0, b, 1:5], by_tile(cf[:, b % 2, 0, :]), AX.X, ALU.max)
                nc.vector.tensor_reduce(rows[:, 0, 1, b, 1:5], by_tile(cf[:, b % 2, 1, :]), AX.X, ALU.max).then_inc(x_mx, 1)
            v.wait_ge(x_sum, B)
            for i in range(2):
                ins = nc.vector.tensor_scalar(rows[:, 1, i, :, 1:5], rows[:, 1, i, :, 1:5], 1.0 / (N_CRUCIAL, N_REST)[i], None, ALU.mult)
            ins.then_inc(x_rows, 1)
            v.wait_ge(x_z, 1)
            link(v, v_chain, nc.vector.tensor_copy(z[:, :, :], bank[2][:, 0:64].rearrange("p (i n) -> p i n", i=2)))
            link(v, v_chain, nc.vector.tensor_reduce(zs[:, 0, :], z[:, :, :], AX.X, ALU.add))
            nc.vector.tensor_scalar(zs[:, 1, :], zs[:, 0, :], 1.0 / (B * D), None, ALU.mult).then_inc(x_zs, 1)
            v.wait_ge(x_tot, 1)
            link(v, v_chain, nc.vector.tensor_copy(zs[:, 6, :], bank[3][:, 0:2]))
            for i in range(2):
                ins = nc.vector.tensor_scalar(z[:, i, :], z[:, i, :], zs[:, 6, i:i + 1], None, ALU.subtract)
            link(v, v_chain, ins)
            link(v, v_chain, nc.vector.tensor_tensor(zz[:, :, :], z[:, :, :], z[:, :, :], ALU.mult))
            link(v, v_chain, nc.vector.tensor_reduce(zs[:, 0, :], zz[:, :, :], AX.X, ALU.add))
            nc.vector.tensor_scalar(zs[:, 2, :], zs[:, 0, :], 1.0 / (B * D), None, ALU.mult).then_inc(x_zs, 1)
            v.wait_ge(x_tot, 2)
            nc.vector.tensor_copy(zs[:, 3, :], bank[4][:, 0:2]).then_inc(x_var, 1)
            v.wait_ge(x_rs, 1)
            link(v, v_chain, nc.vector.tensor_scalar(zs[:, 7, :], zs[:, 5, :], conv[:, 14:15], None, ALU.mult))
            for i in range(2):
                ins = nc.vector.tensor_scalar(z[:, i, :], z[:, i, :], zs[:, 7, i:i + 1], conv[:, 15:16], ALU.mult, ALU.add)
            link(v, v_chain, ins)
            nc.vector.tensor_scalar(z[:, :, :], z[:, :, :], 0.0, None, ALU.max).then_inc(x_arg, 1)
            v.wait_ge(x_e, 1)
            link(v, v_chain, nc.vector.tensor_scalar(zz[:, :, :], zz[:, :, :], 1.0, None, ALU.add))
            link(v, v_chain, nc.vector.reciprocal(gains[:, 0:2, :], zz[:, :, :]))
            link(v, v_chain, nc.vector.tensor_tensor(gains[:, 2, :], gains[:, 0, :], gains[:, 1, :], ALU.subtract))

            def gains_by_channel(b):
                if b >= 2:
                    v.wait_ge(x_gp, b - 1)
                for q in range(4):
                    i = 4 * b + q
                    ins = nc.vector.tensor_scalar(gT[:, b % 2, q * P:(q + 1) * P], crucial[:, i, :], gains[:, 2, i:i + 1],
                                                  gains[:, 1, i:i + 1], ALU.mult, ALU.add)
                ins.then_inc(x_gt, 1)

            gains_by_channel(0)
            for b in range(B):
                if b + 1 < B:
                    gains_by_channel(b + 1)
                v.wait_ge(x_gp, b + 1)
                link(v, v_chain, nc.vector.tensor_tensor(tmpx[:, b % 2, :], bank[b % 2][:], xnf[:, b, :], ALU.mult))
                nc.vector.tensor_tensor(X[:, b, :], X[:, b, :], tmpx[:, b % 2, :], ALU.add).then_inc(x_done, 1)
                ln_step(v, LN_L1F[0], b)
            ln_step(v, LN_L1F[0], B)
            ln_step(v, LN_L1F[0], B + 1)
            ln_dve(v, *LN_L1F, xTh_a, xTl_a)
            router_dve(v, 1, LN_L2X[0])
            nc.vector.memset(v2[:, :, :, :], 0.0).then_inc(a2_one, 1)

            ln_dve(v, *LN_L2X, xTh_b, xTl_b)
            for s in range(2):
                for l in range(42):
                    n = 32 * s + l
                    if 10 <= l < 39 and l % 4 == 2:
                        b = (l - 10) // 4
                        v.wait_ge(a2_y, 8 * s + b + 1)
                        if s:
                            v.wait_ge(x_done, XD_L2X + B)
                        nc.vector.tensor_tensor(X[:, b, :], X[:, b, :], bank[7][:], ALU.add).then_inc(x_done, 1)
                        if s:
                            ln_step(v, LN_L2F[0], b)
                    if 1 <= l < 33:
                        m = n - 1
                        v.wait_ge(a2_e, m + 1)
                        if m >= 4:
                            v.wait_ge(a2_pn, m - 3)
                        nc.vector.reciprocal(rsums[:, m % 4, :], psums[:, m % 4, :]).then_inc(a2_rc, 1)
                    if l < 32:
                        v.wait_ge(a2_s, n + 1)
                        nc.vector.tensor_reduce(nbias[:, n % 4, :], by_tile(bank[n % 3][:]), AX.X, ALU.min).then_inc(a2_mx, 1)
                    if 9 <= l < 38 and l % 4 == 1:
                        m = 8 * s + (l - 9) // 4
                        v.wait_ge(a2_oh, m + 1)
                        nc.vector.tensor_tensor(onT_l[:, m % 2, :], bank[5 + m % 2][:], f32(onT_h[:, m % 2, :]),
                                                ALU.subtract).then_inc(a2_ol, 1)
            ln_step(v, LN_L2F[0], B)
            ln_step(v, LN_L2F[0], B + 1)
            def low2(n, group):
                v.wait_ge(g_hh, n + 1)
                f, half = n // 2 - group[0], n % 2
                c = slice(half * HALF, (half + 1) * HALF)
                nc.vector.tensor_tensor(hid_l[:, f, c], hid[:, n % 2, :], f32(hid_h[:, f, c]), ALU.subtract).then_inc(g_hl, 1)

            ln_dve(v, *LN_L2F, xTh_b, xTl_b)
            for i, group in enumerate(FGROUPS):
                for n in range(2 * group[0], 2 * group[-1] + 2):
                    v.wait_ge(g_s, n + 1)
                    v.wait_ge(g_p, 2 * n + 2)
                    if n >= 2:
                        v.wait_ge(g_hl, n - 1)
                    nc.vector.tensor_tensor(hid[:, n % 2, :], silu[:, n % 2, :], bank[2 + n % 2][:], ALU.mult).then_inc(g_h, 1)
                    if n > 2 * group[0]:
                        low2(n - 1, group)
                low2(2 * group[-1] + 1, group)
                for b in range(B):
                    v.wait_ge(g_y, B * i + b + 1)
                    if i:
                        v.wait_ge(x_done, XD_L2F + B * i)
                    nc.vector.tensor_tensor(X[:, b, :], X[:, b, :], bank[4 + b % 2][:], ALU.add).then_inc(x_done, 1)
                    if i == len(FGROUPS) - 1:
                        ln_step(v, LN_L3X[0], b)
            ln_step(v, LN_L3X[0], B)
            ln_step(v, LN_L3X[0], B + 1)
            nc.vector.memset(big[:, :], BIG)
            v.wait_ge(s_m3, 16)
            nc.vector.tensor_scalar(mask3[:, :, :], mask3[:, :, :], 0.0, None, ALU.is_equal).then_inc(a3_m, 1)
            v.wait_ge(a3_m, 1)
            ln_dve(v, *LN_L3X, xTh_b, xTl_b)
            v.wait_ge(ln_t, B * (LN_L3X[1] + 1))
            SCALE3 = -1.0 / float(np.sqrt(np.float32(P)))

            def rope(h, j):
                i = 10 * h + j
                half = j if j < 2 else (j - 2) // 4
                c = slice(half * HALF, (half + 1) * HALF)
                v.wait_ge(a3_pj, 12 * h + j + 1)
                if i >= 2:
                    v.wait_ge(a3_qk, i - 1)
                src, swapped = bank[6 + j % 2], ((slice(0, 64), slice(64, P)), (slice(64, P), slice(0, 64)))
                if j < 2:
                    nc.vector.scalar_tensor_tensor(xn[:, j % 2, :], src[:], SCALE3, cosT[:, c], ALU.mult, ALU.mult)
                    for to, fro in swapped:
                        ins = nc.vector.scalar_tensor_tensor(xn[to, 2 + j % 2, :], src[fro, :], SCALE3, sinT[to, c],
                                                             ALU.mult, ALU.mult)
                else:
                    nc.vector.tensor_tensor(xn[:, j % 2, :], src[:], cosT[:, c], ALU.mult)
                    for to, fro in swapped:
                        ins = nc.vector.tensor_tensor(xn[to, 2 + j % 2, :], src[fro, :], sinT[to, c], ALU.mult)
                ins.then_inc(a3_rp, 1)

            for h in range(8):
                for j in range(2 if h else 0, 10):
                    rope(h, j)
                for l in range(11):
                    n = B * h + l
                    if 1 <= l <= B:
                        m = n - 1
                        v.wait_ge(a3_e, m + 1)
                        if m >= 4:
                            v.wait_ge(a3_pn, m - 3)
                        nc.vector.reciprocal(rsums[:, m % 4, :], psums[:, m % 4, :]).then_inc(a3_rc, 1)
                    if l < B:
                        v.wait_ge(a3_s, n + 1)
                        if n >= 4:
                            v.wait_ge(a3_e, n - 3)
                        s4 = by_tile(bank[n % 2][:])
                        link(v, v_chain, nc.vector.copy_predicated(s4, mask3[:, l, :].unsqueeze(1).to_broadcast((P, 4, P)),
                                                                   big[:, :].unsqueeze(1).to_broadcast((P, 4, P))))
                        nc.vector.tensor_reduce(nbias[:, n % 4, :], s4, AX.X, ALU.min).then_inc(a3_mx, 1)
                    if l == B + 1 and h < 7:
                        rope(h + 1, 0)
                    if 2 <= l < B + 2:
                        m = n - 2
                        v.wait_ge(a3_oh, m + 1)
                        nc.vector.tensor_tensor(o3l[:, m % 2, :], bank[4][:], f32(o3h[:, m % 2, :]), ALU.subtract).then_inc(a3_ol, 1)
                    if l == B + 2 and h < 7:
                        rope(h + 1, 1)
                    if l >= 3:
                        m = n - 3
                        v.wait_ge(a3_y, m + 1)
                        if h:
                            v.wait_ge(x_done, XD_L3X + B * h)
                        nc.vector.tensor_tensor(X[:, l - 3, :], X[:, l - 3, :], bank[5][:], ALU.add).then_inc(x_done, 1)
                        if h == 7:
                            ln_step(v, LN_L3F[0], l - 3)
            ln_step(v, LN_L3F[0], B)
            ln_step(v, LN_L3F[0], B + 1)
            ln_dve(v, *LN_L3F, xTh_b, xTl_b)
            v.wait_ge(s_perm, 32)
            nc.vector.tensor_copy(perm_f[:, 0:516], perm_i[:, 0:516]).then_inc(z_pf, 1)
            v.wait_ge(z_pf, 1)
            for k in range(KT):
                nc.vector.tensor_scalar(pick[:, k, :], perm_f[:, 0:512], col(C_IOTA + k), None, ALU.is_equal).then_inc(z_pick, 1)
            def tile_lo(n):
                v.wait_ge(z_th, n + 1)
                c = slice(n % 2 * HALF, (n % 2 + 1) * HALF)
                nc.vector.tensor_tensor(tTl[:, n // 2, c], bank[n % 4][:], f32(tTh[:, n // 2, c]), ALU.subtract).then_inc(z_tl, 1)

            for n in range(3):
                tile_lo(n)
            nc.vector.memset(down_h[:, :, :].bitcast(F32), 0.0)
            nc.vector.memset(down_l[:, :, :].bitcast(F32), 0.0).then_inc(z_dz, 1)
            v.wait_ge(z_dz, 1)
            v.wait_ge(w_lo, U_L3F + 2)
            for to, fro in ((down_h, slot(U_L3F + 1)[0]), (down_l, slot(U_L3F + 1)[1])):
                for gr in range(4):
                    dst = to[:, :, :].rearrange("p (t g) c -> p t g c", g=4)[:, :, gr, 32 * gr:32 * gr + 32]
                    ins = nc.vector.tensor_copy(dst, f32(fro).rearrange("p (t g c) -> p t g c", t=4, g=4)[:, :, gr, :])
            ins.then_inc(z_dn, 1)
            for k in range(KT):
                ins = nc.vector.tensor_scalar(put[:, k, :], iota[:, :], perm_f[:, 512 + k:513 + k], None, ALU.is_equal)
            ins.then_inc(z_pick, 1)

            def last_lo(o):
                v.wait_ge(z_oh, o + 1)
                c = slice(o % 2 * HALF, (o % 2 + 1) * HALF)
                nc.vector.tensor_tensor(t2l[:, o // 2, c], bank[6 + o % 2][:], f32(t2h[:, o // 2, c]), ALU.subtract).then_inc(z_ol, 1)

            for n in range(32):
                v.wait_ge(z_g, n + 1)
                if n >= 2:
                    v.wait_ge(z_dp, n - 1)
                nc.vector.tensor_copy(gel_h[:, n % 2, :], gel[:, n % 2, :]).then_inc(z_gh, 1)
                if n < 5:
                    tile_lo(n + 3)
                if n % 4 == 3 and n > 4:
                    last_lo(n // 4 - 1)
            last_lo(7)
            for b in range(B):
                v.wait_ge(z_y, b + 1)
                nc.vector.tensor_tensor(X[:, b, :], X[:, b, :], bank[b % 4][:], ALU.add).then_inc(x_done, 1)


        @block.tensor
        def _(t):
            used = [0]

            def unit(u):
                t.wait_ge(w_lo, u + 1)
                return slot(u)

            t.wait_ge(s_tab, 32)
            t.wait_ge(s_con, 48)
            t.wait_ge(su_hot, 1)
            for i in range(4):
                for k in range(KT):
                    ins = nc.tensor.matmul(bank[i][:], tabs[:, i // 2, k, :], hot[:, k, i % 2 * HALF:(i % 2 + 1) * HALF],
                                           start=k == 0, stop=k == KT - 1)
                ins.then_inc(su_rope, 1)
            def projection0(b, p):
                if pj0(b, p) >= 2:
                    used0(t, pj0(b, p) - 2)
                dst = bank0(b, p)
                if p < 4:
                    c = slice((W0Q, W0K)[p // 2] + p % 2 * P, (W0Q, W0K)[p // 2] + p % 2 * P + P)
                    mm3(dst[:], w0h[:, c], w0l[:, c], xnh[:, b % 2, :], xnl[:, b % 2, :], True, False)
                    nc.tensor.matmul(dst[:], biasr[:, c], ones_r[0:2, :], start=False, stop=True).then_inc(a0_pj, 1)
                    return
                t.wait_ge(s_ctx[b % 2], 16 * (b // 2 + 1))
                nc.tensor.matmul(dst[:, 0:256].rearrange("j (p e) -> j p e", p=4), ones_r[0:2, 0:P],
                                 biasr[:, W0V:W0V + 64].unsqueeze(1).to_broadcast((2, 4, 64)), start=True, stop=False)
                for q in range(4):
                    ins = nc.tensor.matmul(dst[:, q * 64:(q + 1) * 64], ctx_n[:, b % 2, q * P:(q + 1) * P], w0v[:, :],
                                           start=False, stop=q == 3)
                ins.then_inc(a0_pj, 1)

            def scores0(n, p):
                b, s, rows32, c = n // 8, n % 8 // 4, slice(32 * (n % 4), 32 * (n % 4) + 32), slice(p * P, (p + 1) * P)
                return nc.tensor.matmul(bank[n % 3][:, c], q0[rows32, b % 2, s, c], k0[rows32, b % 2, s, c], start=False, stop=p == 3)

            t.wait_ge(su_w0, 2)
            t.wait_ge(su_bias, 1)
            t.wait_ge(su_rc, 4)
            t.wait_ge(a0_one, 1)
            t.wait_ge(a0_c, 1)
            for p in range(5):
                projection0(0, p)
            for n in range(67):
                b, u, m = n // 8, n % 8, n - 3
                if n < 64:
                    two = slice(32 * (u % 4), 32 * (u % 4) + 2)
                    if u == 0:
                        t.wait_ge(a0_pf, 4 * b + 4)
                        t.wait_ge(a0_vc, b + 1)
                        t.wait_ge(a0_m0, b + 1)
                    if n >= 3:
                        t.wait_ge(a0_e, n - 2)
                    nc.tensor.matmul(bank[n % 3][:], ones_r[two, 0:P], mrow[two, b % 2, :], start=True, stop=False)
                h = m % 8
                if n < 64 and h == 0:
                    for p in range(4):
                        ins = scores0(n, p)
                    ins.then_inc(a0_s, 1)
                if m >= 0:
                    t.wait_ge(a0_pt, m + 1)
                    if h == 0:
                        if m:
                            t.wait_ge(a0_ot, m // 8)
                        nc.tensor.matmul(bank[5][0:64, :], zeros_r[:, :], ones_r[0:2, :], start=True, stop=False)
                for p in range(4):
                    c = slice(p * P, (p + 1) * P)
                    if m >= 0:
                        pv = nc.tensor.matmul(bank[5][0:64, c], v0[:, m // 8 % 2, p, 64 * h:64 * h + 64], probsT[:, m % 3, c],
                                              start=False, stop=h == 7 and p == 3)
                    if n < 64 and h:
                        ins = scores0(n, p)
                if m >= 0:
                    pv.then_inc(a0_pv, 1)
                if n < 64 and h:
                    ins.then_inc(a0_s, 1)
                m = n - 2
                if 0 <= m < 64:
                    t.wait_ge(a0_pn, m + 1)
                    if m >= 2:
                        t.wait_ge(a0_pt, m - 1)
                    for p in range(4):
                        c = slice(p * P, (p + 1) * P)
                        ins = nc.tensor.transpose(bank[3 + m % 2][:, c], probs[:, m % 3, c], ident[:, :])
                    ins.then_inc(a0_t, 1)
                if b < B - 1 and u <= 4:
                    if u == 0:
                        t.wait_ge(a0_c, b + 2)
                    projection0(b + 1, u)
            for b in range(B):
                t.wait_ge(o0_gl, b + 1)
                if b >= 2:
                    t.wait_ge(x_done, XD_L0A + b - 1)
                mm3(bank[b % 2][:], w0h[0:64, W0O:W0O + P], w0l[0:64, W0O:W0O + P], g0h[:, b % 2, :], g0l[:, b % 2, :],
                    True, True).then_inc(o0_y, 1)
            ln_pe(t, LN_L0F[1])
            router_low_pe(t, 0, U_L0F, xTh_a, xTl_a)
            router_turn_pe(t, 0)
            bh, bl = unit(U_L0F + 1)
            for b in range(B):
                if b in (0, 4):
                    t.wait_ge(f_tl, b // 4 + 1)
                if b >= 4:
                    t.wait_ge(x_done, XD_L0F + b - 3)
                elif b < 2:
                    t.wait_ge(f_lowc, B)
                c = slice(b * P, (b + 1) * P)
                mm3(bank[b % 4][:], lowT_h[:, c], lowT_l[:, c], bh, bl, True, True).then_inc(f_y, 1)
            owed[0] += 1
            for b in range(B):
                t.wait_ge(x_x, b + 1)
                if b >= 2:
                    t.wait_ge(x_cf, b - 1)
                for k in range(KT):
                    c = slice(k * P, (k + 1) * P)
                    ins = nc.tensor.transpose(bank[b % 2][:, c], xnf[:, b, c], ident[:, :])
                ins.then_inc(x_t, 1)
            t.wait_ge(x_rows, 1)
            for s in range(2):
                o = bank[2][:, s * 32:(s + 1) * 32].rearrange("p (b q) -> p b q", b=B)
                for i in range(6):
                    ins = nc.tensor.matmul(o, bands[:, i, :], rows[:, i // 3, s, :, i % 3:i % 3 + 4], start=i == 0, stop=i == 5)
            ins.then_inc(x_z, 1)
            for j in range(2):
                t.wait_ge(x_zs, j + 1)
                nc.tensor.matmul(bank[3 + j][:, 0:2], ones_f[:, :], zs[:, 1 + j, :], start=True, stop=True).then_inc(x_tot, 1)
            for b in range(B):
                t.wait_ge(x_gt, b + 1)
                if b >= 2:
                    t.wait_ge(x_done, XD_L1X + b - 1)
                for k in range(KT):
                    c = slice(k * P, (k + 1) * P)
                    ins = nc.tensor.transpose(bank[b % 2][:, c], gT[:, b % 2, c], ident[:, :])
                ins.then_inc(x_gp, 1)
            ln_pe(t, LN_L1F[1])
            router_low_pe(t, 1, U_L1F, xTh_a, xTl_a)

            def base1(b):
                if b >= 4:
                    t.wait_ge(x_done, XD_L1F + b - 3)
                elif b < 2:
                    t.wait_ge(f_lowc, 2 * B - 1 + b % 2)
                c = slice(b * P, (b + 1) * P)
                for k in range(KT):
                    wh, wl = unit(U_L1F + 1 + k)
                    mm3(bank[b % 4][:], xTh_a[:, k, c], xTl_a[:, k, c], wh, wl, k == 0, False)
                nc.tensor.matmul(bank[b % 4][:], ones_r[0:2, 0:P], biasr[:, 576:1088], start=False, stop=False)

            base1(0)
            base1(1)
            router_turn_pe(t, 1)
            bh, bl = unit(U_L1F + 5)
            for b in range(B):
                if b + 2 < B:
                    base1(b + 2)
                if b in (0, 4):
                    t.wait_ge(f_tl, 3 + b // 4)
                c = slice(b * P, (b + 1) * P)
                mm3(bank[b % 4][:], lowT_h[:, c], lowT_l[:, c], bh, bl, False, True).then_inc(f_y, 1)
            owed[0] += 5
            def piece2(i, uh, ul, th, tl, half):
                if i >= 2:
                    t.wait_ge(a2_pf, i - 1)
                for k in range(KT):
                    kc, c = slice(k * P, (k + 1) * P), slice(half * HALF, (half + 1) * HALF)
                    ins = mm3(bank[6 + i % 2][:], uh[:, kc], ul[:, kc], th[:, k, c], tl[:, k, c], k == 0, k == KT - 1)
                ins.then_inc(a2_pj, 1)

            def queries2(s):
                for half in range(2):
                    for r in range(4):
                        uh, ul = unit(unit2(s, "q", r))
                        piece2(pj2(s, 2 + 4 * half + r), uh, ul, xTh_b, xTl_b, half)
                owed[0] += 4

            def keys2(s):
                uh, ul = unit(unit2(s, "k"))
                for half in range(2):
                    piece2(pj2(s, half), uh, ul, cTh, cTl, half)
                owed[0] += 1

            for s in range(2):
                if s == 0:
                    ln_pe(t, LN_L2X[1])
                    t.wait_ge(ln_lo, B * (LN_L2X[1] + 1))
                    queries2(0)
                    t.wait_ge(c_lo, KT)
                    keys2(0)
                    uh, ul = unit(unit2(0, "v"))
                    for half in range(2):
                        t.wait_ge(a2_pf, 9 + half)
                        for b in range(4 * half, 4 * half + 4):
                            o, c = bank[6 + half][:, b % 4 * P:(b % 4 + 1) * P], slice(b * P, (b + 1) * P)
                            for k in range(KT):
                                kc = slice(k * P, (k + 1) * P)
                                ins = mm3(o, cTh[:, k, c], cTl[:, k, c], uh[:, kc], ul[:, kc], k == 0, k == KT - 1)
                        ins.then_inc(a2_pj, 1)
                    owed[0] += 1
                else:
                    t.wait_ge(x_done, XD_L2X + B)
                    keys2(1)
                    queries2(1)
                t.wait_ge(a2_pf, 12 if s == 0 else 22)
                for l in range(41):
                    n = 32 * s + l
                    if l < 32:
                        b, gr = l // 4, slice(32 * (l % 4), 32 * (l % 4) + 16)
                        c = slice(b * P, (b + 1) * P)
                        if n >= 3:
                            t.wait_ge(a2_e, n - 2)
                        for r in range(4):
                            ins = nc.tensor.matmul(bank[n % 3][:, r * P:(r + 1) * P], q2[gr, r, c], k2[gr, c], start=True, stop=True)
                        ins.then_inc(a2_s, 1)
                    m = n - 3
                    if 3 <= l < 35:
                        t.wait_ge(a2_pn, m + 1)
                        if m >= 2:
                            t.wait_ge(a2_pt, m - 1)
                        for r in range(4):
                            c = slice(r * P, (r + 1) * P)
                            ins = nc.tensor.transpose(bank[3 + m % 2][:, c], xn[:, m % 4, c], ident[:, :])
                        ins.then_inc(a2_t, 1)
                    m = n - 4
                    if 4 <= l < 36:
                        t.wait_ge(a2_pt, m + 1)
                        o = m // 4
                        if m % 4 == 0 and o >= 2:
                            t.wait_ge(a2_ol, o - 1)
                        gr = 32 * (m % 4)
                        nc.tensor.matmul(bank[5 + o % 2][gr:gr + 32, :], v2[:, o % 8, 4 * s + m % 4, :], probsT[:, m % 3, :],
                                         start=True, stop=True, tile_position=(0, gr)).then_inc(a2_pv, 1)
                    if l >= 9 and l % 4 == 1:
                        m = 8 * s + (l - 9) // 4
                        t.wait_ge(a2_ol, m + 1)
                        if m % 8:
                            t.wait_ge(x_done, XD_L2X + m)
                        for r in range(4):
                            c = slice(r * P, (r + 1) * P)
                            uh, ul = unit(unit2(s, "o", r))
                            ins = mm3(bank[7][:], onT_h[:, m % 2, c], onT_l[:, m % 2, c], uh, ul, r == 0, r == 3)
                        ins.then_inc(a2_y, 1)
                owed[0] += 4
            ln_pe(t, LN_L2F[1])
            t.wait_ge(ln_lo, B * (LN_L2F[1] + 1))
            u = U_L2F
            for i, group in enumerate(FGROUPS):
                for f in group:
                    for half in range(2):
                        n = 2 * f + half
                        if n >= 2:
                            t.wait_ge(g_h, n - 1)
                        for j in range(2):
                            uh, ul = unit(u + j)
                            for k in range(KT):
                                kc, c = slice(k * P, (k + 1) * P), slice(half * HALF, (half + 1) * HALF)
                                ins = mm3(bank[2 * j + n % 2][:], uh[:, kc], ul[:, kc], xTh_b[:, k, c], xTl_b[:, k, c],
                                          k == 0, k == KT - 1)
                            ins.then_inc(g_p, 1)
                            owed[0] += half
                    u += 2
                for b in range(B):
                    t.wait_ge(g_hl, 2 * group[-1] + 1 + b // 4)
                    if i or b >= 2:
                        t.wait_ge(x_done, XD_L2F + B * i + b - 1)
                    c = slice(b * P, (b + 1) * P)
                    for f in range(len(group)):
                        uh, ul = unit(u + f)
                        ins = mm3(bank[4 + b % 2][:], hid_h[:, f, c], hid_l[:, f, c], uh, ul, f == 0, f == len(group) - 1)
                    ins.then_inc(g_y, 1)
                u += len(group)
                owed[0] += len(group)
            ln_pe(t, LN_L3X[1])
            t.wait_ge(ln_lo, B * (LN_L3X[1] + 1))

            def piece3(h, j):
                half, r = ((j - 2) // 4, (j - 2) % 4) if 2 <= j < 10 else (j % 2, 0)
                uh, ul = unit(U_L3X + 10 * h + (0 if j < 2 else 5 if j >= 10 else 1 + r))
                th, tl = (xTh_b, xTl_b) if 2 <= j < 10 else (cTh, cTl)
                if j >= 2:
                    t.wait_ge(a3_rp, 10 * h + j - 1)
                elif h:
                    t.wait_ge(a3_v, 2 * h - 1 + j)
                for k in range(KT):
                    kc, c = slice(k * P, (k + 1) * P), slice(half * HALF, (half + 1) * HALF)
                    ins = mm3(bank[6 + j % 2][:], uh[:, kc], ul[:, kc], th[:, k, c], tl[:, k, c], k == 0, k == KT - 1)
                ins.then_inc(a3_pj, 1)

            def turn3(h, half):
                t.wait_ge(a3_vc, 2 * h + half + 1)
                for q in range(4):
                    c = slice(q * P, (q + 1) * P)
                    ins = nc.tensor.transpose(bank[6 + half][:, c], vT[:, half, c], ident[:, :])
                ins.then_inc(a3_vt, 1)

            for h in range(8):
                base = U_L3X + 10 * h
                if h == 0:
                    piece3(0, 0)
                    piece3(0, 1)
                owed[0] += 1
                for j in range(2, 10):
                    piece3(h, j)
                owed[0] += 4
                for l in range(11):
                    n = B * h + l
                    m = n - 2
                    if l == 2:
                        turn3(h, 1)
                    if 2 <= l < B + 2:
                        t.wait_ge(a3_pn, m + 1)
                        if m >= 2:
                            t.wait_ge(a3_pt, m - 1)
                        for r in range(4):
                            c = slice(r * P, (r + 1) * P)
                            ins = nc.tensor.transpose(bank[2 + m % 2][:, c], probs[:, m % 3, c], ident[:, :])
                        ins.then_inc(a3_t, 1)
                    if l < B:
                        if n >= 2:
                            t.wait_ge(a3_e, n - 1)
                        t.wait_ge(a3_qk, 10 * h + (6 if l < 4 else 10))
                        b = slice(l * P, (l + 1) * P)
                        for r in range(4):
                            ins = nc.tensor.matmul(bank[n % 2][:, r * P:(r + 1) * P], q3[:, r, b], k3[:, b], start=True, stop=True)
                        ins.then_inc(a3_s, 1)
                    if l < 2:
                        piece3(h, 10 + l)
                    if l == 1:
                        owed[0] += 1
                        turn3(h, 0)
                    if l == B + 1 and h < 7:
                        piece3(h + 1, 0)
                    if l == B + 2 and h < 7:
                        piece3(h + 1, 1)
                    if 2 <= l < B + 2:
                        t.wait_ge(a3_pt, m + 1)
                        t.wait_ge(a3_v, 2 * h + (1 if l < 6 else 2))
                        if m:
                            t.wait_ge(a3_ol, m)
                        nc.tensor.matmul(bank[4][:], v3[:, l - 2, :], probsT[:, m % 3, :], start=True, stop=True).then_inc(a3_pv, 1)
                    if l >= 3:
                        m = n - 3
                        t.wait_ge(a3_ol, m + 1)
                        if m:
                            t.wait_ge(x_done, XD_L3X + m)
                        for r in range(4):
                            uh, ul = unit(base + 6 + r)
                            c = slice(r * P, (r + 1) * P)
                            ins = mm3(bank[5][:], o3h[:, m % 2, c], o3l[:, m % 2, c], uh, ul, r == 0, r == 3)
                        ins.then_inc(a3_y, 1)
                owed[0] += 4
            ln_pe(t, LN_L3F[1])
            t.wait_ge(ln_lo, B * (LN_L3F[1] + 1))
            def permuted(n):
                if n >= 4:
                    t.wait_ge(z_tl, n - 3)
                c = slice(n % 2 * HALF, (n % 2 + 1) * HALF)
                for k in range(KT):
                    if n == 0:
                        t.wait_ge(z_pick, k + 1)
                    w = pick[:, k, n // 2 * P:(n // 2 + 1) * P]
                    nc.tensor.matmul(bank[n % 4][:], w, xTh_b[:, k, c], start=k == 0, stop=False)
                    ins = nc.tensor.matmul(bank[n % 4][:], w, xTl_b[:, k, c], start=False, stop=k == KT - 1)
                ins.then_inc(z_t, 1)

            for n in range(3):
                permuted(n)
            uh, ul = unit(U_L3F)
            for n in range(34):
                if n < 32:
                    i4, half, gr = n // 8, n // 4 % 2, slice(32 * (n % 4), 32 * (n % 4) + 32)
                    if n % 4 == 0:
                        t.wait_ge(z_tl, n // 4 + 1)
                    if n >= 2:
                        t.wait_ge(z_g, n - 1)
                    w, c = slice(i4 * P, (i4 + 1) * P), slice(half * HALF, (half + 1) * HALF)
                    mm3(bank[4 + n % 2][:], uh[gr, w], ul[gr, w], tTh[gr, i4, c], tTl[gr, i4, c], True, True).then_inc(z_up, 1)
                    if n < 5:
                        permuted(n + 3)
                m = n - 2
                if m >= 0:
                    o = m // 4
                    if m == 0:
                        t.wait_ge(z_dn, 1)
                    if m % 4 == 0 and o >= 2:
                        t.wait_ge(z_ol, o - 1)
                    t.wait_ge(z_gl, m + 1)
                    hh = 4 * (m // 8) + m % 4
                    dst = bank[6 + o % 2][:]
                    nc.tensor.matmul(dst, down_h[:, hh, :], gel_h[:, m % 2, :], start=m % 4 == 0, stop=False)
                    nc.tensor.matmul(dst, down_l[:, hh, :], gel_h[:, m % 2, :], start=False, stop=False)
                    nc.tensor.matmul(dst, down_h[:, hh, :], gel_l[:, m % 2, :], start=False, stop=m % 4 == 3).then_inc(z_dp, 1)
            t.wait_ge(z_pick, KT + 1)
            t.wait_ge(z_ol, 8)
            for b in range(B):
                if b >= 4:
                    t.wait_ge(x_done, XD_L3F + b - 3)
                c = slice(b * P, (b + 1) * P)
                for k in range(KT):
                    nc.tensor.matmul(bank[b % 4][:], t2h[:, k, c], put[:, k, :], start=k == 0, stop=False)
                    ins = nc.tensor.matmul(bank[b % 4][:], t2l[:, k, c], put[:, k, :], start=False, stop=k == KT - 1)
                ins.then_inc(z_y, 1)



def kernel(**inputs):
    import numpy as _np
    import concourse.bacc as _bacc
    from concourse import mybir as _mybir
    from concourse.bass_utils import run_bass_kernel_spmd as _run

    nc = _bacc.Bacc("TRN2", target_bir_lowering=False, num_devices=1)
    arrays, d = {}, {}
    for name, a in lay_out({k: _np.asarray(v) for k, v in inputs.items()}).items():
        arrays[f"in_{name}_dram"] = a
        d[name] = nc.dram_tensor(f"in_{name}_dram", a.shape, _mybir.dt.from_np(a.dtype), kind="ExternalInput").ap()
    out = nc.dram_tensor("out_0_dram", (B, P, D), _mybir.dt.float32, kind="ExternalOutput").ap()
    program(nc, d, out)
    r = _run(nc, [arrays], core_ids=[0])
    return r.results[0]["out_0_dram"]
```
